# Optimizing a Trainium2 kernel written in Bass

```python
import numpy as np
import jax
import jax.numpy as jnp

def _softmax(x, axis=-1):
    return jax.nn.softmax(x, axis=axis)

def _gelu(x):
    return jax.nn.gelu(x, approximate=True)

def _silu(x):
    return jax.nn.silu(x)

def _sigmoid(x):
    return jax.nn.sigmoid(x)

def _layernorm(x, axis=-1, eps=1e-05):
    m = jnp.mean(x, axis=axis, keepdims=True)
    v = jnp.var(x, axis=axis, keepdims=True)
    return (x - m) / jnp.sqrt(v + eps)

def _scatter_add(tgt, idx, src, axis=0):
    return tgt.at[idx].add(src)

def _segment_sum(src, seg, n):
    return jax.ops.segment_sum(src, seg, n)
kernel_name = 'mk_macaron_d2_jaxref_r8_6f9858'

def setup_inputs(seed: int=0):
    np.random.seed(seed)
    _w = jnp.asarray

    def _L0_attn_setup():
        import jax, jax.numpy as jnp
        import numpy as np
        D_MODEL = 128
        N_HEADS = 16
        HEAD_DIM = D_MODEL // N_HEADS

        def _rope(x):
            B = x.shape[0]
            half = HEAD_DIM // 2
            theta = 1.0 / 10000.0 ** (jnp.arange(0, HEAD_DIM, 2, dtype=jnp.float32) / HEAD_DIM)
            pos = jnp.arange(B, dtype=jnp.float32)
            ang = pos[:, None] * theta[None, :]
            ang2 = jnp.concatenate([ang, ang], axis=-1)
            cos = jnp.cos(ang2)[:, None, None, :]
            sin = jnp.sin(ang2)[:, None, None, :]
            neg_half = jnp.concatenate([x[..., :half], -x[..., half:]], axis=-1)
            return x * cos + neg_half * sin
        key = jax.random.key(seed)
        k_x, k_q, k_k, k_v = jax.random.split(key, 4)
        B, S = (4, 256)
        scale = 1.0 / np.sqrt(D_MODEL)
        x = jax.random.normal(k_x, (B, S, D_MODEL), dtype=jnp.float32)
        Wq = jax.random.normal(k_q, (D_MODEL, D_MODEL), dtype=jnp.float32) * scale
        Wk = jax.random.normal(k_k, (D_MODEL, D_MODEL), dtype=jnp.float32) * scale
        Wv = jax.random.normal(k_v, (D_MODEL, D_MODEL), dtype=jnp.float32) * scale
        return {'x': x, 'Wq': Wq, 'Wk': Wk, 'Wv': Wv}
    _L0_attn_in = _L0_attn_setup()

    def _L0_ffn_setup():
        import jax, jax.numpy as jnp
        import numpy as np
        B, T, D = (2, 256, 128)
        E, DFF, TOPK = (8, 512, 2)
        TEMPERATURE = 1.0
        key = jax.random.key(seed)
        k_x, k_w1, k_w2, k_r = jax.random.split(key, 4)
        x = jax.random.normal(k_x, (B, T, D), dtype=jnp.float32)
        W1 = jax.random.normal(k_w1, (E, DFF, D), dtype=jnp.float32) * 0.02
        W2 = jax.random.normal(k_w2, (E, D, DFF), dtype=jnp.float32) * 0.02
        Wr = jax.random.normal(k_r, (E, D), dtype=jnp.float32) * 0.02
        return {'x': x, 'W1': W1, 'W2': W2, 'Wr': Wr}
    _L0_ffn_in = _L0_ffn_setup()

    def _L1_attn_setup():
        import jax, jax.numpy as jnp
        import numpy as np
        HEADS = 16
        HEAD_DIM = 64
        DIM = 128
        INNER = HEADS * HEAD_DIM

        def rotate_half(t):
            x1, x2 = jnp.split(t, 2, axis=-1)
            return jnp.concatenate((-x2, x1), axis=-1)

        def rope_table(n, head_dim, dtype):
            inv_freq = 1.0 / 10000.0 ** (jnp.arange(0, head_dim, 2, dtype=jnp.float32) / head_dim)
            freqs = jnp.arange(n, dtype=jnp.float32)[:, None] * inv_freq[None, :]
            return jnp.concatenate((freqs, freqs), axis=-1).astype(dtype)
        key = jax.random.key(seed)
        k1, k2, k3, k4 = jax.random.split(key, 4)
        x = jax.random.normal(k1, (1, 512, DIM), dtype=jnp.float32)
        s = 0.02
        W_qkv = jax.random.normal(k2, (DIM, 3 * INNER), dtype=jnp.float32) * s
        W_o1 = jax.random.normal(k3, (INNER, DIM), dtype=jnp.float32) * s
        W_o2 = jax.random.normal(k4, (DIM, DIM), dtype=jnp.float32) * s
        gamma = jnp.ones((DIM,), dtype=jnp.float32)
        return {'x': x, 'W_qkv': W_qkv, 'W_o1': W_o1, 'W_o2': W_o2, 'gamma': gamma}
    _L1_attn_in = _L1_attn_setup()

    def _L1_ffn_setup():
        import jax, jax.numpy as jnp
        import numpy as np
        D = 128
        H = 4
        DF = 512
        E = 8
        EPS = 1e-05

        def _layer_norm(x, g, b):
            mu = jnp.mean(x, axis=-1, keepdims=True)
            var = jnp.mean(jnp.square(x - mu), axis=-1, keepdims=True)
            return (x - mu) * jax.lax.rsqrt(var + EPS) * g + b

        def _mha(x, Wqkv, bqkv, Wo, bo):
            S, B, _ = x.shape
            hd = D // H
            qkv = x @ Wqkv.T + bqkv
            q, k, v = jnp.split(qkv, 3, axis=-1)
            to_heads = lambda t: t.reshape(S, B, H, hd).transpose(1, 2, 0, 3)
            q, k, v = (to_heads(q), to_heads(k), to_heads(v))
            scores = jnp.einsum('bhqd,bhkd->bhqk', q, k) * (1.0 / np.sqrt(hd))
            att = jax.nn.softmax(scores, axis=-1)
            o = jnp.einsum('bhqk,bhkd->bhqd', att, v)
            o = o.transpose(2, 0, 1, 3).reshape(S, B, D)
            return o @ Wo.T + bo

        def _moe(x, Wg, W1, b1, W2, b2):
            S, B, _ = x.shape
            xf = x.reshape(S * B, D)
            logits = xf @ Wg.T
            idx = jnp.argmax(logits, axis=-1)
            out = jnp.zeros_like(xf)
            for e in range(E):
                m = (idx == e)[:, None].astype(xf.dtype)
                h = jax.nn.relu(xf @ W1[e] + b1[e])
                out = out + m * (h @ W2[e] + b2[e])
            return out.reshape(S, B, D)
        key = jax.random.key(seed)
        ks = jax.random.split(key, 16)
        S, B = (64, 8)
        s = lambda k, shape, fan: jax.random.normal(k, shape, jnp.float32) * (1.0 / np.sqrt(fan))
        return {'x': jax.random.normal(ks[0], (S, B, D), jnp.float32), 'Wqkv': s(ks[1], (3 * D, D), D), 'bqkv': jnp.zeros((3 * D,), jnp.float32), 'Wo': s(ks[2], (D, D), D), 'bo': jnp.zeros((D,), jnp.float32), 'g1': jnp.ones((D,), jnp.float32), 'be1': jnp.zeros((D,), jnp.float32), 'g2': jnp.ones((D,), jnp.float32), 'be2': jnp.zeros((D,), jnp.float32), 'Wg': s(ks[3], (E, D), D), 'W1': s(ks[4], (E, D, DF), D), 'b1': jnp.zeros((E, DF), jnp.float32), 'W2': s(ks[5], (E, DF, D), DF), 'b2': jnp.zeros((E, D), jnp.float32)}
    _L1_ffn_in = _L1_ffn_setup()
    _d = {'L0_attn_x': _L0_attn_in['x'], 'L0_attn_Wq': _L0_attn_in['Wq'], 'L0_attn_Wk': _L0_attn_in['Wk'], 'L0_attn_Wv': _L0_attn_in['Wv'], 'L0_ffn_W1': _L0_ffn_in['W1'], 'L0_ffn_W2': _L0_ffn_in['W2'], 'L0_ffn_Wr': _L0_ffn_in['Wr'], 'L1_attn_W_qkv': _L1_attn_in['W_qkv'], 'L1_attn_W_o1': _L1_attn_in['W_o1'], 'L1_attn_W_o2': _L1_attn_in['W_o2'], 'L1_attn_gamma': _L1_attn_in['gamma'], 'L1_ffn_Wqkv': _L1_ffn_in['Wqkv'], 'L1_ffn_bqkv': _L1_ffn_in['bqkv'], 'L1_ffn_Wo': _L1_ffn_in['Wo'], 'L1_ffn_bo': _L1_ffn_in['bo'], 'L1_ffn_g1': _L1_ffn_in['g1'], 'L1_ffn_be1': _L1_ffn_in['be1'], 'L1_ffn_g2': _L1_ffn_in['g2'], 'L1_ffn_be2': _L1_ffn_in['be2'], 'L1_ffn_Wg': _L1_ffn_in['Wg'], 'L1_ffn_W1': _L1_ffn_in['W1'], 'L1_ffn_b1': _L1_ffn_in['b1'], 'L1_ffn_W2': _L1_ffn_in['W2'], 'L1_ffn_b2': _L1_ffn_in['b2']}
    _x0 = _d['L0_attn_x']
    _d['L0_attn_x'] = jax.random.normal(jax.random.fold_in(jax.random.key(seed), 1), (4, 512, 128), dtype=_x0.dtype)
    del _x0
    return _d

def reference(L0_attn_x, L0_attn_Wq, L0_attn_Wk, L0_attn_Wv, L0_ffn_W1, L0_ffn_W2, L0_ffn_Wr, L1_attn_W_qkv, L1_attn_W_o1, L1_attn_W_o2, L1_attn_gamma, L1_ffn_Wqkv, L1_ffn_bqkv, L1_ffn_Wo, L1_ffn_bo, L1_ffn_g1, L1_ffn_be1, L1_ffn_g2, L1_ffn_be2, L1_ffn_Wg, L1_ffn_W1, L1_ffn_b1, L1_ffn_W2, L1_ffn_b2):

    def _L0_attn_ref(x, Wq, Wk, Wv):
        import jax, jax.numpy as jnp
        import numpy as np
        D_MODEL = 128
        N_HEADS = 16
        HEAD_DIM = D_MODEL // N_HEADS

        def _rope(x):
            B = x.shape[0]
            half = HEAD_DIM // 2
            theta = 1.0 / 10000.0 ** (jnp.arange(0, HEAD_DIM, 2, dtype=jnp.float32) / HEAD_DIM)
            pos = jnp.arange(B, dtype=jnp.float32)
            ang = pos[:, None] * theta[None, :]
            ang2 = jnp.concatenate([ang, ang], axis=-1)
            cos = jnp.cos(ang2)[:, None, None, :]
            sin = jnp.sin(ang2)[:, None, None, :]
            neg_half = jnp.concatenate([x[..., :half], -x[..., half:]], axis=-1)
            return x * cos + neg_half * sin
        B, S, D = x.shape
        q = (x @ Wq.T).reshape(B, S, N_HEADS, HEAD_DIM)
        k = (x @ Wk.T).reshape(B, S, N_HEADS, HEAD_DIM)
        v = (x @ Wv.T).reshape(B, S, N_HEADS, HEAD_DIM)
        q = _rope(q)
        k = _rope(k)
        q = q.transpose(0, 2, 1, 3)
        k = k.transpose(0, 2, 1, 3)
        v = v.transpose(0, 2, 1, 3)
        scores = jnp.einsum('bhqd,bhkd->bhqk', q, k) / np.sqrt(HEAD_DIM)
        weights = jax.nn.softmax(scores, axis=-1)
        out = jnp.einsum('bhqk,bhkd->bhqd', weights, v)
        return out.transpose(0, 2, 1, 3).reshape(B, S, D)

    def _L0_ffn_ref(x, W1, W2, Wr):
        import jax, jax.numpy as jnp
        import numpy as np
        B, T, D = (2, 256, 128)
        E, DFF, TOPK = (8, 512, 2)
        TEMPERATURE = 1.0
        logits = jnp.einsum('btd,ed->bte', x, Wr)
        probs = jax.nn.softmax(logits / TEMPERATURE, axis=-1)
        topk_vals, topk_idx = jax.lax.top_k(probs, TOPK)
        router_weights = topk_vals / topk_vals.sum(-1, keepdims=True)
        one_hot = jax.nn.one_hot(topk_idx, E, dtype=x.dtype)
        gate = jnp.einsum('btk,btke->bte', router_weights, one_hot)
        h = jax.nn.silu(jnp.einsum('btd,efd->btef', x, W1))
        y = jnp.einsum('btef,edf->bted', h, W2)
        out = jnp.einsum('bte,bted->btd', gate, y)
        return out

    def _L1_attn_ref(x, W_qkv, W_o1, W_o2, gamma):
        import jax, jax.numpy as jnp
        import numpy as np
        HEADS = 16
        HEAD_DIM = 64
        DIM = 128
        INNER = HEADS * HEAD_DIM

        def rotate_half(t):
            x1, x2 = jnp.split(t, 2, axis=-1)
            return jnp.concatenate((-x2, x1), axis=-1)

        def rope_table(n, head_dim, dtype):
            inv_freq = 1.0 / 10000.0 ** (jnp.arange(0, head_dim, 2, dtype=jnp.float32) / head_dim)
            freqs = jnp.arange(n, dtype=jnp.float32)[:, None] * inv_freq[None, :]
            return jnp.concatenate((freqs, freqs), axis=-1).astype(dtype)
        b, n, _ = x.shape
        scale = HEAD_DIM ** (-0.5)
        qkv = x @ W_qkv
        q, k, v = jnp.split(qkv, 3, axis=-1)
        to_heads = lambda t: t.reshape(b, n, HEADS, HEAD_DIM).transpose(0, 2, 1, 3)
        q, k, v = (to_heads(q), to_heads(k), to_heads(v))
        pos = rope_table(n, HEAD_DIM, x.dtype)
        cos, sin = (jnp.cos(pos), jnp.sin(pos))
        apply_rope = lambda t: t * cos + rotate_half(t) * sin
        q, k = (apply_rope(q), apply_rope(k))
        dots = jnp.einsum('bhid,bhjd->bhij', q, k) * scale
        causal = jnp.triu(jnp.ones((n, n), dtype=bool), 1)
        neg = -jnp.finfo(dots.dtype).max
        dots = jnp.where(causal, neg, dots)
        attn = jax.nn.softmax(dots, axis=-1)
        out = jnp.einsum('bhij,bhjd->bhid', attn, v)
        out = out.transpose(0, 2, 1, 3).reshape(b, n, INNER)
        out = jax.nn.relu(out @ W_o1) @ W_o2
        mean = jnp.mean(out, axis=-1, keepdims=True)
        var = jnp.var(out, axis=-1, keepdims=True)
        out = (out - mean) * jax.lax.rsqrt(var + 1e-05) * gamma
        return out

    def _L1_ffn_ref(x, Wqkv, bqkv, Wo, bo, g1, be1, g2, be2, Wg, W1, b1, W2, b2):
        import jax, jax.numpy as jnp
        import numpy as np
        D = 128
        H = 4
        DF = 512
        E = 8
        EPS = 1e-05

        def _layer_norm(x, g, b):
            mu = jnp.mean(x, axis=-1, keepdims=True)
            var = jnp.mean(jnp.square(x - mu), axis=-1, keepdims=True)
            return (x - mu) * jax.lax.rsqrt(var + EPS) * g + b

        def _mha(x, Wqkv, bqkv, Wo, bo):
            S, B, _ = x.shape
            hd = D // H
            qkv = x @ Wqkv.T + bqkv
            q, k, v = jnp.split(qkv, 3, axis=-1)
            to_heads = lambda t: t.reshape(S, B, H, hd).transpose(1, 2, 0, 3)
            q, k, v = (to_heads(q), to_heads(k), to_heads(v))
            scores = jnp.einsum('bhqd,bhkd->bhqk', q, k) * (1.0 / np.sqrt(hd))
            att = jax.nn.softmax(scores, axis=-1)
            o = jnp.einsum('bhqk,bhkd->bhqd', att, v)
            o = o.transpose(2, 0, 1, 3).reshape(S, B, D)
            return o @ Wo.T + bo

        def _moe(x, Wg, W1, b1, W2, b2):
            S, B, _ = x.shape
            xf = x.reshape(S * B, D)
            logits = xf @ Wg.T
            idx = jnp.argmax(logits, axis=-1)
            out = jnp.zeros_like(xf)
            for e in range(E):
                m = (idx == e)[:, None].astype(xf.dtype)
                h = jax.nn.relu(xf @ W1[e] + b1[e])
                out = out + m * (h @ W2[e] + b2[e])
            return out.reshape(S, B, D)
        y = _layer_norm(x + _mha(x, Wqkv, bqkv, Wo, bo), g1, be1)
        z = _layer_norm(y + _moe(y, Wg, W1, b1, W2, b2), g2, be2)
        return z
    x = L0_attn_x
    x = x + 0.5 * _L0_ffn_ref(_layernorm(x, axis=-1), L0_ffn_W1, L0_ffn_W2, L0_ffn_Wr)
    x = x + _L0_attn_ref(_layernorm(x, axis=-1), L0_attn_Wq, L0_attn_Wk, L0_attn_Wv)
    x = x + 0.5 * _L0_ffn_ref(_layernorm(x, axis=-1), L0_ffn_W1, L0_ffn_W2, L0_ffn_Wr)
    x = x + 0.5 * _L1_ffn_ref(_layernorm(x, axis=-1), L1_ffn_Wqkv, L1_ffn_bqkv, L1_ffn_Wo, L1_ffn_bo, L1_ffn_g1, L1_ffn_be1, L1_ffn_g2, L1_ffn_be2, L1_ffn_Wg, L1_ffn_W1, L1_ffn_b1, L1_ffn_W2, L1_ffn_b2)
    x = x + _L1_attn_ref(_layernorm(x, axis=-1), L1_attn_W_qkv, L1_attn_W_o1, L1_attn_W_o2, L1_attn_gamma)
    x = x + 0.5 * _L1_ffn_ref(_layernorm(x, axis=-1), L1_ffn_Wqkv, L1_ffn_bqkv, L1_ffn_Wo, L1_ffn_bo, L1_ffn_g1, L1_ffn_be1, L1_ffn_g2, L1_ffn_be2, L1_ffn_Wg, L1_ffn_W1, L1_ffn_b1, L1_ffn_W2, L1_ffn_b2)
    return x

_drawn_inputs = setup_inputs


def setup_inputs(seed=0):
    import zlib

    import numpy as np

    out = dict(_drawn_inputs(seed))
    spreads = {'L1_attn_gamma': (1.0, 0.2),
     'L1_ffn_bqkv': (0.0, 0.1),
     'L1_ffn_bo': (0.0, 0.1),
     'L1_ffn_g1': (1.0, 0.2),
     'L1_ffn_be1': (0.0, 0.1),
     'L1_ffn_g2': (1.0, 0.2),
     'L1_ffn_be2': (0.0, 0.1),
     'L1_ffn_b1': (0.0, 0.1),
     'L1_ffn_b2': (0.0, 0.1)}
    factors = {}
    for name, (base, spread) in spreads.items():
        noise = np.random.default_rng([zlib.crc32(name.encode()), seed]).standard_normal(out[name].shape)
        drawn = base * np.exp(spread * noise) if base else spread * noise
        out[name] = jnp.asarray(drawn.astype(out[name].dtype))
    for name, factor in factors.items():
        out[name] = (out[name] * factor).astype(out[name].dtype)
    return out
```

```python
from contextlib import ExitStack

import numpy as np

import concourse.bass as bass
from concourse import mybir

F32 = mybir.dt.float32
F32R = mybir.dt.float32r
U32 = mybir.dt.uint32
ALU = mybir.AluOpType
ACT = mybir.ActivationFunctionType
AX = mybir.AxisListType

P = 128
B, S, D = 4, 512, 128
TILES = B * S // P
GROUP = 4
GROUPS = TILES // GROUP
E, DFF = 8, 512
FC = DFF // P
EPS = 1e-5
BANK = 512


class Core:

    def __init__(self, nc, ctx):
        self.nc, self.ctx = nc, ctx
        self.cleared, self.cleared_at = 0, {}
        self.x = self.sb("x_res", [P, TILES, D])
        self.ident = self.sb("ident", [P, P])
        self.ident_r = self.sb("ident_r", [P, P], F32R)
        self.neg_half = self.sb("neg_half", [P, TILES])
        self.iota8 = self.sb("iota8", [P, TILES, E])
        self.ps = ctx.enter_context(nc.psum_tensor("ps", [P, 8, BANK], F32))

    def sb(self, name, shape, dt=F32):
        return self.ctx.enter_context(self.nc.sbuf_tensor(name, shape, dt))


class Stage:

    def __init__(self, core, name, ctx):
        self.core, self.name, self.ctx, self.nc = core, name, ctx, core.nc
        self.sems, self.nums = [], []
        ctx.callback(self.clear)

    def clear(self):
        if self.sems:
            self.nc.clear_and_free_semaphores(self.sems)
            self.core.cleared += 1
            self.core.cleared_at.update({n: self.core.cleared for n in self.nums})

    def sb(self, name, shape, dt=F32):
        return self.ctx.enter_context(self.nc.sbuf_tensor(f"{self.name}_{name}", shape, dt))

    def sem(self, name):
        num = min(self.nc.free_semaphores, key=lambda n: self.core.cleared_at.get(n, 0))
        self.sems.append(self.nc.alloc_semaphore(name=f"{self.name}_{name}", num=num))
        self.nums.append(num)
        return self.sems[-1]


def setup(core, x_in):
    nc = core.nc
    with ExitStack() as ctx:
        st = Stage(core, "setup", ctx)
        x_loaded, zeroed, ident_built, consts = (st.sem(n) for n in ("x_loaded", "zeroed", "ident_built", "consts"))
        block = ctx.enter_context(nc.Block())

        @block.sync
        def _(sp):
            sp.dma_start(core.x[:], x_in.rearrange("b (t p) d -> p (b t) d", p=P)).then_inc(x_loaded, 16)
            sp.wait_ge(x_loaded, 16)

        @block.gpsimd
        def _(pool):
            pool.memset(core.ident[:], 0.0).then_inc(zeroed, 1)
            pool.memset(core.neg_half[:], -0.5).then_inc(consts, 1)
            pool.iota(core.iota8[:], [[0, TILES], [1, E]], base=0, channel_multiplier=0,
                      allow_small_or_imprecise_dtypes=True).then_inc(consts, 1)
            pool.wait_ge(zeroed, 1)
            pool.affine_select(out=core.ident[:], in_=core.ident[:], compare_op=ALU.not_equal, fill=1.0,
                               base=0, pattern=[[-1, P]], channel_multiplier=1).then_inc(ident_built, 1)

        @block.vector
        def _(dve):
            dve.wait_ge(ident_built, 1)
            dve.tensor_copy(core.ident_r[:], core.ident[:]).then_inc(consts, 1)


def norm_turn(core, name, src, xt=None, xn=None, w_v=None, v=None, affine=None, add_to=None, add_scale=0.5):
    ps, ident = core.ps, core.ident
    with ExitStack() as ctx:
        st = Stage(core, name, ctx)
        stats = st.sb("stats", [P, TILES, 6])
        moments = st.sb("moments", [P, TILES, 2])
        rstd = st.sb("rstd", [P, TILES])
        if xn is None:
            xn = st.sb("xn", [P, TILES, D])
        have_stats, have_moments, var_eps, have_rstd, normed, turned, copied = (
            st.sem(n) for n in ("have_stats", "have_moments", "var_eps", "have_rstd", "normed", "turned", "copied"))
        if affine is not None:
            gb = st.sb("gb", [P, 2, D])
            gb_loaded, scaled, shifted = (st.sem(n) for n in ("gb_loaded", "scaled", "shifted"))
        if v is not None:
            w_sb = st.sb("w_v", [P, D])
            w_loaded, v_in_psum, v_copied = (st.sem(n) for n in ("w_loaded", "v_in_psum", "v_copied"))
        block = ctx.enter_context(core.nc.Block())
        PT = [ps[:, q, :] for q in range(2)]
        PV = [ps[:, 2 + q, :] for q in range(2)]

        @block.sync
        def _(sp):
            if v is not None:
                sp.dma_start(w_sb[:], w_v).then_inc(w_loaded, 16)
            if affine is not None:
                for k, w in enumerate(affine):
                    if w is not None:
                        sp.dma_start(gb[:, k, :], w.partition_broadcast(P)).then_inc(gb_loaded, 16)

        @block.vector
        def _(dve):
            for t in range(TILES):
                dve.bn_stats(stats[:, t, :], src[:, t, :]).then_inc(have_stats, 1)
            for t in range(TILES):
                dve.wait_ge(have_stats, t + 1)
                dve.bn_aggr(moments[:, t, :], stats[:, t, :]).then_inc(have_moments, 1)
            dve.wait_ge(have_rstd, 1)
            for t in range(TILES):
                dve.tensor_scalar(xn[:, t, :], src[:, t, :], moments[:, t, 0:1], rstd[:, t:t + 1],
                                  ALU.subtract, ALU.mult).then_inc(normed, 1)
            if affine is not None:
                dve.wait_ge(gb_loaded, 16 * sum(w is not None for w in affine))
                wide = [P, GROUP, D]
                for g in range(GROUPS):
                    z = xn[:, GROUP * g:GROUP * (g + 1), :]
                    dve.wait_ge(normed, GROUP * (g + 1))
                    done = scaled if affine[1] is not None else shifted
                    dve.tensor_tensor(z, z, gb[:, 0:1, :].to_broadcast(wide), ALU.mult).then_inc(done, 1)
                    if affine[1] is not None:
                        dve.wait_ge(scaled, g + 1)
                        dve.tensor_tensor(z, z, gb[:, 1:2, :].to_broadcast(wide), ALU.add).then_inc(shifted, 1)
                    if add_to is not None:
                        r = add_to[:, GROUP * g:GROUP * (g + 1), :]
                        dve.wait_ge(shifted, g + 1)
                        dve.scalar_tensor_tensor(out=r, in0=z, scalar=add_scale, in1=r, op0=ALU.mult, op1=ALU.add)

        @block.gpsimd
        def _(pool):
            pool.wait_ge(have_moments, TILES)
            pool.tensor_scalar(rstd[:], moments[:, :, 1], EPS, None, ALU.add).then_inc(var_eps, 1)
            pool.wait_ge(var_eps, 1)
            pool.tensor_tensor(rstd[:], rstd[:], core.neg_half[:], ALU.pow).then_inc(have_rstd, 1)

        if xt is None:
            return

        @block.tensor
        def _(pe):
            if v is not None:
                pe.wait_ge(w_loaded, 16)
            for g in range(GROUPS):
                if affine is None:
                    pe.wait_ge(normed, GROUP * (g + 1))
                else:
                    pe.wait_ge(shifted, g + 1)
                if g >= 2:
                    pe.wait_ge(copied, g - 1)
                for j in range(GROUP):
                    last = pe.transpose(PT[g % 2][:, j * P:(j + 1) * P], xn[:, GROUP * g + j, :], ident[:])
                last.then_inc(turned, 1)
                if v is not None:
                    pe.wait_ge(copied, g + 1)
                    if g >= 2:
                        pe.wait_ge(v_copied, g - 1)
                    for j in range(GROUP):
                        t = GROUP * g + j
                        last = pe.matmul(PV[g % 2][:, j * P:(j + 1) * P], xt[:, t * P:(t + 1) * P], w_sb[:],
                                         start=True, stop=True)
                    last.then_inc(v_in_psum, 1)

        @block.scalar
        def _(act):
            for g in range(GROUPS):
                act.wait_ge(turned, g + 1)
                act.activation(xt[:, g * BANK:(g + 1) * BANK], PT[g % 2], ACT.Copy).then_inc(copied, 1)
                if v is not None:
                    act.wait_ge(v_in_psum, g + 1)
                    act.activation(v[:, GROUP * g:GROUP * (g + 1), :],
                                   PV[g % 2].rearrange("p (j d) -> p j d", d=D), ACT.Copy).then_inc(v_copied, 1)


def moe(core, name, src, acc, w1, w2, wr, top2, b1=None, b2=None):
    with ExitStack() as ctx:
        st = Stage(core, name, ctx)
        xh = st.sb("xh", [P, TILES * P], F32R)
        xl = st.sb("xl", [P, TILES * P], F32R)
        gate = st.sb("gate", [P, TILES, E])
        with ExitStack() as c1:
            route(core, Stage(core, name + "_route", c1), src, xh, xl, gate, wr, top2)
        if b2 is not None:
            with ExitStack() as c2:
                add_bias2(core, Stage(core, name + "_b2", c2), acc, gate, b2)
        with ExitStack() as c3:
            experts(core, Stage(core, name + "_exp", c3), acc, xh, xl, gate, w1, w2, top2, b1)


def route(core, st, xt, xh, xl, gate, wr, top2):
    ps = core.ps
    w_route = st.sb("w_route", [P, E])
    lg = st.sb("lg", [P, TILES, E])
    best = st.sb("best", [P, TILES, 8])
    place_i = st.sb("place_i", [P, TILES, 8], U32)
    place = st.sb("place", [P, TILES, 8])
    small = st.sb("small", [P, 4, TILES])
    second_mask = st.sb("second_mask", [P, TILES, E])
    gap_t, exp_t, g1_t, g2_t = (small[:, k, :] for k in range(4))
    wr_loaded, logits, high, chain, gap, gap_exp, ranked, placed = (
        st.sem(n) for n in ("wr_loaded", "logits", "high", "chain", "gap", "gap_exp", "ranked", "placed"))
    block = st.ctx.enter_context(core.nc.Block())
    PL = ps[:, 0, 0:TILES * E]

    @block.sync
    def _(sp):
        sp.dma_start(w_route[:], wr).then_inc(wr_loaded, 16)

    @block.tensor
    def _(pe):
        pe.wait_ge(wr_loaded, 16)
        for t in range(TILES):
            last = pe.matmul(PL[:, t * E:(t + 1) * E], xt[:, t * P:(t + 1) * P], w_route[:], start=True, stop=True)
        last.then_inc(logits, 1)

    @block.scalar
    def _(act):
        act.activation(xh[:], xt[:], ACT.Copy).then_inc(high, 1)
        if top2:
            act.wait_ge(gap, 1)
            act.activation(exp_t, gap_t, ACT.Exp).then_inc(gap_exp, 1)

    @block.vector
    def _(dve):
        steps = [0]

        def link(ins):
            steps[0] += 1
            ins.then_inc(chain, 1)
            dve.wait_ge(chain, steps[0])

        dve.wait_ge(logits, 1)
        link(dve.tensor_copy(lg[:], PL.rearrange("p (t e) -> p t e", e=E)))
        for t in range(TILES):
            dve.max(best[:, t, :], lg[:, t, :]).then_inc(ranked, 1)
        for t in range(TILES):
            dve.wait_ge(ranked, t + 1)
            dve.max_index(place_i[:, t, :], best[:, t, :], lg[:, t, :]).then_inc(placed, 1)
        dve.wait_ge(placed, TILES)
        link(dve.tensor_copy(place[:], place_i[:]))
        first = place[:, :, 0:1].to_broadcast([P, TILES, E])
        if not top2:
            link(dve.tensor_tensor(gate[:], core.iota8[:], first, ALU.is_equal))
        else:
            second = place[:, :, 1:2].to_broadcast([P, TILES, E])
            dve.tensor_tensor(gap_t, best[:, :, 1], best[:, :, 0], ALU.subtract).then_inc(gap, 1)
            link(dve.tensor_tensor(second_mask[:], core.iota8[:], second, ALU.is_equal))
            link(dve.tensor_tensor(gate[:], core.iota8[:], first, ALU.is_equal))
            dve.wait_ge(gap_exp, 1)
            link(dve.tensor_scalar(g2_t, exp_t, 1.0, 2.0, ALU.add, ALU.mult))
            link(dve.reciprocal(g1_t, g2_t))
            link(dve.tensor_tensor(g2_t, g1_t, exp_t, ALU.mult))
            wide = [P, TILES, E]
            link(dve.tensor_tensor(gate[:], gate[:], g1_t.unsqueeze(2).to_broadcast(wide), ALU.mult))
            link(dve.tensor_tensor(second_mask[:], second_mask[:], g2_t.unsqueeze(2).to_broadcast(wide), ALU.mult))
            link(dve.tensor_tensor(gate[:], gate[:], second_mask[:], ALU.add))
        dve.wait_ge(high, 1)
        dve.tensor_tensor(xl[:], xt[:], xh[:].bitcast(F32), ALU.subtract).then_inc(chain, 1)


def add_bias2(core, st, acc, gate, b2):
    nc, ident, ps = core.nc, core.ident, core.ps
    b2_sb = st.sb("b2", [E, D])
    gt = st.sb("gt", [E, 2, GROUP * P])
    b2_loaded, turned, copied, biased, added = (st.sem(n) for n in ("b2_loaded", "turned", "copied", "biased", "added"))
    block = st.ctx.enter_context(nc.Block())

    @block.sync
    def _(sp):
        sp.dma_start(b2_sb[:], b2).then_inc(b2_loaded, 16)

    @block.tensor
    def _(pe):
        pe.wait_ge(b2_loaded, 16)
        for g in range(GROUPS):
            q = g % 2
            if g >= 2:
                pe.wait_ge(copied, g - 1)
            for j in range(GROUP):
                last = pe.transpose(ps[0:E, q, j * P:(j + 1) * P], gate[:, GROUP * g + j, :], ident[:])
            last.then_inc(turned, 1)
            pe.wait_ge(copied, g + 1)
            if g >= 2:
                pe.wait_ge(added, g - 1)
            for j in range(GROUP):
                last = pe.matmul(ps[:, 2 + q, j * P:(j + 1) * P], gt[:, q, j * P:(j + 1) * P], b2_sb[:],
                                 start=True, stop=True)
            last.then_inc(biased, 1)

    @block.scalar
    def _(act):
        for g in range(GROUPS):
            act.wait_ge(turned, g + 1)
            if g >= 2:
                act.wait_ge(biased, g - 1)
            act.activation(gt[:, g % 2, :], ps[0:E, g % 2, :], ACT.Copy).then_inc(copied, 1)

    @block.vector
    def _(dve):
        for g in range(GROUPS):
            dve.wait_ge(biased, g + 1)
            a = acc[:, GROUP * g:GROUP * (g + 1), :].rearrange("p a d -> p (a d)")
            dve.tensor_tensor(a, a, ps[:, 2 + g % 2, :], ALU.add).then_inc(added, 1)


def experts(core, st, acc, xh, xl, gate, w1, w2, top2, b1):
    ps = core.ps
    w1_f = st.sb("w1_f", [P, 2, DFF])
    w1h = st.sb("w1h", [P, 2, DFF], F32R)
    w1l = st.sb("w1l", [P, 2, DFF], F32R)
    w2_f = st.sb("w2_f", [P, 2, FC, D])
    h = st.sb("h", [P, 2, FC, GROUP * P])
    w1_loaded, w2_loaded = ([st.sem(f"{n}{q}") for q in range(2)] for n in ("w1_loaded", "w2_loaded"))
    w1_high, w1_split = st.sem("w1_high"), st.sem("w1_split")
    h_in_psum = st.sem("h_in_psum")
    h_ready = st.sem("h_ready")
    y_in_psum = st.sem("y_in_psum")
    y_added = st.sem("y_added")
    if b1 is not None:
        b1_sb, b1_now = st.sb("b1", [P, E * FC]), st.sb("b1_now", [P, 2, FC])
        b1_loaded, b1_set = st.sem("b1_loaded"), st.sem("b1_set")
    block = st.ctx.enter_context(core.nc.Block())
    STEPS = 2 * GROUPS
    PH = [ps[:, 2 * k:2 * k + 2, :] for k in range(2)]
    PY = [ps[:, 4 + k, :] for k in range(2)]

    @block.sync
    def _(sp):
        if b1 is not None:
            sp.dma_start(b1_sb[:], b1).then_inc(b1_loaded, 16)
        for e in range(E):
            q = e % 2
            if e >= 2:
                sp.wait_ge(w1_split, e - 1)
            sp.dma_start(w1_f[:, q, :], w1[e]).then_inc(w1_loaded[q], 16)
            if e >= 2:
                sp.wait_ge(y_in_psum, 2 + GROUPS * (e - 1))
            sp.dma_start(w2_f[:, q, :, :], w2[e]).then_inc(w2_loaded[q], 16)

    @block.gpsimd
    def _(pool):
        if b1 is not None:
            pool.wait_ge(b1_loaded, 16)
        for e in range(E):
            q = e % 2
            if b1 is not None:
                if e >= 2:
                    pool.wait_ge(h_ready, 2 + 2 * GROUPS * (e - 1))
                pool.tensor_copy(b1_now[:, q, :], b1_sb[:, e * FC:(e + 1) * FC]).then_inc(b1_set, 1)
            pool.wait_ge(w1_loaded[q], 16 * (e // 2 + 1))
            if e >= 2:
                pool.wait_ge(h_in_psum, 2 * GROUPS * (e - 1))
            pool.tensor_copy(w1h[:, q, :], w1_f[:, q, :]).then_inc(w1_high, 1)
            pool.wait_ge(w1_high, e + 1)
            pool.tensor_tensor(w1l[:, q, :], w1_f[:, q, :], w1h[:, q, :].bitcast(F32),
                               ALU.subtract).then_inc(w1_split, 1)

    @block.tensor
    def _(pe):
        def first_layer(pair, s):
            e, t = (s // GROUPS) % 2, s % GROUPS
            if t == 0:
                pe.wait_ge(w1_split, 2 * pair + s // GROUPS + 1)
            for k in range(2):
                pe.wait_ge(h_ready, 2 * (STEPS * pair + s) + k + 1)
                for c in range(2):
                    w = slice((2 * k + c) * P, (2 * k + c + 1) * P)
                    x = slice(t * GROUP * P, (t + 1) * GROUP * P)
                    pe.matmul(PH[k][:, c, :], w1h[:, e, w], xh[:, x], start=True, stop=False)
                    pe.matmul(PH[k][:, c, :], w1h[:, e, w], xl[:, x], start=False, stop=False)
                    last = pe.matmul(PH[k][:, c, :], w1l[:, e, w], xh[:, x], start=False, stop=True)
                last.then_inc(h_in_psum, 1)

        def second_layer(pair, s):
            e, q, n = s // GROUPS, s % 2, STEPS * pair + s
            if s % GROUPS == 0:
                pe.wait_ge(w2_loaded[e], 16 * (pair + 1))
            pe.wait_ge(h_ready, 2 + 2 * (n + 1))
            pe.wait_ge(y_added, n + 1)
            for j in range(GROUP):
                for f in range(FC):
                    last = pe.matmul(PY[q][:, j * P:(j + 1) * P], h[:, q, f, j * P:(j + 1) * P],
                                     w2_f[:, e, f, :], start=(f == 0), stop=(f == FC - 1))
            last.then_inc(y_in_psum, 1)

        pe.sem_inc(y_in_psum, 2)
        first_layer(0, 0)
        with pe.Fori(0, E // 2 - 1) as pair:
            for s in range(STEPS):
                first_layer(pair, s + 1)
                second_layer(pair, s)
        for s in range(STEPS):
            if s + 1 < STEPS:
                first_layer(E // 2 - 1, s + 1)
            second_layer(E // 2 - 1, s)

    @block.scalar
    def _(act):
        act.sem_inc(h_ready, 2)
        with act.Fori(0, E // 2) as pair:
            for s in range(STEPS):
                n, q, e = STEPS * pair + s, s % 2, s // GROUPS
                if b1 is not None and s % GROUPS == 0:
                    act.wait_ge(b1_set, 2 * pair + e + 1)
                act.wait_ge(y_in_psum, n + 1)
                for k in range(2):
                    act.wait_ge(h_in_psum, 2 * n + k + 1)
                    if b1 is None:
                        act.activation(h[:, q, 2 * k:2 * k + 2, :], PH[k], ACT.Silu).then_inc(h_ready, 1)
                    else:
                        for c in range(2):
                            f = 2 * k + c
                            last = act.activation(h[:, q, f, :], PH[k][:, c, :], ACT.Relu,
                                                  bias=b1_now[:, e, f:f + 1])
                        last.then_inc(h_ready, 1)

    @block.vector
    def _(dve):
        dve.sem_inc(y_added, 2)
        with dve.Fori(0, E) as e:
            for t in range(GROUPS):
                n, q = GROUPS * e + t, t % 2
                dve.wait_ge(y_in_psum, n + 3)
                dve.wait_ge(y_added, n + 1)
                for j in range(GROUP):
                    tile = GROUP * t + j
                    last = dve.scalar_tensor_tensor(
                        out=acc[:, tile, :], in0=PY[q][:, j * P:(j + 1) * P],
                        scalar=gate[:, tile, bass.ds(e, 1)], in1=acc[:, tile, :], op0=ALU.mult, op1=ALU.add)
                last.then_inc(y_added, 1)


HEADS8, HD8 = 16, 8
PER = 4
HGROUPS = HEADS8 // PER
ROWS = P // PER


def attention8(core, name, x, wq, wk, wv, rope, row_consts):
    ps, ident = core.ps, core.ident
    NG = B * HGROUPS
    with ExitStack() as ctx:
        st = Stage(core, name, ctx)
        xt = st.sb("xt", [P, TILES * P + BANK])
        v = st.sb("v", [P, TILES, D])
        norm_turn(core, name + "_ln", x, xt, w_v=wv, v=v)

        wq_c, wk_c = st.sb("wq_c", [P, D]), st.sb("wk_c", [P, D])
        wq_r, wk_r = (st.sb(n, [P, HGROUPS, PER, ROWS]) for n in ("wq_r", "wk_r"))
        rope_sb = st.sb("rope", [P, B + 1])
        rope_now = st.sb("rope_now", [P, 1])
        consts = st.sb("consts", [P, 3])
        zero = st.sb("zero", [P, BANK])
        tq, tk, hq, hk = (st.sb(n, [P, BANK]) for n in ("tq", "tk", "hq", "hk"))
        k_all = st.sb("k_all", [P, BANK], F32R)
        k_one = st.sb("k_one", [P, HGROUPS, PER, BANK], F32R)
        q_all = st.sb("q_all", [P, HGROUPS, BANK], F32R)
        tops = st.sb("tops", [P, 2, GROUP, P], F32R)
        probs = st.sb("probs", [P, 2, GROUP, PER, BANK])
        v_one = st.sb("v_one", [P, GROUP, HEADS8, ROWS])
        o_sb = st.sb("o_sb", [P, BANK])
        rec = st.sb("rec", [P, GROUP, PER])
        o_n = st.sb("o_n", [P, GROUP, PER, HD8])
        names = ("loaded", "zeroed", "placed", "filled", "projected", "roped", "high", "q_split", "k_split",
                 "rope_set", "top_filled", "top_read", "rows_in_psum", "q_ready", "scored", "exped", "summed",
                 "v_set", "o_copied", "o_turned", "o_added", "inverted", "scaled")
        (loaded, zeroed, placed, filled, projected, roped, high, q_split, k_split,
         rope_set, top_filled, top_read, rows_in_psum, q_ready, scored, exped, summed,
         v_set, o_copied, o_turned, o_added, inverted, scaled) = (st.sem(n) for n in names)
        k_spread = [st.sem(f"k_spread{gi}") for gi in range(HGROUPS)]
        PTOP = [ps[:, 2 * k:2 * k + 2, :] for k in range(2)]
        PSC = [ps[:, 4 + k, :] for k in range(2)]
        PO, PM = ps[:, 6, :], ps[:, 7, :]

        with core.nc.Block() as block:
            @block.sync
            def _(sp):
                for dst, src in ((wq_c, wq), (wk_c, wk), (rope_sb, rope), (consts, row_consts)):
                    sp.dma_start(dst[:], src).then_inc(loaded, 16)

            @block.gpsimd
            def _(pool):
                pool.memset(xt[:, TILES * P:], 0.0).then_inc(zeroed, 1)
                pool.memset(zero[:], 0.0).then_inc(zeroed, 1)
                pool.memset(v_one[:], 0.0).then_inc(zeroed, 1)
                pool.memset(k_one[:].bitcast(F32), 0.0).then_inc(zeroed, 1)
                pool.wait_ge(zeroed, 3)
                pool.memset(v_one[:, :, :, HD8:HD8 + 1], 1.0).then_inc(filled, 1)

            @block.vector
            def _(dve):
                dve.memset(wq_r[:], 0.0).then_inc(placed, 1)
                dve.memset(wk_r[:], 0.0).then_inc(placed, 1)
                dve.memset(tops[:].bitcast(F32), 0.0).then_inc(placed, 1)
                dve.wait_ge(loaded, 64)
                dve.wait_ge(placed, 2)
                for w_c, w_r in ((wq_c, wq_r), (wk_c, wk_r)):
                    for c in range(1, 4):
                        dve.tensor_copy(w_r[:, :, :, HD8 * c:HD8 * (c + 1)],
                                        w_c[:].rearrange("p (g h d) -> p g h d", h=PER, d=HD8)).then_inc(filled, 1)

        block = ctx.enter_context(core.nc.Block())

        @block.sync
        def _(sp):
            def spread(i, gi):
                sp.wait_ge(k_split, i + 1 + 1)
                for hh in range(PER):
                    r = slice(ROWS * hh, ROWS * (hh + 1))
                    sp.dma_start(k_one[r, gi, hh, :].bitcast(F32), k_all[r, :].bitcast(F32)).then_inc(k_spread[gi], 16)

            with sp.Fori(0, B) as b:
                for gi in range(HGROUPS):
                    spread(HGROUPS * b + gi, gi)
            for gi in range(2):
                spread(NG + gi, gi)
            for gi in range(2):
                sp.wait_ge(k_spread[gi], 16 * PER * (B + 1))

        @block.gpsimd
        def _(pool):
            with pool.Fori(0, NG + 2) as i:
                pool.wait_ge(roped, 2 * i + 1)
                pool.wait_ge(q_split, i + 1)
                pool.tensor_tensor(hq[:].bitcast(F32R), tq[:], zero[:], ALU.add).then_inc(high, 1)
                pool.wait_ge(roped, 2 * i + 2)
                pool.wait_ge(k_split, i + 1)
                pool.tensor_tensor(hk[:].bitcast(F32R), tk[:], zero[:], ALU.add).then_inc(high, 1)

        @block.tensor
        def _(pe):
            def project(i, b, gi, w_r, ready, count):
                if ready is not None:
                    pe.wait_ge(ready, count)
                pe.matmul(PM, w_r[:, gi, :, :].rearrange("p h r -> p (h r)"), xt[:, bass.ts(b, BANK)],
                          start=True, stop=True).then_inc(projected, 1)

            def top_scores(i, turn, gi, hh, k):
                if hh == 0 and k == 0:
                    pe.wait_ge(k_spread[gi], 16 * PER * (turn + 1))
                    pe.wait_ge(q_split, i + 1 + 1)
                pe.wait_ge(top_read, 2 * PER * i + 2 * hh + k + 1)
                for c in range(2):
                    qc = 2 * k + c
                    last = pe.matmul(PTOP[k][:, c, :], q_all[:, gi, qc * P:(qc + 1) * P], k_one[:, gi, hh, :],
                                     start=True, stop=True)
                last.then_inc(top_filled, 1)

            def scores(m, gi, hh, kc):
                pe.wait_ge(exped, 4 * PER * m + 4 * hh + kc + 1)
                pe.matmul(PSC[kc % 2], k_one[:, gi, hh, kc * P:(kc + 1) * P], q_all[:, gi, :],
                          start=True, stop=True).then_inc(scored, 1)

            def sums(m, gi, kc):
                if kc == 0:
                    pe.wait_ge(exped, 2 + 4 * PER * (m + 1))
                    pe.wait_ge(o_copied, m + 1)
                    if gi == 0:
                        pe.wait_ge(v_set, m // HGROUPS + 1)
                for hh in range(PER):
                    r = slice(ROWS * hh, ROWS * (hh + 1))
                    last = pe.matmul(PO[r, :], v_one[:, kc, PER * gi + hh, :], probs[:, gi % 2, kc, hh, :],
                                     start=(kc == 0), stop=(kc == GROUP - 1))
                if kc == GROUP - 1:
                    last.then_inc(summed, 1)

            def turn_out(m, ready, count):
                pe.wait_ge(o_copied, m + 1 + 1)
                pe.wait_ge(ready, count)
                for j in range(GROUP):
                    last = pe.transpose(PM[:, j * P:(j + 1) * P], o_sb[:, j * P:(j + 1) * P], ident[:])
                last.then_inc(o_turned, 1)

            pe.sem_inc(summed, 2)
            pe.sem_inc(o_turned, 1)
            project(0, 0, 0, wq_r, None, 0)
            project(0, 0, 0, wk_r, roped, 1)
            project(1, 0, 1, wq_r, roped, 2)
            project(1, 0, 1, wk_r, roped, 3)
            for hh in range(PER):
                for k in range(2):
                    top_scores(0, 0, 0, hh, k)
            with pe.Fori(0, B) as b:
                for gi in range(HGROUPS):
                    m = HGROUPS * b + gi
                    nxt, far = (gi + 1) % HGROUPS, (gi + 2) % HGROUPS
                    far_b = b + (gi + 2) // HGROUPS
                    pe.wait_ge(top_read, 2 + 2 * PER * (m + 1))
                    if gi == 1:
                        pe.wait_ge(roped, 2 * m + 4)
                    else:
                        pe.wait_ge(roped, 2 * m + 4)
                        pe.wait_ge(o_added, HGROUPS * b + max(gi - 1, 0) + 1)
                    for j in range(GROUP):
                        last = pe.matmul(PM[:, j * P:(j + 1) * P], tops[:, gi % 2, j, :], core.ident_r[:],
                                         start=True, stop=True)
                    last.then_inc(rows_in_psum, 1)
                    for hh in range(PER):
                        top_scores(m + 1, b + (gi + 1) // HGROUPS, nxt, hh, 0)
                        if hh == 0:
                            pe.wait_ge(q_ready, m + 1)
                        scores(m, gi, hh, 0)
                        scores(m, gi, hh, 1)
                        top_scores(m + 1, b + (gi + 1) // HGROUPS, nxt, hh, 1)
                        scores(m, gi, hh, 2)
                        scores(m, gi, hh, 3)
                        if gi > 0:
                            sums(m - 1, gi - 1, hh)
                        if hh == 0:
                            project(m + 2, far_b, far, wq_r, q_ready, m + 1)
                        if hh == 1:
                            project(m + 2, far_b, far, wk_r, roped, 2 * (m + 2) + 1)
                    if gi > 0:
                        turn_out(m - 1, roped, 2 * (m + 2) + 2)
                    if gi == HGROUPS - 1:
                        for kc in range(GROUP):
                            sums(m, gi, kc)
                        turn_out(m, o_added, m + 1)

        @block.scalar
        def _(act):
            def rotate(i, which, t, bias):
                act.wait_ge(projected, 2 * i + which + 1)
                if bias is None:
                    act.activation(t[:], PM, ACT.Copy, scale=rope_now[:, 0:1]).then_inc(roped, 1)
                else:
                    act.activation(t[:], PM, ACT.Identity, scale=rope_now[:, 0:1], bias=bias).then_inc(roped, 1)

            def copy_out(m):
                act.wait_ge(summed, 2 + m + 1)
                act.wait_ge(o_turned, m + 1)
                act.activation(o_sb[:], PO, ACT.Copy).then_inc(o_copied, 1)

            act.sem_inc(exped, 2)
            act.sem_inc(o_copied, 1)
            act.wait_ge(rope_set, 1)
            for i in range(2):
                act.wait_ge(q_split, i + 1)
                rotate(i, 0, tq, None)
                act.wait_ge(k_split, i + 1)
                rotate(i, 1, tk, consts[:, 0:1])
            with act.Fori(0, B) as b:
                for gi in range(HGROUPS):
                    m = HGROUPS * b + gi
                    act.wait_ge(summed, m + 1)
                    if gi == 2:
                        act.wait_ge(rope_set, b + 2)
                    for hh in range(PER):
                        for kc in range(GROUP):
                            act.wait_ge(scored, 4 * PER * m + 4 * hh + kc + 1)
                            act.activation(probs[:, gi % 2, kc, hh, :], PSC[kc % 2], ACT.Exp,
                                           scale=HD8 ** -0.5).then_inc(exped, 1)
                        if hh == 0:
                            act.wait_ge(q_split, m + 2 + 1)
                            rotate(m + 2, 0, tq, None)
                        if hh == 1:
                            act.wait_ge(k_split, m + 2 + 1)
                            rotate(m + 2, 1, tk, consts[:, 0:1])
                    if gi > 0:
                        copy_out(m - 1)
                    if gi == HGROUPS - 1:
                        copy_out(m)

        @block.vector
        def _(dve):
            def split(i, which, t, hi, dst, done):
                dve.wait_ge(high, 2 * i + which + 1)
                dve.scalar_tensor_tensor(out=dst, in0=hi[:], scalar=consts[:, 1 + which:2 + which], in1=t[:],
                                         op0=ALU.mult, op1=ALU.add).then_inc(done, 1)

            def top(i, gi, hh, k):
                dve.wait_ge(top_filled, 2 * PER * i + 2 * hh + k + 1)
                dve.tensor_reduce(tops[:, gi % 2, 2 * k:2 * k + 2, ROWS * hh], PTOP[k], AX.X, ALU.max,
                                  negate=True).then_inc(top_read, 1)

            def add_out(b, gi, m):
                dve.wait_ge(o_turned, m + 1 + 1)
                o = PM.rearrange("p (j h r) -> p j h r", j=GROUP, h=PER)
                dve.reciprocal(rec[:], o[:, :, :, HD8]).then_inc(inverted, 1)
                dve.wait_ge(inverted, m + 1)
                dve.tensor_tensor(o_n[:], o[:, :, :, 0:HD8], rec[:].unsqueeze(3).to_broadcast([P, GROUP, PER, HD8]),
                                  ALU.mult).then_inc(scaled, 1)
                dve.wait_ge(scaled, m + 1)
                xs = x[:, bass.ts(b, GROUP), gi * PER * HD8:(gi + 1) * PER * HD8]
                dve.tensor_tensor(xs, xs, o_n[:].rearrange("p j h d -> p j (h d)"), ALU.add).then_inc(o_added, 1)

            def set_rope(b):
                dve.tensor_tensor(rope_now[:], rope_sb[:, bass.ds(b, 1)], zero[:, 0:1], ALU.add).then_inc(rope_set, 1)

            def set_v(b):
                dve.tensor_tensor(v_one[:, :, :, 0:HD8],
                                  v[:, bass.ts(b, GROUP), :].rearrange("p j (h d) -> p j h d", d=HD8),
                                  zero[:, 0:BANK].rearrange("p (j h d) -> p j h d", j=GROUP, d=HD8),
                                  ALU.add).then_inc(v_set, 1)

            dve.sem_inc(top_read, 2)
            for start_at_one in (q_split, k_split, o_added):
                dve.sem_inc(start_at_one, 1)
            set_rope(0)
            for i in range(2):
                split(i, 0, tq, hq, q_all[:, i, :], q_split)
                if i:
                    dve.wait_ge(k_spread[0], 16 * PER)
                split(i, 1, tk, hk, k_all[:], k_split)
            for hh in range(PER):
                for k in range(2):
                    top(0, 0, hh, k)
            with dve.Fori(0, B) as b:
                for gi in range(HGROUPS):
                    m = HGROUPS * b + gi
                    nxt, far = (gi + 1) % HGROUPS, (gi + 2) % HGROUPS
                    dve.wait_ge(rows_in_psum, m + 1)
                    q = q_all[:, gi, :]
                    dve.tensor_tensor(q, PM, q.bitcast(F32), ALU.add).then_inc(q_ready, 1)
                    if gi == 1:
                        dve.wait_ge(summed, 2 + HGROUPS * b)
                        set_v(b)
                    if gi == 2:
                        dve.wait_ge(roped, 2 * m + 4)
                        set_rope(b + 1)
                    for hh in range(PER):
                        for k in range(2):
                            top(m + 1, nxt, hh, k)
                        if hh == 1:
                            split(m + 2, 0, tq, hq, q_all[:, far, :], q_split)
                        if hh == 2:
                            dve.wait_ge(k_spread[nxt], 16 * PER * (b + (gi + 1) // HGROUPS + 1))
                            split(m + 2, 1, tk, hk, k_all[:], k_split)
                    if gi > 0:
                        add_out(b, gi - 1, m - 1)
                    if gi == HGROUPS - 1:
                        add_out(b, gi, m)


HEADS64, HD64 = 16, 64
INNER = HEADS64 * HD64
PAIRS = HEADS64 // 2
BIG = -1e30
SCORE_AT = {3: (0, 0, 0), 2: (1, 0, 512), 0: (1, 384, 896), 1: (2, 0, 1024)}
SCORE_BANKS = ((3,), (2, 0), (1,))
CAUSAL = sum((qc + 1) * P for qc in range(4))
TURN_AT = {0: (0, 0, 0), 1: (1, 0, 512), 2: (2, 0, 896), 3: (2, 256, 1152)}
TURN_BANKS = ((0,), (1,), (2, 3))


def values64(core, name, xt, wv, v):
    ps = core.ps
    with ExitStack() as ctx:
        st = Stage(core, name, ctx)
        w_sb = st.sb("w", [P, INNER])
        loaded, in_psum = st.sem("loaded"), st.sem("in_psum")
        copied = [st.sem("copied_act"), st.sem("copied_dve")]
        block = ctx.enter_context(core.nc.Block())

        @block.sync
        def _(sp):
            sp.dma_start(w_sb[:], wv).then_inc(loaded, 16)

        @block.tensor
        def _(pe):
            pe.wait_ge(loaded, 16)
            for t in range(TILES):
                for k in range(2):
                    if t >= 2:
                        pe.wait_ge(copied[k], t - 1)
                    pe.matmul(ps[:, 2 * (t % 2) + k, :], xt[:, t * P:(t + 1) * P], w_sb[:, k * BANK:(k + 1) * BANK],
                              start=True, stop=True).then_inc(in_psum, 1)

        @block.scalar
        def _(act):
            for t in range(TILES):
                act.wait_ge(in_psum, 2 * t + 1)
                act.activation(v[:, t, 0:BANK], ps[:, 2 * (t % 2), :], ACT.Copy).then_inc(copied[0], 1)

        @block.vector
        def _(dve):
            for t in range(TILES):
                dve.wait_ge(in_psum, 2 * t + 2)
                dve.tensor_copy(v[:, t, BANK:], ps[:, 2 * (t % 2) + 1, :]).then_inc(copied[1], 1)


def attention64(core, name, x, wqk, wv, wo1, wo2, tables, mask, gamma):
    ps, ident = core.ps, core.ident
    with ExitStack() as ctx:
        st = Stage(core, name, ctx)
        y = st.sb("y", [P, TILES, D])
        with ExitStack() as c1:
            s1 = Stage(core, name + "_main", c1)
            xt = s1.sb("xt", [P, TILES * P + BANK])
            v_all = s1.sb("v_all", [P, TILES, INNER])
            norm_turn(core, name + "_ln", x, xt)
            values64(core, name + "_v", xt, wv, v_all)
            heads64(core, s1, xt, v_all, y, wqk, wo1, wo2, tables, mask)
        norm_turn(core, name + "_ln2", y, xn=y, affine=(gamma, None), add_to=x, add_scale=1.0)


def heads64(core, st, xt, v_all, y, wqk, wo1, wo2, tables, mask):
    ps, ident, ctx = core.ps, core.ident, st.ctx
    NP = B * PAIRS
    w_sb = st.sb("wqk", [P, 4, INNER])
    wo1_sb, wo2_sb = st.sb("wo1", [P, PAIRS, D]), st.sb("wo2", [P, D])
    tab = st.sb("tab", [P, 4, BANK])
    mask_f, mask_r = st.sb("mask_f", [P, P]), st.sb("mask_r", [P, P], F32R)
    part = st.sb("part", [P, 4, BANK])
    q = st.sb("q", [P, 2, BANK])
    k_one = st.sb("k_one", [P, 2, 2, BANK])
    v_now = st.sb("v_now", [P, GROUP, INNER])
    neg_top = st.sb("neg_top", [P, 2, GROUP])
    total, rec = st.sb("total", [P, 2, GROUP]), st.sb("rec", [P, 2, GROUP])
    probs = st.sb("probs", [P, 2, CAUSAL])
    turned = st.sb("turned", [P, 2, CAUSAL])
    o_t = st.sb("o_t", [P, PAIRS, BANK])
    hid = st.sb("hid", [P, BANK])
    names = ("loaded", "zeroed", "set", "projected", "parted", "q_ready", "k_ready", "s_ready", "top_done", "exped",
             "inverted", "normed", "t_ready", "t_copied", "summed", "o_copied", "hidden", "relued", "y_ready", "y_copied")
    (loaded, zeroed, set_, projected, parted, q_ready, k_ready, s_ready, top_done, exped,
     inverted, normed, t_ready, t_copied, summed, o_copied, hidden, relued, y_ready, y_copied) = (st.sem(n) for n in names)
    v_loaded = [st.sem(f"v_loaded{j}") for j in range(PAIRS)]
    PS = [ps[:, k, :] for k in range(3)]
    PT = [ps[:, 3 + k, :] for k in range(3)]
    PO, PM = ps[:, 6, :], ps[:, 7, :]

    with core.nc.Block() as block:
        @block.sync
        def _(sp):
            for w in range(4):
                sp.dma_start(w_sb[:, w, :], wqk[w]).then_inc(loaded, 16)
            sp.dma_start(wo1_sb[:], wo1.rearrange("(j p) d -> p j d", p=P)).then_inc(loaded, 16)
            sp.dma_start(wo2_sb[:], wo2).then_inc(loaded, 16)
            sp.dma_start(tab[:], tables).then_inc(loaded, 16)
            sp.dma_start(mask_f[:], mask).then_inc(loaded, 16)
            sp.wait_ge(loaded, 128)

        @block.gpsimd
        def _(pool):
            pool.memset(xt[:, TILES * P:], 0.0).then_inc(zeroed, 1)
            pool.memset(k_one[:], 0.0).then_inc(zeroed, 1)

        @block.vector
        def _(dve):
            dve.wait_ge(loaded, 128)
            dve.tensor_copy(mask_r[:], mask_f[:]).then_inc(set_, 1)

    block = ctx.enter_context(core.nc.Block())

    @block.sync
    def _(sp):
        with sp.Fori(0, B) as b:
            for j in range(PAIRS):
                sp.wait_ge(summed, PAIRS * b + j + 1)
                c = slice(j * P, (j + 1) * P)
                sp.dma_start(v_now[:, :, c], v_all[:, bass.ts(b, GROUP), c]).then_inc(v_loaded[j], 16)
        for j in range(PAIRS):
            sp.wait_ge(v_loaded[j], 16 * B)

    @block.gpsimd
    def _(pool):
        def rotate(p, par):
            pool.wait_ge(parted, 4 * p + 2 + 1)
            pool.wait_ge(s_ready, 6 * p + 1)
            pool.wait_ge(k_ready, 2 * p + 1)
            pool.tensor_tensor(q[:, par, :], part[:, 0, :], part[:, 1, :], ALU.add).then_inc(q_ready, 1)
            pool.wait_ge(parted, 4 * p + 4 + 1)
            for hh in range(2):
                r = slice(HD64 * hh, HD64 * (hh + 1))
                if hh:
                    pool.wait_ge(k_ready, 2 * p + 1 + 1)
                pool.tensor_tensor(k_one[r, par, hh, :], part[r, 2, :], part[r, 3, :], ALU.add).then_inc(k_ready, 1)

        pool.sem_inc(q_ready, 1)
        pool.sem_inc(k_ready, 1)
        with pool.Fori(0, NP // 2) as p2:
            for par in range(2):
                rotate(2 * p2 + par, par)
        rotate(NP, 0)

    @block.tensor
    def _(pe):
        def project(p, b, j, w):
            pe.wait_ge(parted, 4 * p + w + 1)
            pe.matmul(PM, w_sb[:, w, j * P:(j + 1) * P], xt[:, bass.ts(b, BANK)], start=True, stop=True)\
              .then_inc(projected, 1)

        def scores(n, p, j, hh):
            if hh == 0:
                pe.wait_ge(q_ready, p + 1 + 1)
                pe.wait_ge(k_ready, 2 * (p + 1) + 1)
            for bank, chunks in enumerate(SCORE_BANKS):
                pe.wait_ge(exped, 3 * n + bank + 1 + 1)
                for qc in chunks:
                    _, at, _ = SCORE_AT[qc]
                    keys = (qc + 1) * P
                    pe.matmul(PS[bank][:, at:at + keys], q[:, j % 2, qc * P:(qc + 1) * P], k_one[:, j % 2, hh, 0:keys],
                              start=True, stop=False)
                    last = pe.matmul(PS[bank][:, at + keys - P:at + keys], core.ident_r[:], mask_r[:],
                                     start=False, stop=True)
                last.then_inc(s_ready, 1)

        def turn(n, hh):
            pe.wait_ge(normed, n + 1)
            for bank, chunks in enumerate(TURN_BANKS):
                pe.wait_ge(t_copied, 3 * n + bank + 1)
                for kc in chunks:
                    _, at, _ = TURN_AT[kc]
                    for qc in range(kc, GROUP):
                        row = SCORE_AT[qc][2] + kc * P
                        to = at + (qc - kc) * P
                        last = pe.transpose(PT[bank][:, to:to + P], probs[:, hh, row:row + P], ident[:])
                last.then_inc(t_ready, 1)

        def sums(b, p, j):
            pe.wait_ge(t_copied, 3 + 6 * (p + 1))
            pe.wait_ge(o_copied, p + 1)
            pe.wait_ge(v_loaded[j], 16 * (b + 1))
            for kc in range(GROUP):
                row, n = TURN_AT[kc][2], BANK - kc * P
                for hh in range(2):
                    r = slice(HD64 * hh, HD64 * (hh + 1))
                    c = (2 * j + hh) * HD64
                    last = pe.matmul(PO[r, kc * P:], v_now[:, kc, c:c + HD64], turned[:, hh, row:row + n],
                                     start=(kc == 0), stop=(kc == GROUP - 1))
            last.then_inc(summed, 1)

        pe.sem_inc(s_ready, 7)
        pe.sem_inc(t_ready, 7)
        pe.sem_inc(y_ready, 1)
        pe.sem_inc(summed, PAIRS)
        for w in range(4):
            project(0, 0, 0, w)
        with pe.Fori(0, B) as b:
            for j in range(PAIRS):
                p = PAIRS * b + j
                nxt, nxt_b = (j + 1) % PAIRS, b + (j + 1) // PAIRS
                scores(2 * p, p, j, 0)
                if j:
                    turn(2 * p - 1, 1)
                else:
                    pe.wait_ge(y_copied, b + 1)
                project(p + 1, nxt_b, nxt, 0)
                project(p + 1, nxt_b, nxt, 1)
                if j:
                    sums(b, p - 1, j - 1)
                scores(2 * p + 1, p, j, 1)
                turn(2 * p, 0)
                project(p + 1, nxt_b, nxt, 2)
                project(p + 1, nxt_b, nxt, 3)
            turn(PAIRS * 2 * b + 2 * PAIRS - 1, 1)
            sums(b, PAIRS * b + PAIRS - 1, PAIRS - 1)
            pe.wait_ge(parted, 4 * (PAIRS * b + PAIRS + 1) + 1)
            pe.wait_ge(o_copied, PAIRS * (b + 1) + 1)
            for j in range(PAIRS):
                last = pe.matmul(PM, wo1_sb[:, j, :], o_t[:, j, :], start=(j == 0), stop=(j == PAIRS - 1))
            last.then_inc(hidden, 1)
            pe.wait_ge(relued, b + 1)
            for t in range(GROUP):
                last = pe.matmul(PM[:, t * P:(t + 1) * P], hid[:, t * P:(t + 1) * P], wo2_sb[:], start=True, stop=True)
            last.then_inc(y_ready, 1)

    @block.scalar
    def _(act):
        def exps(n, par):
            for bank, chunks in enumerate(SCORE_BANKS):
                act.wait_ge(top_done, 3 * n + bank + 1)
                if bank == 0:
                    act.wait_ge(t_ready, 3 * n + 1)
                for qc in chunks:
                    _, at, row = SCORE_AT[qc]
                    keys = (qc + 1) * P
                    last = act.activation(probs[:, par, row:row + keys], PS[bank][:, at:at + keys], ACT.Exp,
                                          bias=neg_top[:, par, qc:qc + 1], accum_out=total[:, par, qc:qc + 1])
                last.then_inc(exped, 1)

        def copy_turned(n, p, hh):
            if hh == 0:
                act.wait_ge(summed, PAIRS + p)
            for bank, chunks in enumerate(TURN_BANKS):
                act.wait_ge(t_ready, 6 + 3 * n + bank + 1 + 1)
                row = TURN_AT[chunks[0]][2]
                size = sum(BANK - kc * P for kc in chunks)
                act.activation(turned[:, hh, row:row + size], PT[bank][:, 0:size], ACT.Copy).then_inc(t_copied, 1)

        def copy_out(p, j):
            act.wait_ge(summed, PAIRS + p + 1)
            act.activation(o_t[:, j, :], PO, ACT.Copy).then_inc(o_copied, 1)

        act.sem_inc(exped, 4)
        act.sem_inc(o_copied, 1)
        act.sem_inc(t_copied, 3)
        with act.Fori(0, B) as b:
            for j in range(PAIRS):
                p = PAIRS * b + j
                if j == 0:
                    act.wait_ge(y_ready, b + 1)
                exps(2 * p, 0)
                if j:
                    copy_turned(2 * p - 1, p - 1, 1)
                    copy_out(p - 1, j - 1)
                exps(2 * p + 1, 1)
                copy_turned(2 * p, p, 0)
            copy_turned(2 * PAIRS * b + 2 * PAIRS - 1, 0, 1)
            copy_out(PAIRS * b + PAIRS - 1, PAIRS - 1)
            act.wait_ge(hidden, b + 1)
            act.activation(hid[:], PM, ACT.Relu).then_inc(relued, 1)

    @block.vector
    def _(dve):
        def tops(n, par):
            dve.wait_ge(exped, 3 * n + 1)
            for bank, chunks in enumerate(SCORE_BANKS):
                dve.wait_ge(s_ready, 6 + 3 * n + bank + 1 + 1)
                for qc in chunks:
                    _, at, _ = SCORE_AT[qc]
                    last = dve.tensor_reduce(neg_top[:, par, qc:qc + 1], PS[bank][:, at:at + (qc + 1) * P], AX.X,
                                             ALU.max, negate=True)
                last.then_inc(top_done, 1)

        def norms(n, par):
            dve.wait_ge(exped, 3 + 3 * (n + 1) + 1)
            dve.reciprocal(rec[:, par, :], total[:, par, :]).then_inc(inverted, 1)
            dve.wait_ge(inverted, n + 1)
            for qc in range(GROUP):
                r = slice(SCORE_AT[qc][2], SCORE_AT[qc][2] + (qc + 1) * P)
                last = dve.tensor_scalar(probs[:, par, r], probs[:, par, r], rec[:, par, qc:qc + 1], None, ALU.mult)
            last.then_inc(normed, 1)

        def take_part(p, w):
            dve.wait_ge(projected, 4 * p + w + 1)
            if w < 2:
                dve.wait_ge(q_ready, p + 1)
            else:
                dve.wait_ge(k_ready, 2 * p + 1)
            dve.tensor_tensor(part[:, w, :], PM, tab[:, w, :], ALU.mult).then_inc(parted, 1)

        dve.sem_inc(parted, 1)
        dve.sem_inc(y_copied, 1)
        for w in range(4):
            take_part(0, w)
        with dve.Fori(0, B) as b:
            for j in range(PAIRS):
                p = PAIRS * b + j
                tops(2 * p, 0)
                take_part(p + 1, 0)
                take_part(p + 1, 1)
                norms(2 * p, 0)
                tops(2 * p + 1, 1)
                take_part(p + 1, 2)
                take_part(p + 1, 3)
                norms(2 * p + 1, 1)
            dve.wait_ge(y_ready, b + 1 + 1)
            dve.tensor_scalar(y[:, bass.ts(b, GROUP), :], PM.rearrange("p (t d) -> p t d", d=D), 1.0, None,
                              ALU.mult).then_inc(y_copied, 1)


HEADS4, HD4 = 4, 32


def attention_rows(core, name, xi, xt, y, wqkv, bqkv, wo, bo):
    ps, ident = core.ps, core.ident
    U = TILES // B
    with ExitStack() as ctx:
        st = Stage(core, name, ctx)
        w_sb, bias = st.sb("wqkv", [P, 3 * D]), st.sb("bias", [P, 3 * D])
        wo_sb, bo_sb = st.sb("wo", [P, D]), st.sb("bo", [P, 1, D])
        qkv = st.sb("qkv", [P, B, U, 3 * D])
        prod = st.sb("prod", [P, 2, B, D])
        sc = st.sb("sc", [P, U * B, B, HEADS4])
        mx, total = st.sb("mx", [P, U * B, 1, HEADS4]), st.sb("total", [P, U * B, 1, HEADS4])
        o = st.sb("o", [P, B, U, D])
        ot = st.sb("ot", [P, 2, BANK])
        names = ("loaded", "projected", "biased", "multiplied", "reduced", "chain", "shifted", "exped", "weights",
                 "turned", "copied", "mixed", "added")
        (loaded, projected, biased, multiplied, reduced, chain, shifted, exped, weights,
         turned, copied, mixed, added) = (st.sem(n) for n in names)
        block = ctx.enter_context(core.nc.Block())
        PQ = [ps[:, q, 0:3 * D] for q in range(2)]
        PT = [ps[:, 2 + q, :] for q in range(2)]
        PX = [ps[:, 4 + q, :] for q in range(2)]
        N = U * B
        order = [B_ * U + u for u in range(U) for B_ in range(B)]

        @block.sync
        def _(sp):
            sp.dma_start(w_sb[:], wqkv).then_inc(loaded, 16)
            sp.dma_start(bias[:], bqkv.partition_broadcast(P)).then_inc(loaded, 16)
            sp.dma_start(wo_sb[:], wo).then_inc(loaded, 16)
            sp.dma_start(bo_sb[:, 0, :], bo.partition_broadcast(P)).then_inc(loaded, 16)

        @block.tensor
        def _(pe):
            pe.wait_ge(loaded, 64)
            for n, t in enumerate(order):
                if n >= 2:
                    pe.wait_ge(biased, n - 1)
                pe.matmul(PQ[n % 2], xt[:, t * P:(t + 1) * P], w_sb[:], start=True, stop=True).then_inc(projected, 1)
            for s in range(B):
                pe.wait_ge(reduced, 2 * N)
                if s >= 2:
                    pe.wait_ge(copied, s - 1)
                for u in range(U):
                    last = pe.transpose(PT[s % 2][:, u * P:(u + 1) * P], o[:, s, u, :], ident[:])
                last.then_inc(turned, 1)
                pe.wait_ge(copied, s + 1)
                if s >= 2:
                    pe.wait_ge(added, s - 1)
                for u in range(U):
                    last = pe.matmul(PX[s % 2][:, u * P:(u + 1) * P], ot[:, s % 2, u * P:(u + 1) * P], wo_sb[:],
                                     start=True, stop=True)
                last.then_inc(mixed, 1)

        @block.scalar
        def _(act):
            act.wait_ge(shifted, 1)
            act.activation(sc[:], sc[:], ACT.Exp, scale=HD4 ** -0.5).then_inc(exped, 1)
            for s in range(B):
                act.wait_ge(turned, s + 1)
                if s >= 2:
                    act.wait_ge(mixed, s - 1)
                act.activation(ot[:, s % 2, :], PT[s % 2], ACT.Copy).then_inc(copied, 1)

        @block.gpsimd
        def _(pool):
            for n in range(N):
                u, s = n // B, n % B
                pool.wait_ge(biased, B * (u + 1))
                if n >= 2:
                    pool.wait_ge(reduced, n - 1)
                pool.tensor_tensor(prod[:, n % 2, :, :], qkv[:, s:s + 1, u, 0:D].to_broadcast([P, B, D]),
                                   qkv[:, :, u, D:2 * D], ALU.mult).then_inc(multiplied, 1)
            pool.wait_ge(weights, 1)
            wide = [P, B, HEADS4, HD4]
            for n in range(N):
                u, s = n // B, n % B
                pool.wait_ge(reduced, N + n - 1)
                pool.tensor_tensor(prod[:, n % 2, :, :].rearrange("p s (h d) -> p s h d", d=HD4),
                                   qkv[:, :, u, 2 * D:3 * D].rearrange("p s (h d) -> p s h d", d=HD4),
                                   sc[:, n, :, :].unsqueeze(3).to_broadcast(wide), ALU.mult).then_inc(multiplied, 1)

        @block.vector
        def _(dve):
            steps = [0]

            def link(ins):
                steps[0] += 1
                ins.then_inc(chain, 1)
                dve.wait_ge(chain, steps[0])

            dve.wait_ge(loaded, 64)
            for n, t in enumerate(order):
                dve.wait_ge(projected, n + 1)
                dve.tensor_tensor(qkv[:, t // U, t % U, :], PQ[n % 2], bias[:], ALU.add).then_inc(biased, 1)
            for n in range(N):
                dve.wait_ge(multiplied, n + 1)
                dve.tensor_reduce(sc[:, n, :, :], prod[:, n % 2, :, :].rearrange("p s (h d) -> p s h d", d=HD4),
                                  AX.X, ALU.add).then_inc(reduced, 1)
            dve.wait_ge(reduced, N)
            wide = [P, N, B, HEADS4]
            by_key = sc[:].rearrange("p n k h -> p n h k")
            link(dve.tensor_reduce(mx[:, :, 0, :], by_key, AX.X, ALU.max))
            dve.tensor_tensor(sc[:], sc[:], mx[:].to_broadcast(wide), ALU.subtract).then_inc(shifted, 1)
            dve.wait_ge(exped, 1)
            link(dve.tensor_reduce(total[:, :, 0, :], by_key, AX.X, ALU.add))
            link(dve.reciprocal(total[:], total[:]))
            dve.tensor_tensor(sc[:], sc[:], total[:].to_broadcast(wide), ALU.mult).then_inc(weights, 1)
            for n in range(N):
                dve.wait_ge(multiplied, N + n + 1)
                dve.tensor_reduce(o[:, n % B, n // B, :], prod[:, n % 2, :, :].rearrange("p s c -> p c s"),
                                  AX.X, ALU.add).then_inc(reduced, 1)
            for s in range(B):
                rows = slice(U * s, U * (s + 1))
                dve.wait_ge(mixed, s + 1)
                link(dve.tensor_tensor(y[:, rows, :], PX[s % 2].rearrange("p (u d) -> p u d", d=D), xi[:, rows, :],
                                       ALU.add))
                dve.tensor_tensor(y[:, rows, :], y[:, rows, :], bo_sb[:].to_broadcast([P, U, D]),
                                  ALU.add).then_inc(added, 1)


def store(core, out):
    with ExitStack() as ctx:
        st = Stage(core, "store", ctx)
        stored = st.sem("stored")
        block = ctx.enter_context(core.nc.Block())

        @block.sync
        def _(sp):
            sp.dma_start(out.rearrange("b (t p) d -> p (b t) d", p=P), core.x[:]).then_inc(stored, 16)
            sp.wait_ge(stored, 16)


def silu_experts(core, name, a):
    with ExitStack() as c:
        xt = Stage(core, name, c).sb("xt", [P, TILES * P])
        norm_turn(core, name + "_ln", core.x, xt)
        moe(core, name, xt, core.x, a["L0_W1"], a["L0_W2"], a["L0_Wr"], top2=True)


def row_experts(core, name, a):
    with ExitStack() as c:
        st = Stage(core, name, c)
        xt, xi, y = st.sb("xt", [P, TILES * P]), st.sb("xi", [P, TILES, D]), st.sb("y", [P, TILES, D])
        norm_turn(core, name + "_ln0", core.x, xt, xn=xi)
        attention_rows(core, name + "_mha", xi, xt, y, a["L1_Wqkv"], a["L1_bqkv"], a["L1_Wo"], a["L1_bo"])
        norm_turn(core, name + "_ln1", y, xt, xn=y, affine=(a["L1_g1"], a["L1_be1"]))
        moe(core, name, xt, y, a["L1_W1"], a["L1_W2"], a["L1_Wg"], top2=False, b1=a["L1_b1"], b2=a["L1_b2"])
        norm_turn(core, name + "_ln2", y, xn=y, affine=(a["L1_g2"], a["L1_be2"]), add_to=core.x)


def program(nc, a, out, upto=99, start=0):
    with ExitStack() as ctx:
        core = Core(nc, ctx)
        setup(core, a["x"])
        run = lambda n: start < n <= upto
        if run(1):
            silu_experts(core, "f0a", a)
        if run(2):
            attention8(core, "a8", core.x, a["L0_Wq"], a["L0_Wk"], a["L0_Wv"], a["rope8"], a["rows8"])
        if run(3):
            silu_experts(core, "f0b", a)
        if run(4):
            row_experts(core, "r0", a)
        if run(5):
            attention64(core, "a64", core.x, a["L1_Wqk"], a["L1_Wv"], a["L1_Wo1"], a["L1_Wo2"], a["rope64"],
                        a["causal"], a["L1_gamma"])
        if run(6):
            row_experts(core, "r1", a)
        store(core, out)


def layouts(i):
    c = np.ascontiguousarray
    t = lambda n: np.asarray(i[n])
    chunks = lambda w: c(w.reshape(E, FC, P, D).transpose(0, 2, 1, 3))
    theta = 1.0 / 10000.0 ** (np.arange(0, HD8, 2, dtype=np.float32) / HD8)
    angle = np.arange(B, dtype=np.float32)[:, None] * np.concatenate([theta, theta])[None, :]
    sign = np.where(np.arange(HD8) < HD8 // 2, 1.0, -1.0)
    rope8 = np.zeros((P, B + 1), np.float32)
    rope8[:, :B] = np.tile((np.cos(angle) + sign * np.sin(angle)).T, (P // HD8, 1))
    row = np.arange(P) % ROWS
    rows8 = np.stack([row == 0, -((row >= 16) & (row < 24)).astype(np.float32), -(row >= 24).astype(np.float32)], 1)
    inv_freq = 1.0 / 10000.0 ** (np.arange(0, HD64, 2, dtype=np.float32) / HD64)
    freqs = np.arange(S, dtype=np.float32)[None, :] * np.tile(inv_freq, 2)[:, None]
    swap = np.where(np.arange(HD64) < HD64 // 2, -1.0, 1.0)[:, None]
    both = np.stack([np.cos(freqs), swap * np.sin(freqs)], 1)
    rope64 = np.tile(np.concatenate([both * HD64 ** -0.5, both], 1), (2, 1, 1)).astype(np.float32)
    w = t("L1_attn_W_qkv").reshape(D, 3, HEADS64, 2, HD64 // 2)
    flat = lambda m: m.reshape(D, INNER)
    wqk = np.stack([flat(w[:, 0]), flat(w[:, 0, :, ::-1]), flat(w[:, 1]), flat(w[:, 1, :, ::-1])])
    return {
        "x": c(t("L0_attn_x")),
        "L1_Wqk": c(wqk),
        "L1_Wv": c(flat(w[:, 2])),
        "L1_Wo1": c(t("L1_attn_W_o1")),
        "L1_Wo2": c(t("L1_attn_W_o2")),
        "L1_gamma": c(t("L1_attn_gamma")),
        "rope64": rope64,
        "causal": np.triu(np.full((P, P), BIG, np.float32), 1),
        "L0_Wq": c(t("L0_attn_Wq").T),
        "L0_Wk": c(t("L0_attn_Wk").T),
        "L0_Wv": c(t("L0_attn_Wv").T),
        "L1_Wqkv": c(t("L1_ffn_Wqkv").T),
        "L1_bqkv": c(t("L1_ffn_bqkv")),
        "L1_Wo": c(t("L1_ffn_Wo").T),
        "L1_bo": c(t("L1_ffn_bo")),
        "L1_g1": c(t("L1_ffn_g1")),
        "L1_be1": c(t("L1_ffn_be1")),
        "L1_g2": c(t("L1_ffn_g2")),
        "L1_be2": c(t("L1_ffn_be2")),
        "L1_Wg": c(t("L1_ffn_Wg").T),
        "L1_W1": c(t("L1_ffn_W1")),
        "L1_b1": c(t("L1_ffn_b1").reshape(E, FC, P).transpose(2, 0, 1).reshape(P, E * FC)),
        "L1_W2": chunks(t("L1_ffn_W2")),
        "L1_b2": c(t("L1_ffn_b2")),
        "rope8": rope8,
        "rows8": rows8.astype(np.float32),
        "L0_W1": c(t("L0_ffn_W1").transpose(0, 2, 1)),
        "L0_W2": chunks(t("L0_ffn_W2").transpose(0, 2, 1)),
        "L0_Wr": c(t("L0_ffn_Wr").T),
    }


def kernel(**inputs):
    import concourse.bacc as bacc
    from concourse.bass_utils import run_bass_kernel_spmd

    nc = bacc.Bacc("TRN2", target_bir_lowering=False, num_devices=1)
    arrays = layouts(inputs)
    aps = {n: nc.dram_tensor(f"in_{n}", v.shape, mybir.dt.from_np(v.dtype), kind="ExternalInput").ap()
           for n, v in arrays.items()}
    out = nc.dram_tensor("out", (B, S, D), F32, kind="ExternalOutput").ap()
    program(nc, aps, out)
    r = run_bass_kernel_spmd(nc, [{f"in_{n}": v for n, v in arrays.items()}], core_ids=[0])
    return r.results[0]["out"]
```

```python
from contextlib import ExitStack

import numpy as np

import concourse.bass as bass
from concourse import mybir

F32 = mybir.dt.float32
F32R = mybir.dt.float32r
U32 = mybir.dt.uint32
ALU = mybir.AluOpType
ACT = mybir.ActivationFunctionType
AX = mybir.AxisListType

P = 128
B, S, D = 4, 512, 128
TILES = B * S // P
GROUP = 4
GROUPS = TILES // GROUP
E, DFF = 8, 512
FC = DFF // P
EPS = 1e-5
BANK = 512


class Core:

    def __init__(self, nc, ctx):
        self.nc, self.ctx = nc, ctx
        self.cleared, self.cleared_at = 0, {}
        self.x = self.sb("x_res", [P, TILES, D])
        self.ident = self.sb("ident", [P, P])
        self.ident_r = self.sb("ident_r", [P, P], F32R)
        self.neg_half = self.sb("neg_half", [P, TILES])
        self.iota8 = self.sb("iota8", [P, TILES, E])
        self.ps = ctx.enter_context(nc.psum_tensor("ps", [P, 8, BANK], F32))

    def sb(self, name, shape, dt=F32):
        return self.ctx.enter_context(self.nc.sbuf_tensor(name, shape, dt))


class Stage:

    def __init__(self, core, name, ctx):
        self.core, self.name, self.ctx, self.nc = core, name, ctx, core.nc
        self.sems, self.nums = [], []
        ctx.callback(self.clear)

    def clear(self):
        if self.sems:
            self.nc.clear_and_free_semaphores(self.sems)
            self.core.cleared += 1
            self.core.cleared_at.update({n: self.core.cleared for n in self.nums})

    def sb(self, name, shape, dt=F32):
        return self.ctx.enter_context(self.nc.sbuf_tensor(f"{self.name}_{name}", shape, dt))

    def sem(self, name):
        num = min(self.nc.free_semaphores, key=lambda n: self.core.cleared_at.get(n, 0))
        self.sems.append(self.nc.alloc_semaphore(name=f"{self.name}_{name}", num=num))
        self.nums.append(num)
        return self.sems[-1]


def setup(core, x_in):
    nc = core.nc
    with ExitStack() as ctx:
        st = Stage(core, "setup", ctx)
        x_loaded, zeroed, ident_built, consts = (st.sem(n) for n in ("x_loaded", "zeroed", "ident_built", "consts"))
        block = ctx.enter_context(nc.Block())

        @block.sync
        def _(sp):
            sp.dma_start(core.x[:], x_in.rearrange("b (t p) d -> p (b t) d", p=P)).then_inc(x_loaded, 16)
            sp.wait_ge(x_loaded, 16)

        @block.gpsimd
        def _(pool):
            pool.memset(core.ident[:], 0.0).then_inc(zeroed, 1)
            pool.memset(core.neg_half[:], -0.5).then_inc(consts, 1)
            pool.iota(core.iota8[:], [[0, TILES], [1, E]], base=0, channel_multiplier=0,
                      allow_small_or_imprecise_dtypes=True).then_inc(consts, 1)
            pool.wait_ge(zeroed, 1)
            pool.affine_select(out=core.ident[:], in_=core.ident[:], compare_op=ALU.not_equal, fill=1.0,
                               base=0, pattern=[[-1, P]], channel_multiplier=1).then_inc(ident_built, 1)

        @block.vector
        def _(dve):
            dve.wait_ge(ident_built, 1)
            dve.tensor_copy(core.ident_r[:], core.ident[:]).then_inc(consts, 1)


def norm_turn(core, name, src, xt=None, xn=None, w_v=None, v=None, affine=None, add_to=None, add_scale=0.5,
              parts=None, first=None):
    ps, ident = core.ps, core.ident
    beta = affine is not None and affine[1] is not None
    with ExitStack() as ctx:
        st = Stage(core, name, ctx)
        stats = st.sb("stats", [P, TILES, 6])
        moments = st.sb("moments", [P, TILES, 2])
        rstd = st.sb("rstd", [P, TILES])
        if xn is None:
            xn = st.sb("xn", [P, TILES, D])
        have_stats, have_moments, var_eps, have_rstd, normed, turned, copied = (
            st.sem(n) for n in ("have_stats", "have_moments", "var_eps", "have_rstd", "normed", "turned", "copied"))
        if affine is not None:
            gb = st.sb("gb", [P, 2, D])
            gb_loaded, scaled, shifted = (st.sem(n) for n in ("gb_loaded", "scaled", "shifted"))
        if v is not None:
            w_sb = st.sb("w_v", [P, D])
            w_loaded, v_in_psum, v_copied = (st.sem(n) for n in ("w_loaded", "v_in_psum", "v_copied"))
        if parts is not None:
            high = st.sem("high")
        if first is not None:
            first_loaded, first_high = st.sem("first_loaded"), st.sem("first_high")
        block = ctx.enter_context(core.nc.Block())
        PT = [ps[:, q, :] for q in range(2)]
        PV = [ps[:, 2 + q, :] for q in range(2)]
        tiles = lambda g: range(GROUP * g, GROUP * (g + 1))
        rows = lambda g: slice(GROUP * g, GROUP * (g + 1))
        wide = [P, GROUP, D]
        whole = lambda g: (normed, GROUP * (g + 1)) if affine is None else (shifted if beta else scaled, g + 1)

        @block.sync
        def _(sp):
            if v is not None:
                sp.dma_start(w_sb[:], w_v).then_inc(w_loaded, 16)
            if affine is not None:
                for k, w in enumerate(affine):
                    if w is not None:
                        sp.dma_start(gb[:, k, :], w.partition_broadcast(P)).then_inc(gb_loaded, 16)
            if first is not None:
                w1, w1_f, _, _, w2, w2_f = first
                sp.dma_start(w1_f, w1).then_inc(first_loaded, 16)
                sp.dma_start(w2_f, w2).then_inc(first_loaded, 16)

        @block.vector
        def _(dve):
            def measure(g):
                for t in tiles(g):
                    dve.bn_stats(stats[:, t, :], src[:, t, :]).then_inc(have_stats, 1)
                for t in tiles(g):
                    dve.wait_ge(have_stats, t + 1)
                    dve.bn_aggr(moments[:, t, :], stats[:, t, :]).then_inc(have_moments, 1)

            def normalise(g):
                dve.wait_ge(have_rstd, g + 1)
                for t in tiles(g):
                    dve.tensor_scalar(xn[:, t, :], src[:, t, :], moments[:, t, 0:1], rstd[:, t:t + 1],
                                      ALU.subtract, ALU.mult).then_inc(normed, 1)
                if affine is not None:
                    if g == 0:
                        dve.wait_ge(gb_loaded, 16 * sum(w is not None for w in affine))
                    dve.wait_ge(normed, GROUP * (g + 1))
                    z = xn[:, rows(g), :]
                    dve.tensor_tensor(z, z, gb[:, 0:1, :].to_broadcast(wide), ALU.mult).then_inc(scaled, 1)

            def finish(g):
                if add_to is not None:
                    dve.wait_ge(*whole(g))
                    r = add_to[:, rows(g), :]
                    dve.scalar_tensor_tensor(out=r, in0=xn[:, rows(g), :], scalar=add_scale, in1=r,
                                             op0=ALU.mult, op1=ALU.add)
                if parts is not None:
                    tok = slice(g * BANK, (g + 1) * BANK)
                    dve.wait_ge(high, g + 1)
                    dve.tensor_tensor(parts[1][:, tok], xt[:, tok], parts[0][:, tok].bitcast(F32), ALU.subtract)

            measure(0)
            for g in range(1, GROUPS):
                measure(g)
                normalise(g - 1)
                if g >= 3:
                    finish(g - 3)
            normalise(GROUPS - 1)
            for g in range(GROUPS - 3, GROUPS):
                finish(g)

        @block.gpsimd
        def _(pool):
            def root(g):
                r = rstd[:, rows(g)]
                pool.wait_ge(have_moments, GROUP * (g + 1))
                pool.tensor_scalar(r, moments[:, rows(g), 1], EPS, None, ALU.add).then_inc(var_eps, 1)
                pool.wait_ge(var_eps, g + 1)
                pool.tensor_tensor(r, r, core.neg_half[:, rows(g)], ALU.pow).then_inc(have_rstd, 1)

            def shift(g):
                if beta:
                    z = xn[:, rows(g), :]
                    pool.wait_ge(scaled, g + 1)
                    pool.tensor_tensor(z, z, gb[:, 1:2, :].to_broadcast(wide), ALU.add).then_inc(shifted, 1)

            root(0)
            for g in range(1, GROUPS):
                root(g)
                shift(g - 1)
            shift(GROUPS - 1)
            if first is not None:
                _, w1_f, w1h, w1l, _, _ = first
                pool.wait_ge(first_loaded, 32)
                pool.tensor_copy(w1h, w1_f).then_inc(first_high, 1)
                pool.wait_ge(first_high, 1)
                pool.tensor_tensor(w1l, w1_f, w1h.bitcast(F32), ALU.subtract)

        if xt is None:
            return

        @block.tensor
        def _(pe):
            if v is not None:
                pe.wait_ge(w_loaded, 16)
            for g in range(GROUPS):
                pe.wait_ge(*whole(g))
                if g >= 2:
                    pe.wait_ge(copied, g - 1)
                for j in range(GROUP):
                    last = pe.transpose(PT[g % 2][:, j * P:(j + 1) * P], xn[:, GROUP * g + j, :], ident[:])
                last.then_inc(turned, 1)
                if v is not None:
                    pe.wait_ge(copied, g + 1)
                    if g >= 2:
                        pe.wait_ge(v_copied, g - 1)
                    for j in range(GROUP):
                        t = GROUP * g + j
                        last = pe.matmul(PV[g % 2][:, j * P:(j + 1) * P], xt[:, t * P:(t + 1) * P], w_sb[:],
                                         start=True, stop=True)
                    last.then_inc(v_in_psum, 1)

        @block.scalar
        def _(act):
            for g in range(GROUPS):
                tok = slice(g * BANK, (g + 1) * BANK)
                act.wait_ge(turned, g + 1)
                act.activation(xt[:, tok], PT[g % 2], ACT.Copy).then_inc(copied, 1)
                if v is not None:
                    act.wait_ge(v_in_psum, g + 1)
                    act.activation(v[:, rows(g), :], PV[g % 2].rearrange("p (j d) -> p j d", d=D),
                                   ACT.Copy).then_inc(v_copied, 1)
                if parts is not None:
                    act.wait_ge(copied, g + 1)
                    act.activation(parts[0][:, tok], xt[:, tok], ACT.Copy).then_inc(high, 1)


def moe(core, name, src, acc, w1, w2, wr, top2, b1=None, b2=None, **norm):
    with ExitStack() as ctx:
        st = Stage(core, name, ctx)
        xt = st.sb("xt", [P, TILES * P])
        xh = st.sb("xh", [P, TILES * P], F32R)
        xl = st.sb("xl", [P, TILES * P], F32R)
        w1_f = st.sb("w1_f", [P, 2, DFF])
        w1h = st.sb("w1h", [P, 2, DFF], F32R)
        w1l = st.sb("w1l", [P, 2, DFF], F32R)
        w2_f = st.sb("w2_f", [P, 2, FC, D])
        first = (w1[0], w1_f[:, 0, :], w1h[:, 0, :], w1l[:, 0, :], w2[0], w2_f[:, 0, :, :])
        norm_turn(core, name + "_ln", src, xt, parts=(xh, xl), first=first, **norm)
        with ExitStack() as c2:
            experts(core, Stage(core, name + "_exp", c2), acc, xt, xh, xl, w1_f, w1h, w1l, w2_f,
                    w1, w2, wr, top2, b1, b2)


def experts(core, st, acc, xt, xh, xl, w1_f, w1h, w1l, w2_f, w1, w2, wr, top2, b1, b2):
    ps, ident = core.ps, core.ident
    h = st.sb("h", [P, 2, FC, GROUP * P])
    w1_loaded, w2_loaded = ([st.sem(f"{n}{q}") for q in range(2)] for n in ("w1_loaded", "w2_loaded"))
    w1_high, w1_split = st.sem("w1_high"), st.sem("w1_split")
    h_in_psum = st.sem("h_in_psum")
    h_ready = st.sem("h_ready")
    y_in_psum = st.sem("y_in_psum")
    y_added = st.sem("y_added")
    w_route = st.sb("w_route", [P, E])
    gate = st.sb("gate", [P, TILES, E])
    lg = st.sb("lg", [P, TILES, E])
    best = st.sb("best", [P, TILES, 8])
    place_i = st.sb("place_i", [P, TILES, 8], U32)
    place = st.sb("place", [P, TILES, 8])
    small = st.sb("small", [P, 4, TILES])
    second_mask = st.sb("second_mask", [P, TILES, E])
    gap_t, exp_t, g1_t, g2_t = (small[:, k, :] for k in range(4))
    wr_loaded, logits, chain, gap, gap_exp, ranked, placed, gated = (
        st.sem(n) for n in ("wr_loaded", "logits", "chain", "gap", "gap_exp", "ranked", "placed", "gated"))
    if b1 is not None:
        b1_sb, b1_now = st.sb("b1", [P, E * FC]), st.sb("b1_now", [P, 2, FC])
        b2_sb = st.sb("b2", [E, D])
        gt = st.sb("gt", [E, 2, GROUP * P])
        b1_loaded, b1_set, b2_loaded, g_turned, g_copied, biased, b_added = (
            st.sem(n) for n in ("b1_loaded", "b1_set", "b2_loaded", "g_turned", "g_copied", "biased", "b_added"))
    block = st.ctx.enter_context(core.nc.Block())
    STEPS = 2 * GROUPS
    PH = [ps[:, 2 * k:2 * k + 2, :] for k in range(2)]
    PY = [ps[:, 4 + k, :] for k in range(2)]
    PL, PB = ps[:, 6, :], ps[:, 7, :]

    @block.sync
    def _(sp):
        sp.dma_start(w_route[:], wr).then_inc(wr_loaded, 16)
        if b1 is not None:
            sp.dma_start(b1_sb[:], b1).then_inc(b1_loaded, 16)
            sp.dma_start(b2_sb[:], b2).then_inc(b2_loaded, 16)
        sp.sem_inc(w2_loaded[0], 16)
        for e in range(1, E):
            q = e % 2
            if e >= 2:
                sp.wait_ge(w1_split, e - 1)
            sp.dma_start(w1_f[:, q, :], w1[e]).then_inc(w1_loaded[q], 16)
            if e >= 2:
                sp.wait_ge(y_in_psum, 2 + GROUPS * (e - 1))
            sp.dma_start(w2_f[:, q, :, :], w2[e]).then_inc(w2_loaded[q], 16)

    @block.gpsimd
    def _(pool):
        pool.sem_inc(w1_split, 1)
        if b1 is not None:
            pool.wait_ge(b1_loaded, 16)
        for e in range(E):
            q = e % 2
            if b1 is not None:
                if e >= 2:
                    pool.wait_ge(h_ready, 2 + 2 * GROUPS * (e - 1))
                pool.tensor_copy(b1_now[:, q, :], b1_sb[:, e * FC:(e + 1) * FC]).then_inc(b1_set, 1)
            if e == 0:
                continue
            pool.wait_ge(w1_loaded[q], 16 * ((e + 1) // 2))
            if e >= 2:
                pool.wait_ge(h_in_psum, 2 * GROUPS * (e - 1))
            pool.tensor_copy(w1h[:, q, :], w1_f[:, q, :]).then_inc(w1_high, 1)
            pool.wait_ge(w1_high, e)
            pool.tensor_tensor(w1l[:, q, :], w1_f[:, q, :], w1h[:, q, :].bitcast(F32),
                               ALU.subtract).then_inc(w1_split, 1)

    @block.tensor
    def _(pe):
        def first_layer(pair, s):
            e, t = (s // GROUPS) % 2, s % GROUPS
            if t == 0:
                pe.wait_ge(w1_split, 2 * pair + s // GROUPS + 1)
            for k in range(2):
                pe.wait_ge(h_ready, 2 * (STEPS * pair + s) + k + 1)
                for c in range(2):
                    w = slice((2 * k + c) * P, (2 * k + c + 1) * P)
                    x = slice(t * GROUP * P, (t + 1) * GROUP * P)
                    pe.matmul(PH[k][:, c, :], w1h[:, e, w], xh[:, x], start=True, stop=False)
                    pe.matmul(PH[k][:, c, :], w1h[:, e, w], xl[:, x], start=False, stop=False)
                    last = pe.matmul(PH[k][:, c, :], w1l[:, e, w], xh[:, x], start=False, stop=True)
                last.then_inc(h_in_psum, 1)

        def second_layer(pair, s):
            e, q, n = s // GROUPS, s % 2, STEPS * pair + s
            if s % GROUPS == 0:
                pe.wait_ge(w2_loaded[e], 16 * (pair + 1))
            pe.wait_ge(h_ready, 2 + 2 * (n + 1))
            pe.wait_ge(y_added, n + 1)
            for j in range(GROUP):
                for f in range(FC):
                    last = pe.matmul(PY[q][:, j * P:(j + 1) * P], h[:, q, f, j * P:(j + 1) * P],
                                     w2_f[:, e, f, :], start=(f == 0), stop=(f == FC - 1))
            last.then_inc(y_in_psum, 1)

        def bias_gates():
            pe.wait_ge(gated, 1)
            pe.wait_ge(b2_loaded, 16)
            for g in range(GROUPS):
                if g >= 1:
                    pe.wait_ge(g_copied, g)
                for j in range(GROUP):
                    last = pe.transpose(PL[0:E, j * P:(j + 1) * P], gate[:, GROUP * g + j, :], ident[:])
                last.then_inc(g_turned, 1)
                pe.wait_ge(g_copied, g + 1)
                if g >= 1:
                    pe.wait_ge(b_added, g)
                for j in range(GROUP):
                    last = pe.matmul(PB[:, j * P:(j + 1) * P], gt[:, g % 2, j * P:(j + 1) * P], b2_sb[:],
                                     start=True, stop=True)
                last.then_inc(biased, 1)

        pe.sem_inc(y_in_psum, 2)
        first_layer(0, 0)
        pe.wait_ge(wr_loaded, 16)
        for t in range(TILES):
            last = pe.matmul(PL[:, t * E:(t + 1) * E], xt[:, t * P:(t + 1) * P], w_route[:], start=True, stop=True)
        last.then_inc(logits, 1)
        with pe.Fori(0, E // 2 - 1) as pair:
            for s in range(STEPS):
                first_layer(pair, s + 1)
                second_layer(pair, s)
        for s in range(STEPS):
            if s + 1 < STEPS:
                first_layer(E // 2 - 1, s + 1)
            second_layer(E // 2 - 1, s)
        if b2 is not None:
            bias_gates()

    @block.scalar
    def _(act):
        def hidden(pair, s):
            n, q, e = STEPS * pair + s, s % 2, s // GROUPS
            if b1 is not None and s % GROUPS == 0:
                act.wait_ge(b1_set, 2 * pair + e + 1)
            act.wait_ge(y_in_psum, n + 1)
            for k in range(2):
                act.wait_ge(h_in_psum, 2 * n + k + 1)
                if b1 is None:
                    act.activation(h[:, q, 2 * k:2 * k + 2, :], PH[k], ACT.Silu).then_inc(h_ready, 1)
                else:
                    for c in range(2):
                        f = 2 * k + c
                        last = act.activation(h[:, q, f, :], PH[k][:, c, :], ACT.Relu,
                                              bias=b1_now[:, e, f:f + 1])
                    last.then_inc(h_ready, 1)

        act.sem_inc(h_ready, 2)
        peeled = 0
        if top2:
            peeled = 1
            hidden(0, 0)
            act.wait_ge(gap, 1)
            act.activation(exp_t, gap_t, ACT.Exp).then_inc(gap_exp, 1)
            for s in range(1, STEPS):
                hidden(0, s)
        with act.Fori(peeled, E // 2) as pair:
            for s in range(STEPS):
                hidden(pair, s)
        if b2 is not None:
            for g in range(GROUPS):
                act.wait_ge(g_turned, g + 1)
                if g >= 2:
                    act.wait_ge(biased, g - 1)
                act.activation(gt[:, g % 2, :], PL[0:E, :], ACT.Copy).then_inc(g_copied, 1)

    @block.vector
    def _(dve):
        steps = [0]

        def link(ins):
            steps[0] += 1
            ins.then_inc(chain, 1)
            dve.wait_ge(chain, steps[0])

        def gates():
            dve.wait_ge(logits, 1)
            link(dve.tensor_copy(lg[:], PL[:, 0:TILES * E].rearrange("p (t e) -> p t e", e=E)))
            for t in range(TILES):
                dve.max(best[:, t, :], lg[:, t, :]).then_inc(ranked, 1)
            for t in range(TILES):
                dve.wait_ge(ranked, t + 1)
                dve.max_index(place_i[:, t, :], best[:, t, :], lg[:, t, :]).then_inc(placed, 1)
            dve.wait_ge(placed, TILES)
            link(dve.tensor_copy(place[:], place_i[:]))
            wide = [P, TILES, E]
            first, second = (place[:, :, k:k + 1].to_broadcast(wide) for k in range(2))
            if not top2:
                dve.tensor_tensor(gate[:], core.iota8[:], first, ALU.is_equal).then_inc(gated, 1)
            else:
                dve.tensor_tensor(gap_t, best[:, :, 1], best[:, :, 0], ALU.subtract).then_inc(gap, 1)
                link(dve.tensor_tensor(second_mask[:], core.iota8[:], second, ALU.is_equal))
                link(dve.tensor_tensor(gate[:], core.iota8[:], first, ALU.is_equal))
                dve.wait_ge(gap_exp, 1)
                link(dve.tensor_scalar(g2_t, exp_t, 1.0, 2.0, ALU.add, ALU.mult))
                link(dve.reciprocal(g1_t, g2_t))
                link(dve.tensor_tensor(g2_t, g1_t, exp_t, ALU.mult))
                link(dve.tensor_tensor(gate[:], gate[:], g1_t.unsqueeze(2).to_broadcast(wide), ALU.mult))
                link(dve.tensor_tensor(second_mask[:], second_mask[:], g2_t.unsqueeze(2).to_broadcast(wide), ALU.mult))
                dve.tensor_tensor(gate[:], gate[:], second_mask[:], ALU.add).then_inc(gated, 1)

        gates()
        dve.wait_ge(gated, 1)
        dve.sem_inc(y_added, 2)
        with dve.Fori(0, E) as e:
            for t in range(GROUPS):
                n, q = GROUPS * e + t, t % 2
                dve.wait_ge(y_in_psum, n + 3)
                dve.wait_ge(y_added, n + 1)
                for j in range(GROUP):
                    tile = GROUP * t + j
                    last = dve.scalar_tensor_tensor(
                        out=acc[:, tile, :], in0=PY[q][:, j * P:(j + 1) * P],
                        scalar=gate[:, tile, bass.ds(e, 1)], in1=acc[:, tile, :], op0=ALU.mult, op1=ALU.add)
                last.then_inc(y_added, 1)
        if b2 is not None:
            dve.wait_ge(y_added, 2 + E * GROUPS)
            for g in range(GROUPS):
                dve.wait_ge(biased, g + 1)
                a = acc[:, GROUP * g:GROUP * (g + 1), :].rearrange("p a d -> p (a d)")
                dve.tensor_tensor(a, a, PB, ALU.add).then_inc(b_added, 1)


HEADS8, HD8 = 16, 8
PER = 4
HGROUPS = HEADS8 // PER
ROWS = P // PER


def attention8(core, name, x, wq, wk, wv, rope, row_consts):
    ps, ident = core.ps, core.ident
    NG = B * HGROUPS
    with ExitStack() as ctx:
        st = Stage(core, name, ctx)
        xt = st.sb("xt", [P, TILES * P + BANK])
        v = st.sb("v", [P, TILES, D])
        norm_turn(core, name + "_ln", x, xt, w_v=wv, v=v)

        wq_c, wk_c = st.sb("wq_c", [P, D]), st.sb("wk_c", [P, D])
        wq_r, wk_r = (st.sb(n, [P, HGROUPS, PER, ROWS]) for n in ("wq_r", "wk_r"))
        rope_sb = st.sb("rope", [P, B + 1])
        rope_now = st.sb("rope_now", [P, 1])
        consts = st.sb("consts", [P, 3])
        zero = st.sb("zero", [P, BANK])
        tq, tk, hq, hk = (st.sb(n, [P, BANK]) for n in ("tq", "tk", "hq", "hk"))
        k_all = st.sb("k_all", [P, BANK], F32R)
        k_one = st.sb("k_one", [P, HGROUPS, PER, BANK], F32R)
        q_all = st.sb("q_all", [P, HGROUPS, BANK], F32R)
        tops = st.sb("tops", [P, 2, GROUP, P], F32R)
        probs = st.sb("probs", [P, 2, GROUP, PER, BANK])
        v_one = st.sb("v_one", [P, GROUP, HEADS8, ROWS])
        o_sb = st.sb("o_sb", [P, BANK])
        rec = st.sb("rec", [P, GROUP, PER])
        o_n = st.sb("o_n", [P, GROUP, PER, HD8])
        names = ("loaded", "zeroed", "placed", "filled", "projected", "roped", "high", "q_split", "k_split",
                 "rope_set", "top_filled", "top_read", "rows_in_psum", "q_ready", "scored", "exped", "summed",
                 "v_set", "o_copied", "o_turned", "o_added", "inverted", "scaled")
        (loaded, zeroed, placed, filled, projected, roped, high, q_split, k_split,
         rope_set, top_filled, top_read, rows_in_psum, q_ready, scored, exped, summed,
         v_set, o_copied, o_turned, o_added, inverted, scaled) = (st.sem(n) for n in names)
        k_spread = [st.sem(f"k_spread{gi}") for gi in range(HGROUPS)]
        PTOP = [ps[:, 2 * k:2 * k + 2, :] for k in range(2)]
        PSC = [ps[:, 4 + k, :] for k in range(2)]
        PO, PM = ps[:, 6, :], ps[:, 7, :]

        with core.nc.Block() as block:
            @block.sync
            def _(sp):
                for dst, src in ((wq_c, wq), (wk_c, wk), (rope_sb, rope), (consts, row_consts)):
                    sp.dma_start(dst[:], src).then_inc(loaded, 16)

            @block.gpsimd
            def _(pool):
                pool.memset(xt[:, TILES * P:], 0.0).then_inc(zeroed, 1)
                pool.memset(zero[:], 0.0).then_inc(zeroed, 1)
                pool.memset(v_one[:], 0.0).then_inc(zeroed, 1)
                pool.memset(k_one[:].bitcast(F32), 0.0).then_inc(zeroed, 1)
                pool.wait_ge(zeroed, 3)
                pool.memset(v_one[:, :, :, HD8:HD8 + 1], 1.0).then_inc(filled, 1)

            @block.vector
            def _(dve):
                dve.memset(wq_r[:], 0.0).then_inc(placed, 1)
                dve.memset(wk_r[:], 0.0).then_inc(placed, 1)
                dve.memset(tops[:].bitcast(F32), 0.0).then_inc(placed, 1)
                dve.wait_ge(loaded, 64)
                dve.wait_ge(placed, 2)
                for w_c, w_r in ((wq_c, wq_r), (wk_c, wk_r)):
                    for c in range(1, 4):
                        dve.tensor_copy(w_r[:, :, :, HD8 * c:HD8 * (c + 1)],
                                        w_c[:].rearrange("p (g h d) -> p g h d", h=PER, d=HD8)).then_inc(filled, 1)

        block = ctx.enter_context(core.nc.Block())

        @block.sync
        def _(sp):
            def spread(i, gi):
                sp.wait_ge(k_split, i + 1 + 1)
                for hh in range(PER):
                    r = slice(ROWS * hh, ROWS * (hh + 1))
                    sp.dma_start(k_one[r, gi, hh, :].bitcast(F32), k_all[r, :].bitcast(F32)).then_inc(k_spread[gi], 16)

            with sp.Fori(0, B) as b:
                for gi in range(HGROUPS):
                    spread(HGROUPS * b + gi, gi)
            for gi in range(2):
                spread(NG + gi, gi)
            for gi in range(2):
                sp.wait_ge(k_spread[gi], 16 * PER * (B + 1))

        @block.gpsimd
        def _(pool):
            with pool.Fori(0, NG + 2) as i:
                pool.wait_ge(roped, 2 * i + 1)
                pool.wait_ge(q_split, i + 1)
                pool.tensor_tensor(hq[:].bitcast(F32R), tq[:], zero[:], ALU.add).then_inc(high, 1)
                pool.wait_ge(roped, 2 * i + 2)
                pool.wait_ge(k_split, i + 1)
                pool.tensor_tensor(hk[:].bitcast(F32R), tk[:], zero[:], ALU.add).then_inc(high, 1)

        @block.tensor
        def _(pe):
            def project(i, b, gi, w_r, ready, count):
                if ready is not None:
                    pe.wait_ge(ready, count)
                pe.matmul(PM, w_r[:, gi, :, :].rearrange("p h r -> p (h r)"), xt[:, bass.ts(b, BANK)],
                          start=True, stop=True).then_inc(projected, 1)

            def top_scores(i, turn, gi, hh, k):
                if hh == 0 and k == 0:
                    pe.wait_ge(k_spread[gi], 16 * PER * (turn + 1))
                    pe.wait_ge(q_split, i + 1 + 1)
                pe.wait_ge(top_read, 2 * PER * i + 2 * hh + k + 1)
                for c in range(2):
                    qc = 2 * k + c
                    last = pe.matmul(PTOP[k][:, c, :], q_all[:, gi, qc * P:(qc + 1) * P], k_one[:, gi, hh, :],
                                     start=True, stop=True)
                last.then_inc(top_filled, 1)

            def scores(m, gi, hh, kc):
                pe.wait_ge(exped, 4 * PER * m + 4 * hh + kc + 1)
                pe.matmul(PSC[kc % 2], k_one[:, gi, hh, kc * P:(kc + 1) * P], q_all[:, gi, :],
                          start=True, stop=True).then_inc(scored, 1)

            def sums(m, gi, kc):
                if kc == 0:
                    pe.wait_ge(exped, 2 + 4 * PER * (m + 1))
                    pe.wait_ge(o_copied, m + 1)
                    if gi == 0:
                        pe.wait_ge(v_set, m // HGROUPS + 1)
                for hh in range(PER):
                    r = slice(ROWS * hh, ROWS * (hh + 1))
                    last = pe.matmul(PO[r, :], v_one[:, kc, PER * gi + hh, :], probs[:, gi % 2, kc, hh, :],
                                     start=(kc == 0), stop=(kc == GROUP - 1))
                if kc == GROUP - 1:
                    last.then_inc(summed, 1)

            def turn_out(m, ready, count):
                pe.wait_ge(o_copied, m + 1 + 1)
                pe.wait_ge(ready, count)
                for j in range(GROUP):
                    last = pe.transpose(PM[:, j * P:(j + 1) * P], o_sb[:, j * P:(j + 1) * P], ident[:])
                last.then_inc(o_turned, 1)

            pe.sem_inc(summed, 2)
            pe.sem_inc(o_turned, 1)
            project(0, 0, 0, wq_r, None, 0)
            project(0, 0, 0, wk_r, roped, 1)
            project(1, 0, 1, wq_r, roped, 2)
            project(1, 0, 1, wk_r, roped, 3)
            for hh in range(PER):
                for k in range(2):
                    top_scores(0, 0, 0, hh, k)
            with pe.Fori(0, B) as b:
                for gi in range(HGROUPS):
                    m = HGROUPS * b + gi
                    nxt, far = (gi + 1) % HGROUPS, (gi + 2) % HGROUPS
                    far_b = b + (gi + 2) // HGROUPS
                    pe.wait_ge(top_read, 2 + 2 * PER * (m + 1))
                    if gi == 1:
                        pe.wait_ge(roped, 2 * m + 4)
                    else:
                        pe.wait_ge(roped, 2 * m + 4)
                        pe.wait_ge(o_added, HGROUPS * b + max(gi - 1, 0) + 1)
                    for j in range(GROUP):
                        last = pe.matmul(PM[:, j * P:(j + 1) * P], tops[:, gi % 2, j, :], core.ident_r[:],
                                         start=True, stop=True)
                    last.then_inc(rows_in_psum, 1)
                    for hh in range(PER):
                        top_scores(m + 1, b + (gi + 1) // HGROUPS, nxt, hh, 0)
                        if hh == 0:
                            pe.wait_ge(q_ready, m + 1)
                        scores(m, gi, hh, 0)
                        scores(m, gi, hh, 1)
                        top_scores(m + 1, b + (gi + 1) // HGROUPS, nxt, hh, 1)
                        scores(m, gi, hh, 2)
                        scores(m, gi, hh, 3)
                        if gi > 0:
                            sums(m - 1, gi - 1, hh)
                        if hh == 0:
                            project(m + 2, far_b, far, wq_r, q_ready, m + 1)
                        if hh == 1:
                            project(m + 2, far_b, far, wk_r, roped, 2 * (m + 2) + 1)
                    if gi > 0:
                        turn_out(m - 1, roped, 2 * (m + 2) + 2)
                    if gi == HGROUPS - 1:
                        for kc in range(GROUP):
                            sums(m, gi, kc)
                        turn_out(m, o_added, m + 1)

        @block.scalar
        def _(act):
            def rotate(i, which, t, bias):
                act.wait_ge(projected, 2 * i + which + 1)
                if bias is None:
                    act.activation(t[:], PM, ACT.Copy, scale=rope_now[:, 0:1]).then_inc(roped, 1)
                else:
                    act.activation(t[:], PM, ACT.Identity, scale=rope_now[:, 0:1], bias=bias).then_inc(roped, 1)

            def copy_out(m):
                act.wait_ge(summed, 2 + m + 1)
                act.wait_ge(o_turned, m + 1)
                act.activation(o_sb[:], PO, ACT.Copy).then_inc(o_copied, 1)

            act.sem_inc(exped, 2)
            act.sem_inc(o_copied, 1)
            act.wait_ge(rope_set, 1)
            for i in range(2):
                act.wait_ge(q_split, i + 1)
                rotate(i, 0, tq, None)
                act.wait_ge(k_split, i + 1)
                rotate(i, 1, tk, consts[:, 0:1])
            with act.Fori(0, B) as b:
                for gi in range(HGROUPS):
                    m = HGROUPS * b + gi
                    act.wait_ge(summed, m + 1)
                    if gi == 2:
                        act.wait_ge(rope_set, b + 2)
                    for hh in range(PER):
                        for kc in range(GROUP):
                            act.wait_ge(scored, 4 * PER * m + 4 * hh + kc + 1)
                            act.activation(probs[:, gi % 2, kc, hh, :], PSC[kc % 2], ACT.Exp,
                                           scale=HD8 ** -0.5).then_inc(exped, 1)
                        if hh == 0:
                            act.wait_ge(q_split, m + 2 + 1)
                            rotate(m + 2, 0, tq, None)
                        if hh == 1:
                            act.wait_ge(k_split, m + 2 + 1)
                            rotate(m + 2, 1, tk, consts[:, 0:1])
                    if gi > 0:
                        copy_out(m - 1)
                    if gi == HGROUPS - 1:
                        copy_out(m)

        @block.vector
        def _(dve):
            def split(i, which, t, hi, dst, done):
                dve.wait_ge(high, 2 * i + which + 1)
                dve.scalar_tensor_tensor(out=dst, in0=hi[:], scalar=consts[:, 1 + which:2 + which], in1=t[:],
                                         op0=ALU.mult, op1=ALU.add).then_inc(done, 1)

            def top(i, gi, hh, k):
                dve.wait_ge(top_filled, 2 * PER * i + 2 * hh + k + 1)
                dve.tensor_reduce(tops[:, gi % 2, 2 * k:2 * k + 2, ROWS * hh], PTOP[k], AX.X, ALU.max,
                                  negate=True).then_inc(top_read, 1)

            def add_out(b, gi, m):
                dve.wait_ge(o_turned, m + 1 + 1)
                o = PM.rearrange("p (j h r) -> p j h r", j=GROUP, h=PER)
                dve.reciprocal(rec[:], o[:, :, :, HD8]).then_inc(inverted, 1)
                dve.wait_ge(inverted, m + 1)
                dve.tensor_tensor(o_n[:], o[:, :, :, 0:HD8], rec[:].unsqueeze(3).to_broadcast([P, GROUP, PER, HD8]),
                                  ALU.mult).then_inc(scaled, 1)
                dve.wait_ge(scaled, m + 1)
                xs = x[:, bass.ts(b, GROUP), gi * PER * HD8:(gi + 1) * PER * HD8]
                dve.tensor_tensor(xs, xs, o_n[:].rearrange("p j h d -> p j (h d)"), ALU.add).then_inc(o_added, 1)

            def set_rope(b):
                dve.tensor_tensor(rope_now[:], rope_sb[:, bass.ds(b, 1)], zero[:, 0:1], ALU.add).then_inc(rope_set, 1)

            def set_v(b):
                dve.tensor_tensor(v_one[:, :, :, 0:HD8],
                                  v[:, bass.ts(b, GROUP), :].rearrange("p j (h d) -> p j h d", d=HD8),
                                  zero[:, 0:BANK].rearrange("p (j h d) -> p j h d", j=GROUP, d=HD8),
                                  ALU.add).then_inc(v_set, 1)

            dve.sem_inc(top_read, 2)
            for start_at_one in (q_split, k_split, o_added):
                dve.sem_inc(start_at_one, 1)
            set_rope(0)
            for i in range(2):
                split(i, 0, tq, hq, q_all[:, i, :], q_split)
                if i:
                    dve.wait_ge(k_spread[0], 16 * PER)
                split(i, 1, tk, hk, k_all[:], k_split)
            for hh in range(PER):
                for k in range(2):
                    top(0, 0, hh, k)
            with dve.Fori(0, B) as b:
                for gi in range(HGROUPS):
                    m = HGROUPS * b + gi
                    nxt, far = (gi + 1) % HGROUPS, (gi + 2) % HGROUPS
                    dve.wait_ge(rows_in_psum, m + 1)
                    q = q_all[:, gi, :]
                    dve.tensor_tensor(q, PM, q.bitcast(F32), ALU.add).then_inc(q_ready, 1)
                    if gi == 1:
                        dve.wait_ge(summed, 2 + HGROUPS * b)
                        set_v(b)
                    if gi == 2:
                        dve.wait_ge(roped, 2 * m + 4)
                        set_rope(b + 1)
                    for hh in range(PER):
                        for k in range(2):
                            top(m + 1, nxt, hh, k)
                        if hh == 1:
                            split(m + 2, 0, tq, hq, q_all[:, far, :], q_split)
                        if hh == 2:
                            dve.wait_ge(k_spread[nxt], 16 * PER * (b + (gi + 1) // HGROUPS + 1))
                            split(m + 2, 1, tk, hk, k_all[:], k_split)
                    if gi > 0:
                        add_out(b, gi - 1, m - 1)
                    if gi == HGROUPS - 1:
                        add_out(b, gi, m)


HEADS64, HD64 = 16, 64
INNER = HEADS64 * HD64
PAIRS = HEADS64 // 2
BIG = -1e30
SCORE_AT = {3: (0, 0, 0), 2: (1, 0, 512), 0: (1, 384, 896), 1: (2, 0, 1024)}
SCORE_BANKS = ((3,), (2, 0), (1,))
CAUSAL = sum((qc + 1) * P for qc in range(4))
TURN_AT = {0: (0, 0, 0), 1: (1, 0, 512), 2: (2, 0, 896), 3: (2, 256, 1152)}
TURN_BANKS = ((0,), (1,), (2, 3))


def values64(core, name, xt, wv, v):
    ps = core.ps
    with ExitStack() as ctx:
        st = Stage(core, name, ctx)
        w_sb = st.sb("w", [P, INNER])
        loaded, in_psum = st.sem("loaded"), st.sem("in_psum")
        copied = [st.sem("copied_act"), st.sem("copied_dve")]
        block = ctx.enter_context(core.nc.Block())

        @block.sync
        def _(sp):
            sp.dma_start(w_sb[:], wv).then_inc(loaded, 16)

        @block.tensor
        def _(pe):
            pe.wait_ge(loaded, 16)
            for t in range(TILES):
                for k in range(2):
                    if t >= 2:
                        pe.wait_ge(copied[k], t - 1)
                    pe.matmul(ps[:, 2 * (t % 2) + k, :], xt[:, t * P:(t + 1) * P], w_sb[:, k * BANK:(k + 1) * BANK],
                              start=True, stop=True).then_inc(in_psum, 1)

        @block.scalar
        def _(act):
            for t in range(TILES):
                act.wait_ge(in_psum, 2 * t + 1)
                act.activation(v[:, t, 0:BANK], ps[:, 2 * (t % 2), :], ACT.Copy).then_inc(copied[0], 1)

        @block.vector
        def _(dve):
            for t in range(TILES):
                dve.wait_ge(in_psum, 2 * t + 2)
                dve.tensor_copy(v[:, t, BANK:], ps[:, 2 * (t % 2) + 1, :]).then_inc(copied[1], 1)


def attention64(core, name, x, wkq, wv, wo1, wo2, tables, mask, gamma):
    ps, ident = core.ps, core.ident
    with ExitStack() as ctx:
        st = Stage(core, name, ctx)
        y = st.sb("y", [P, TILES, D])
        with ExitStack() as c1:
            s1 = Stage(core, name + "_main", c1)
            xt = s1.sb("xt", [P, TILES * P])
            v_all = s1.sb("v_all", [P, TILES, INNER])
            norm_turn(core, name + "_ln", x, xt)
            values64(core, name + "_v", xt, wv, v_all)
            heads64(core, s1, xt, v_all, y, wkq, wo1, wo2, tables, mask)
        norm_turn(core, name + "_ln2", y, xn=y, affine=(gamma, None), add_to=x, add_scale=1.0)


def heads64(core, st, xt, v_all, y, wkq, wo1, wo2, tables, mask):
    ps, ident, ctx = core.ps, core.ident, st.ctx
    NP = B * PAIRS
    w_sb = st.sb("wkq", [P, 4, INNER])
    wo1_sb, wo2_sb = st.sb("wo1", [P, PAIRS, D]), st.sb("wo2", [P, D])
    tab = st.sb("tab", [P, 4, BANK])
    mask_f, mask_r = st.sb("mask_f", [P, P]), st.sb("mask_r", [P, P], F32R)
    part = st.sb("part", [P, 4, BANK])
    q = st.sb("q", [P, 2, BANK])
    k_one = st.sb("k_one", [P, 2, 2, BANK])
    v_now = st.sb("v_now", [P, GROUP, INNER])
    neg_top = st.sb("neg_top", [P, 2, GROUP])
    total, rec = st.sb("total", [P, 2, GROUP]), st.sb("rec", [P, 2, GROUP])
    probs = st.sb("probs", [P, 2, CAUSAL])
    turned = st.sb("turned", [P, 2, CAUSAL])
    o_t = st.sb("o_t", [P, PAIRS, BANK])
    hid = st.sb("hid", [P, BANK])
    names = ("loaded", "zeroed", "set", "projected", "parted", "q_ready", "k_ready", "s_ready", "top_done", "exped",
             "inverted", "normed", "t_ready", "t_copied", "summed", "o_copied", "hidden", "relued", "y_ready", "y_copied")
    (loaded, zeroed, set_, projected, parted, q_ready, k_ready, s_ready, top_done, exped,
     inverted, normed, t_ready, t_copied, summed, o_copied, hidden, relued, y_ready, y_copied) = (st.sem(n) for n in names)
    v_loaded = [st.sem(f"v_loaded{j}") for j in range(PAIRS)]
    PS = [ps[:, k, :] for k in range(3)]
    PT = [ps[:, 3 + k, :] for k in range(2)]
    PM = [ps[:, 5 + k, :] for k in range(2)]
    PO = ps[:, 7, :]

    with core.nc.Block() as block:
        @block.sync
        def _(sp):
            for w in range(4):
                sp.dma_start(w_sb[:, w, :], wkq[w]).then_inc(loaded, 16)
            sp.dma_start(wo1_sb[:], wo1.rearrange("(j p) d -> p j d", p=P)).then_inc(loaded, 16)
            sp.dma_start(wo2_sb[:], wo2).then_inc(loaded, 16)
            sp.dma_start(tab[:], tables).then_inc(loaded, 16)
            sp.dma_start(mask_f[:], mask).then_inc(loaded, 16)
            sp.wait_ge(loaded, 128)

        @block.gpsimd
        def _(pool):
            pool.memset(k_one[:], 0.0).then_inc(zeroed, 1)

        @block.vector
        def _(dve):
            dve.wait_ge(loaded, 128)
            dve.tensor_copy(mask_r[:], mask_f[:]).then_inc(set_, 1)

    block = ctx.enter_context(core.nc.Block())

    def place(b, k):
        return b + k // PAIRS, k % PAIRS

    @block.sync
    def _(sp):
        with sp.Fori(0, B) as b:
            for j in range(PAIRS):
                sp.wait_ge(summed, PAIRS * b + j + 1)
                c = slice(j * P, (j + 1) * P)
                sp.dma_start(v_now[:, :, c], v_all[:, bass.ts(b, GROUP), c]).then_inc(v_loaded[j], 16)
        for j in range(PAIRS):
            sp.wait_ge(v_loaded[j], 16 * B)

    @block.gpsimd
    def _(pool):
        def rotate(p, par):
            pool.wait_ge(parted, 2 + 4 * p + 2)
            pool.wait_ge(s_ready, 6 * p + 1)
            pool.wait_ge(q_ready, p + 1)
            for hh in range(2):
                r = slice(HD64 * hh, HD64 * (hh + 1))
                if hh:
                    pool.wait_ge(k_ready, 1 + 2 * p + 1)
                pool.tensor_tensor(k_one[r, par, hh, :], part[r, 0, :], part[r, 1, :], ALU.add).then_inc(k_ready, 1)
            pool.wait_ge(parted, 2 + 4 * p + 4)
            pool.wait_ge(k_ready, 1 + 2 * (p + 1))
            pool.tensor_tensor(q[:, par, :], part[:, 2, :], part[:, 3, :], ALU.add).then_inc(q_ready, 1)

        pool.sem_inc(q_ready, 1)
        pool.sem_inc(k_ready, 1)
        with pool.Fori(0, NP // 2) as p2:
            for par in range(2):
                rotate(2 * p2 + par, par)

    @block.tensor
    def _(pe):
        def project(b, k, w):
            row, j = place(b, k)
            pe.wait_ge(parted, 4 * (PAIRS * b + k) + w + 1)
            pe.matmul(PM[w % 2], w_sb[:, w, j * P:(j + 1) * P], xt[:, bass.ts(row, BANK)], start=True, stop=True)\
              .then_inc(projected, 1)

        def scores(p, j, hh):
            n = 2 * p + hh
            if hh == 0:
                pe.wait_ge(q_ready, 1 + p + 1)
                pe.wait_ge(k_ready, 1 + 2 * (p + 1))
            for bank, chunks in enumerate(SCORE_BANKS):
                pe.wait_ge(exped, 3 * n + bank + 2)
                for qc in chunks:
                    _, at, _ = SCORE_AT[qc]
                    keys = (qc + 1) * P
                    pe.matmul(PS[bank][:, at:at + keys], q[:, j % 2, qc * P:(qc + 1) * P], k_one[:, j % 2, hh, 0:keys],
                              start=True, stop=False)
                    last = pe.matmul(PS[bank][:, at + keys - P:at + keys], core.ident_r[:], mask_r[:],
                                     start=False, stop=True)
                last.then_inc(s_ready, 1)

        def turn(p, hh):
            n = 2 * p + hh
            pe.wait_ge(normed, n + 1)
            for fill, chunks in enumerate(TURN_BANKS):
                pt = PT[(3 * hh + fill) % 2]
                pe.wait_ge(t_copied, 3 * n + fill + 1)
                for kc in chunks:
                    _, at, _ = TURN_AT[kc]
                    for qc in range(kc, GROUP):
                        row = SCORE_AT[qc][2] + kc * P
                        to = at + (qc - kc) * P
                        last = pe.transpose(pt[:, to:to + P], probs[:, hh, row:row + P], ident[:])
                last.then_inc(t_ready, 1)

        def sums(b, k):
            p = PAIRS * b + k
            row, j = place(b, k)
            pe.wait_ge(t_copied, 2 + 6 * (p + 1))
            pe.wait_ge(o_copied, p + 1)
            pe.wait_ge(v_loaded[j], 16 * (row + 1))
            for kc in range(GROUP):
                at, n = TURN_AT[kc][2], BANK - kc * P
                for hh in range(2):
                    r = slice(HD64 * hh, HD64 * (hh + 1))
                    c = (2 * j + hh) * HD64
                    last = pe.matmul(PO[r, kc * P:], v_now[:, kc, c:c + HD64], turned[:, hh, at:at + n],
                                     start=(kc == 0), stop=(kc == GROUP - 1))
            last.then_inc(summed, 1)

        def mix(b, parts):
            pe.wait_ge(parted, 2 + parts)
            pe.wait_ge(o_copied, 1 + PAIRS * (b + 1))
            for j in range(PAIRS):
                last = pe.matmul(PM[0], wo1_sb[:, j, :], o_t[:, j, :], start=(j == 0), stop=(j == PAIRS - 1))
            last.then_inc(hidden, 1)

        def mix2(b, parts):
            pe.wait_ge(parted, 2 + parts)
            pe.wait_ge(relued, b + 1)
            for t in range(GROUP):
                last = pe.matmul(PM[1][:, t * P:(t + 1) * P], hid[:, t * P:(t + 1) * P], wo2_sb[:], start=True, stop=True)
            last.then_inc(y_ready, 1)

        def pair(b, k, last=False):
            p, j = PAIRS * b + k, k % PAIRS
            scores(p, j, 0)
            if not last:
                project(b, k + 1, 0)
                if k == 2:
                    pe.wait_ge(y_copied, b + 1)
                project(b, k + 1, 1)
            if k:
                turn(p - 1, 1)
            if k == PAIRS + 1:
                mix(b, 4 * (p + 1) + 1)
            scores(p, j, 1)
            if not last:
                if k == PAIRS + 1:
                    pe.wait_ge(relued, b + 1)
                project(b, k + 1, 2)
                project(b, k + 1, 3)
            if k:
                sums(b, k - 1)
            turn(p, 0)
            if k == PAIRS + 1:
                mix2(b, 4 * (p + 1) + 4)

        pe.sem_inc(s_ready, 7)
        pe.sem_inc(t_ready, 6)
        pe.sem_inc(y_ready, 1)
        pe.sem_inc(summed, PAIRS)
        for w in range(4):
            project(0, 0, w)
        for k in range(2):
            pair(0, k)
        with pe.Fori(0, B - 1) as b:
            for k in range(2, PAIRS + 2):
                pair(b, k)
        for k in range(2, PAIRS):
            pair(B - 1, k, last=(k == PAIRS - 1))
        turn(NP - 1, 1)
        sums(B - 1, PAIRS - 1)
        mix(B - 1, 4 * NP)
        mix2(B - 1, 4 * NP)

    @block.scalar
    def _(act):
        def exps(p, hh):
            n = 2 * p + hh
            for bank, chunks in enumerate(SCORE_BANKS):
                act.wait_ge(top_done, 3 * n + bank + 1)
                if bank == 0:
                    act.wait_ge(t_ready, 3 * n + 3)
                for qc in chunks:
                    _, at, row = SCORE_AT[qc]
                    keys = (qc + 1) * P
                    last = act.activation(probs[:, hh, row:row + keys], PS[bank][:, at:at + keys], ACT.Exp,
                                          bias=neg_top[:, hh, qc:qc + 1], accum_out=total[:, hh, qc:qc + 1])
                last.then_inc(exped, 1)

        def copy_turned(p, hh):
            for fill, chunks in enumerate(TURN_BANKS):
                act.wait_ge(t_ready, 6 + 3 * (2 * p + hh) + fill + 1)
                row = TURN_AT[chunks[0]][2]
                size = sum(BANK - kc * P for kc in chunks)
                act.activation(turned[:, hh, row:row + size], PT[(3 * hh + fill) % 2][:, 0:size],
                               ACT.Copy).then_inc(t_copied, 1)

        def copy_out(p, j):
            act.wait_ge(summed, PAIRS + p + 1)
            act.activation(o_t[:, j, :], PO, ACT.Copy).then_inc(o_copied, 1)

        def relu(b):
            act.wait_ge(hidden, b + 1)
            act.wait_ge(y_ready, b + 1)
            act.activation(hid[:], PM[0], ACT.Relu).then_inc(relued, 1)

        def pair(b, k):
            p, j = PAIRS * b + k, k % PAIRS
            exps(p, 0)
            if k:
                copy_turned(p - 1, 1)
            if k == PAIRS + 1:
                relu(b)
            exps(p, 1)
            if k:
                copy_out(p - 1, (k - 1) % PAIRS)
            copy_turned(p, 0)

        act.sem_inc(exped, 4)
        act.sem_inc(o_copied, 1)
        act.sem_inc(t_copied, 2)
        for k in range(2):
            pair(0, k)
        with act.Fori(0, B - 1) as b:
            for k in range(2, PAIRS + 2):
                pair(b, k)
        for k in range(2, PAIRS):
            pair(B - 1, k)
        copy_turned(NP - 1, 1)
        copy_out(NP - 1, PAIRS - 1)
        relu(B - 1)

    @block.vector
    def _(dve):
        def tops(p, hh):
            n = 2 * p + hh
            dve.wait_ge(exped, 3 * n + 1)
            for bank, chunks in enumerate(SCORE_BANKS):
                dve.wait_ge(s_ready, 7 + 3 * n + bank + 1)
                for qc in chunks:
                    _, at, _ = SCORE_AT[qc]
                    last = dve.tensor_reduce(neg_top[:, hh, qc:qc + 1], PS[bank][:, at:at + (qc + 1) * P], AX.X,
                                             ALU.max, negate=True)
                last.then_inc(top_done, 1)

        def norms(p, hh):
            n = 2 * p + hh
            dve.wait_ge(exped, 4 + 3 * (n + 1))
            dve.reciprocal(rec[:, hh, :], total[:, hh, :]).then_inc(inverted, 1)
            dve.wait_ge(inverted, n + 1)
            for qc in range(GROUP):
                r = slice(SCORE_AT[qc][2], SCORE_AT[qc][2] + (qc + 1) * P)
                last = dve.tensor_scalar(probs[:, hh, r], probs[:, hh, r], rec[:, hh, qc:qc + 1], None, ALU.mult)
            last.then_inc(normed, 1)

        def take_part(p, w):
            dve.wait_ge(projected, 4 * p + w + 1)
            if w == 0:
                dve.wait_ge(k_ready, 2 * p + 1)
            if w == 2:
                dve.wait_ge(q_ready, p + 1)
            dve.tensor_tensor(part[:, w, :], PM[w % 2], tab[:, w, :], ALU.mult).then_inc(parted, 1)

        def copy_y(b):
            dve.wait_ge(y_ready, 1 + b + 1)
            dve.tensor_scalar(y[:, bass.ts(b, GROUP), :], PM[1].rearrange("p (t d) -> p t d", d=D), 1.0, None,
                              ALU.mult).then_inc(y_copied, 1)

        def pair(b, k, last=False):
            p = PAIRS * b + k
            for hh in range(2):
                tops(p, hh)
                if not last:
                    take_part(p + 1, 2 * hh)
                    take_part(p + 1, 2 * hh + 1)
                norms(p, hh)
            if k == PAIRS + 1:
                copy_y(b)

        dve.sem_inc(parted, 2)
        dve.sem_inc(y_copied, 1)
        for w in range(4):
            take_part(0, w)
        for k in range(2):
            pair(0, k)
        with dve.Fori(0, B - 1) as b:
            for k in range(2, PAIRS + 2):
                pair(b, k)
        for k in range(2, PAIRS):
            pair(B - 1, k, last=(k == PAIRS - 1))
        copy_y(B - 1)


HEADS4, HD4 = 4, 32


def attention_rows(core, name, xi, xt, y, wqkv, bqkv, wo, bo):
    ps, ident = core.ps, core.ident
    U = TILES // B
    with ExitStack() as ctx:
        st = Stage(core, name, ctx)
        w_sb, bias = st.sb("wqkv", [P, 3 * D]), st.sb("bias", [P, 3 * D])
        wo_sb, bo_sb = st.sb("wo", [P, D]), st.sb("bo", [P, 1, D])
        qkv = st.sb("qkv", [P, B, U, 3 * D])
        prod = st.sb("prod", [P, 2, B, D])
        sc = st.sb("sc", [P, U * B, B, HEADS4])
        mx, total = st.sb("mx", [P, U * B, 1, HEADS4]), st.sb("total", [P, U * B, 1, HEADS4])
        o = st.sb("o", [P, B, U, D])
        ot = st.sb("ot", [P, 2, BANK])
        names = ("loaded", "projected", "biased", "multiplied", "reduced", "chain", "shifted", "exped", "weights",
                 "turned", "copied", "mixed", "added")
        (loaded, projected, biased, multiplied, reduced, chain, shifted, exped, weights,
         turned, copied, mixed, added) = (st.sem(n) for n in names)
        block = ctx.enter_context(core.nc.Block())
        PQ = [ps[:, q, 0:3 * D] for q in range(2)]
        PT = [ps[:, 2 + q, :] for q in range(2)]
        PX = [ps[:, 4 + q, :] for q in range(2)]
        N = U * B
        order = [B_ * U + u for u in range(U) for B_ in range(B)]

        @block.sync
        def _(sp):
            sp.dma_start(w_sb[:], wqkv).then_inc(loaded, 16)
            sp.dma_start(bias[:], bqkv.partition_broadcast(P)).then_inc(loaded, 16)
            sp.dma_start(wo_sb[:], wo).then_inc(loaded, 16)
            sp.dma_start(bo_sb[:, 0, :], bo.partition_broadcast(P)).then_inc(loaded, 16)

        @block.tensor
        def _(pe):
            pe.wait_ge(loaded, 64)
            for n, t in enumerate(order):
                if n >= 2:
                    pe.wait_ge(biased, n - 1)
                pe.matmul(PQ[n % 2], xt[:, t * P:(t + 1) * P], w_sb[:], start=True, stop=True).then_inc(projected, 1)
            for s in range(B):
                pe.wait_ge(reduced, 2 * N)
                if s >= 2:
                    pe.wait_ge(copied, s - 1)
                for u in range(U):
                    last = pe.transpose(PT[s % 2][:, u * P:(u + 1) * P], o[:, s, u, :], ident[:])
                last.then_inc(turned, 1)
                pe.wait_ge(copied, s + 1)
                if s >= 2:
                    pe.wait_ge(added, s - 1)
                for u in range(U):
                    last = pe.matmul(PX[s % 2][:, u * P:(u + 1) * P], ot[:, s % 2, u * P:(u + 1) * P], wo_sb[:],
                                     start=True, stop=True)
                last.then_inc(mixed, 1)

        @block.scalar
        def _(act):
            act.wait_ge(shifted, 1)
            act.activation(sc[:], sc[:], ACT.Exp, scale=HD4 ** -0.5).then_inc(exped, 1)
            for s in range(B):
                act.wait_ge(turned, s + 1)
                if s >= 2:
                    act.wait_ge(mixed, s - 1)
                act.activation(ot[:, s % 2, :], PT[s % 2], ACT.Copy).then_inc(copied, 1)

        @block.gpsimd
        def _(pool):
            for n in range(N):
                u, s = n // B, n % B
                pool.wait_ge(biased, B * (u + 1))
                if n >= 2:
                    pool.wait_ge(reduced, n - 1)
                pool.tensor_tensor(prod[:, n % 2, :, :], qkv[:, s:s + 1, u, 0:D].to_broadcast([P, B, D]),
                                   qkv[:, :, u, D:2 * D], ALU.mult).then_inc(multiplied, 1)
            pool.wait_ge(weights, 1)
            wide = [P, B, HEADS4, HD4]
            for n in range(N):
                u, s = n // B, n % B
                pool.wait_ge(reduced, N + n - 1)
                pool.tensor_tensor(prod[:, n % 2, :, :].rearrange("p s (h d) -> p s h d", d=HD4),
                                   qkv[:, :, u, 2 * D:3 * D].rearrange("p s (h d) -> p s h d", d=HD4),
                                   sc[:, n, :, :].unsqueeze(3).to_broadcast(wide), ALU.mult).then_inc(multiplied, 1)

        @block.vector
        def _(dve):
            steps = [0]

            def link(ins):
                steps[0] += 1
                ins.then_inc(chain, 1)
                dve.wait_ge(chain, steps[0])

            dve.wait_ge(loaded, 64)
            for n, t in enumerate(order):
                dve.wait_ge(projected, n + 1)
                dve.tensor_tensor(qkv[:, t // U, t % U, :], PQ[n % 2], bias[:], ALU.add).then_inc(biased, 1)
            for n in range(N):
                dve.wait_ge(multiplied, n + 1)
                dve.tensor_reduce(sc[:, n, :, :], prod[:, n % 2, :, :].rearrange("p s (h d) -> p s h d", d=HD4),
                                  AX.X, ALU.add).then_inc(reduced, 1)
            dve.wait_ge(reduced, N)
            wide = [P, N, B, HEADS4]
            by_key = sc[:].rearrange("p n k h -> p n h k")
            link(dve.tensor_reduce(mx[:, :, 0, :], by_key, AX.X, ALU.max))
            dve.tensor_tensor(sc[:], sc[:], mx[:].to_broadcast(wide), ALU.subtract).then_inc(shifted, 1)
            dve.wait_ge(exped, 1)
            link(dve.tensor_reduce(total[:, :, 0, :], by_key, AX.X, ALU.add))
            link(dve.reciprocal(total[:], total[:]))
            dve.tensor_tensor(sc[:], sc[:], total[:].to_broadcast(wide), ALU.mult).then_inc(weights, 1)
            for n in range(N):
                dve.wait_ge(multiplied, N + n + 1)
                dve.tensor_reduce(o[:, n % B, n // B, :], prod[:, n % 2, :, :].rearrange("p s c -> p c s"),
                                  AX.X, ALU.add).then_inc(reduced, 1)
            for s in range(B):
                rows = slice(U * s, U * (s + 1))
                dve.wait_ge(mixed, s + 1)
                link(dve.tensor_tensor(y[:, rows, :], PX[s % 2].rearrange("p (u d) -> p u d", d=D), xi[:, rows, :],
                                       ALU.add))
                dve.tensor_tensor(y[:, rows, :], y[:, rows, :], bo_sb[:].to_broadcast([P, U, D]),
                                  ALU.add).then_inc(added, 1)


def store(core, out):
    with ExitStack() as ctx:
        st = Stage(core, "store", ctx)
        stored = st.sem("stored")
        block = ctx.enter_context(core.nc.Block())

        @block.sync
        def _(sp):
            sp.dma_start(out.rearrange("b (t p) d -> p (b t) d", p=P), core.x[:]).then_inc(stored, 16)
            sp.wait_ge(stored, 16)


def silu_experts(core, name, a):
    moe(core, name, core.x, core.x, a["L0_W1"], a["L0_W2"], a["L0_Wr"], top2=True)


def row_experts(core, name, a):
    with ExitStack() as c:
        st = Stage(core, name, c)
        y = st.sb("y", [P, TILES, D])
        with ExitStack() as c1:
            s1 = Stage(core, name + "_rows", c1)
            xt, xi = s1.sb("xt", [P, TILES * P]), s1.sb("xi", [P, TILES, D])
            norm_turn(core, name + "_ln0", core.x, xt, xn=xi)
            attention_rows(core, name + "_mha", xi, xt, y, a["L1_Wqkv"], a["L1_bqkv"], a["L1_Wo"], a["L1_bo"])
        moe(core, name + "_moe", y, y, a["L1_W1"], a["L1_W2"], a["L1_Wg"], top2=False, b1=a["L1_b1"], b2=a["L1_b2"],
            xn=y, affine=(a["L1_g1"], a["L1_be1"]))
        norm_turn(core, name + "_ln2", y, xn=y, affine=(a["L1_g2"], a["L1_be2"]), add_to=core.x)


def program(nc, a, out, upto=99, start=0):
    with ExitStack() as ctx:
        core = Core(nc, ctx)
        setup(core, a["x"])
        run = lambda n: start < n <= upto
        if run(1):
            silu_experts(core, "f0a", a)
        if run(2):
            attention8(core, "a8", core.x, a["L0_Wq"], a["L0_Wk"], a["L0_Wv"], a["rope8"], a["rows8"])
        if run(3):
            silu_experts(core, "f0b", a)
        if run(4):
            row_experts(core, "r0", a)
        if run(5):
            attention64(core, "a64", core.x, a["L1_Wkq"], a["L1_Wv"], a["L1_Wo1"], a["L1_Wo2"], a["rope64"],
                        a["causal"], a["L1_gamma"])
        if run(6):
            row_experts(core, "r1", a)
        store(core, out)


def layouts(i):
    c = np.ascontiguousarray
    t = lambda n: np.asarray(i[n])
    chunks = lambda w: c(w.reshape(E, FC, P, D).transpose(0, 2, 1, 3))
    theta = 1.0 / 10000.0 ** (np.arange(0, HD8, 2, dtype=np.float32) / HD8)
    angle = np.arange(B, dtype=np.float32)[:, None] * np.concatenate([theta, theta])[None, :]
    sign = np.where(np.arange(HD8) < HD8 // 2, 1.0, -1.0)
    rope8 = np.zeros((P, B + 1), np.float32)
    rope8[:, :B] = np.tile((np.cos(angle) + sign * np.sin(angle)).T, (P // HD8, 1))
    row = np.arange(P) % ROWS
    rows8 = np.stack([row == 0, -((row >= 16) & (row < 24)).astype(np.float32), -(row >= 24).astype(np.float32)], 1)
    inv_freq = 1.0 / 10000.0 ** (np.arange(0, HD64, 2, dtype=np.float32) / HD64)
    freqs = np.arange(S, dtype=np.float32)[None, :] * np.tile(inv_freq, 2)[:, None]
    swap = np.where(np.arange(HD64) < HD64 // 2, -1.0, 1.0)[:, None]
    both = np.stack([np.cos(freqs), swap * np.sin(freqs)], 1)
    rope64 = np.tile(np.concatenate([both, both * HD64 ** -0.5], 1), (2, 1, 1)).astype(np.float32)
    w = t("L1_attn_W_qkv").reshape(D, 3, HEADS64, 2, HD64 // 2)
    flat = lambda m: m.reshape(D, INNER)
    wkq = np.stack([flat(m) for m in (w[:, 1], w[:, 1, :, ::-1], w[:, 0], w[:, 0, :, ::-1])])
    return {
        "x": c(t("L0_attn_x")),
        "L1_Wkq": c(wkq),
        "L1_Wv": c(flat(w[:, 2])),
        "L1_Wo1": c(t("L1_attn_W_o1")),
        "L1_Wo2": c(t("L1_attn_W_o2")),
        "L1_gamma": c(t("L1_attn_gamma")),
        "rope64": rope64,
        "causal": np.triu(np.full((P, P), BIG, np.float32), 1),
        "L0_Wq": c(t("L0_attn_Wq").T),
        "L0_Wk": c(t("L0_attn_Wk").T),
        "L0_Wv": c(t("L0_attn_Wv").T),
        "L1_Wqkv": c(t("L1_ffn_Wqkv").T),
        "L1_bqkv": c(t("L1_ffn_bqkv")),
        "L1_Wo": c(t("L1_ffn_Wo").T),
        "L1_bo": c(t("L1_ffn_bo")),
        "L1_g1": c(t("L1_ffn_g1")),
        "L1_be1": c(t("L1_ffn_be1")),
        "L1_g2": c(t("L1_ffn_g2")),
        "L1_be2": c(t("L1_ffn_be2")),
        "L1_Wg": c(t("L1_ffn_Wg").T),
        "L1_W1": c(t("L1_ffn_W1")),
        "L1_b1": c(t("L1_ffn_b1").reshape(E, FC, P).transpose(2, 0, 1).reshape(P, E * FC)),
        "L1_W2": chunks(t("L1_ffn_W2")),
        "L1_b2": c(t("L1_ffn_b2")),
        "rope8": rope8,
        "rows8": rows8.astype(np.float32),
        "L0_W1": c(t("L0_ffn_W1").transpose(0, 2, 1)),
        "L0_W2": chunks(t("L0_ffn_W2").transpose(0, 2, 1)),
        "L0_Wr": c(t("L0_ffn_Wr").T),
    }


def kernel(**inputs):
    import concourse.bacc as bacc
    from concourse.bass_utils import run_bass_kernel_spmd

    nc = bacc.Bacc("TRN2", target_bir_lowering=False, num_devices=1)
    arrays = layouts(inputs)
    aps = {n: nc.dram_tensor(f"in_{n}", v.shape, mybir.dt.from_np(v.dtype), kind="ExternalInput").ap()
           for n, v in arrays.items()}
    out = nc.dram_tensor("out", (B, S, D), F32, kind="ExternalOutput").ap()
    program(nc, aps, out)
    r = run_bass_kernel_spmd(nc, [{f"in_{n}": v for n, v in arrays.items()}], core_ids=[0])
    return r.results[0]["out"]
```

```python
from contextlib import ExitStack

import numpy as np

import concourse.bass as bass
from concourse import mybir

F32 = mybir.dt.float32
F32R = mybir.dt.float32r
U32 = mybir.dt.uint32
ALU = mybir.AluOpType
ACT = mybir.ActivationFunctionType
AX = mybir.AxisListType

P = 128
B, S, D = 4, 512, 128
TILES = B * S // P
GROUP = 4
GROUPS = TILES // GROUP
E, DFF = 8, 512
FC = DFF // P
EPS = 1e-5
BANK = 512




class Core:

    def __init__(self, nc, ctx):
        self.nc, self.ctx = nc, ctx
        self.cleared, self.cleared_at = 0, {}
        self.x = self.sb("x_res", [P, TILES, D])
        self.ident = self.sb("ident", [P, P])
        self.ident_r = self.sb("ident_r", [P, P], F32R)
        self.neg_half = self.sb("neg_half", [P, TILES])
        self.iota8 = self.sb("iota8", [P, TILES, E])
        self.first_row = self.sb("first_row", [P, P])
        self.first_row_r = self.sb("first_row_r", [P, P], F32R)
        self.ps = ctx.enter_context(nc.psum_tensor("ps", [P, 8, BANK], F32))

    def sb(self, name, shape, dt=F32):
        return self.ctx.enter_context(self.nc.sbuf_tensor(name, shape, dt))


class Stage:

    def __init__(self, core, name, ctx):
        self.core, self.name, self.ctx, self.nc = core, name, ctx, core.nc
        self.sems, self.nums = [], []
        ctx.callback(self.clear)

    def clear(self):
        if self.sems:
            self.nc.clear_and_free_semaphores(self.sems)
            self.core.cleared += 1
            self.core.cleared_at.update({n: self.core.cleared for n in self.nums})

    def sb(self, name, shape, dt=F32):
        return self.ctx.enter_context(self.nc.sbuf_tensor(f"{self.name}_{name}", shape, dt))

    def sem(self, name):
        num = min(self.nc.free_semaphores, key=lambda n: self.core.cleared_at.get(n, 0))
        self.sems.append(self.nc.alloc_semaphore(name=f"{self.name}_{name}", num=num))
        self.nums.append(num)
        return self.sems[-1]


def setup(core, x_in):
    nc = core.nc
    with ExitStack() as ctx:
        st = Stage(core, "setup", ctx)
        names = ("x_loaded", "zeroed", "rows_zeroed", "row_set", "ident_built", "consts")
        x_loaded, zeroed, rows_zeroed, row_set, ident_built, consts = (st.sem(n) for n in names)
        block = ctx.enter_context(nc.Block())

        @block.sync
        def _(sp):
            sp.dma_start(core.x[:], x_in.rearrange("b (t p) d -> p (b t) d", p=P)).then_inc(x_loaded, 16)
            sp.wait_ge(x_loaded, 16)

        @block.gpsimd
        def _(pool):
            pool.memset(core.ident[:], 0.0).then_inc(zeroed, 1)
            pool.memset(core.neg_half[:], -0.5).then_inc(consts, 1)
            pool.memset(core.first_row[:], 0.0).then_inc(rows_zeroed, 1)
            pool.wait_ge(rows_zeroed, 1)
            pool.memset(core.first_row[0:1, :], 1.0).then_inc(row_set, 1)
            pool.iota(core.iota8[:], [[0, TILES], [1, E]], base=0, channel_multiplier=0,
                      allow_small_or_imprecise_dtypes=True).then_inc(consts, 1)
            pool.wait_ge(zeroed, 1)
            pool.affine_select(out=core.ident[:], in_=core.ident[:], compare_op=ALU.not_equal, fill=1.0,
                               base=0, pattern=[[-1, P]], channel_multiplier=1).then_inc(ident_built, 1)

        @block.vector
        def _(dve):
            dve.wait_ge(row_set, 1)
            dve.tensor_copy(core.first_row_r[:], core.first_row[:]).then_inc(consts, 1)
            dve.wait_ge(ident_built, 1)
            dve.tensor_copy(core.ident_r[:], core.ident[:]).then_inc(consts, 1)


def norm_turn(core, name, src, xt=None, xn=None, w_v=None, v=None, affine=None, add_to=None, add_scale=0.5,
              parts=None, first=None, loads=(), on_vector=None, on_pool=None, early=None,
              on_scalar=None, router=None):
    ps, ident = core.ps, core.ident
    beta = affine is not None and affine[1] is not None
    with ExitStack() as ctx:
        st = Stage(core, name, ctx)
        stats = st.sb("stats", [P, TILES, 6])
        moments = st.sb("moments", [P, TILES, 2])
        rstd, shift_by = st.sb("rstd", [P, TILES]), st.sb("shift_by", [P, TILES])
        if xn is None:
            xn = st.sb("xn", [P, TILES, D])
        have_stats, have_moments, var_eps, have_rstd, have_shift, normed, turned, copied = (
            st.sem(n) for n in ("have_stats", "have_moments", "var_eps", "have_rstd", "have_shift", "normed", "turned",
                                "copied"))
        on_act = xt is None
        if affine is not None:
            gb = st.sb("gb", [P, 2, D])
            gb_loaded, scaled, shifted = (st.sem(n) for n in ("gb_loaded", "scaled", "shifted"))
        if v is not None:
            w_sb = st.sb("w_v", [P, D])
            w_loaded, v_in_psum, v_copied = (st.sem(n) for n in ("w_loaded", "v_in_psum", "v_copied"))
        if parts is not None:
            high = st.sem("high")
        if first is not None:
            first_loaded, first_high = st.sem("first_loaded"), st.sem("first_high")
        ahead_loaded = st.sem("ahead_loaded") if loads else None
        early_loaded = st.sem("early_loaded") if early is not None else None
        block = ctx.enter_context(core.nc.Block())
        PT = [ps[:, q, :] for q in range(2)]
        PV = [ps[:, 2 + q, :] for q in range(2)]
        tiles = lambda g: range(GROUP * g, GROUP * (g + 1))
        rows = lambda g: slice(GROUP * g, GROUP * (g + 1))
        wide = [P, GROUP, D]
        whole = lambda g: (normed, GROUP * (g + 1)) if affine is None else (shifted if beta else scaled, g + 1)

        @block.sync
        def _(sp):
            if early is not None:
                sp.dma_start(*early).then_inc(early_loaded, 16)
            if v is not None:
                sp.dma_start(w_sb[:], w_v).then_inc(w_loaded, 16)
            if affine is not None:
                for k, w in enumerate(affine):
                    if w is not None:
                        sp.dma_start(gb[:, k, :], w.partition_broadcast(P)).then_inc(gb_loaded, 16)
            if first is not None:
                w1, w1_f, _, _, w2, w2_f = first
                sp.dma_start(w1_f, w1).then_inc(first_loaded, 16)
                sp.dma_start(w2_f, w2).then_inc(first_loaded, 16)
            for dst, ap in loads:
                sp.dma_start(dst, ap).then_inc(ahead_loaded, 16)
            if loads:
                sp.wait_ge(ahead_loaded, 16 * len(loads))

        @block.vector
        def _(dve):
            def measure(g):
                for t in tiles(g):
                    dve.bn_stats(stats[:, t, :], src[:, t, :]).then_inc(have_stats, 1)
                for t in tiles(g):
                    dve.wait_ge(have_stats, t + 1)
                    dve.bn_aggr(moments[:, t, :], stats[:, t, :]).then_inc(have_moments, 1)

            def normalise(g):
                dve.wait_ge(have_rstd, g + 1)
                if on_act:
                    dve.scalar_tensor_tensor(out=shift_by[:, rows(g)], in0=moments[:, rows(g), 0], scalar=-1.0,
                                             in1=rstd[:, rows(g)], op0=ALU.mult, op1=ALU.mult).then_inc(have_shift, 1)
                    return
                for t in tiles(g):
                    dve.tensor_scalar(xn[:, t, :], src[:, t, :], moments[:, t, 0:1], rstd[:, t:t + 1],
                                      ALU.subtract, ALU.mult).then_inc(normed, 1)
                multiply(g)

            def multiply(g):
                if affine is not None:
                    if g == 0:
                        dve.wait_ge(gb_loaded, 16 * sum(w is not None for w in affine))
                    dve.wait_ge(normed, GROUP * (g + 1))
                    z = xn[:, rows(g), :]
                    dve.tensor_tensor(z, z, gb[:, 0:1, :].to_broadcast(wide), ALU.mult).then_inc(scaled, 1)

            def finish(g):
                if add_to is not None:
                    dve.wait_ge(*whole(g))
                    r = add_to[:, rows(g), :]
                    dve.scalar_tensor_tensor(out=r, in0=xn[:, rows(g), :], scalar=add_scale, in1=r,
                                             op0=ALU.mult, op1=ALU.add)
                if parts is not None:
                    tok = slice(g * BANK, (g + 1) * BANK)
                    dve.wait_ge(high, g + 1)
                    dve.tensor_tensor(parts[1][:, tok], xt[:, tok], parts[0][:, tok].bitcast(F32), ALU.subtract)

            measure(0)
            for g in range(1, GROUPS):
                measure(g)
                normalise(g - 1)
                if g >= 3 and not on_act:
                    finish(g - 3)
            normalise(GROUPS - 1)
            if on_act:
                for g in range(GROUPS):
                    multiply(g)
                    if g >= 2:
                        finish(g - 2)
                for g in range(GROUPS - 2, GROUPS):
                    finish(g)
            else:
                for g in range(GROUPS - 3, GROUPS):
                    finish(g)
            if on_vector is not None:
                dve.wait_ge(ahead_loaded, 16 * len(loads))
                on_vector(dve)

        @block.gpsimd
        def _(pool):
            def root(g):
                r = rstd[:, rows(g)]
                pool.wait_ge(have_moments, GROUP * (g + 1))
                pool.tensor_scalar(r, moments[:, rows(g), 1], EPS, None, ALU.add).then_inc(var_eps, 1)
                pool.wait_ge(var_eps, g + 1)
                pool.tensor_tensor(r, r, core.neg_half[:, rows(g)], ALU.pow).then_inc(have_rstd, 1)

            def shift(g):
                if beta:
                    z = xn[:, rows(g), :]
                    pool.wait_ge(scaled, g + 1)
                    pool.tensor_tensor(z, z, gb[:, 1:2, :].to_broadcast(wide), ALU.add).then_inc(shifted, 1)

            if on_act:
                for g in range(GROUPS):
                    root(g)
                for g in range(GROUPS):
                    shift(g)
            else:
                root(0)
                for g in range(1, GROUPS):
                    root(g)
                    shift(g - 1)
                shift(GROUPS - 1)
            if first is not None:
                _, w1_f, w1h, w1l, _, _ = first
                pool.wait_ge(first_loaded, 32)
                pool.tensor_copy(w1h, w1_f).then_inc(first_high, 1)
                pool.wait_ge(first_high, 1)
                pool.tensor_tensor(w1l, w1_f, w1h.bitcast(F32), ALU.subtract)
            if on_pool is not None:
                on_pool(pool)

        if on_act:
            @block.scalar
            def _(act):
                for g in range(GROUPS):
                    act.wait_ge(have_shift, g + 1)
                    for t in tiles(g):
                        act.activation(xn[:, t, :], src[:, t, :], ACT.Identity, scale=rstd[:, t:t + 1],
                                       bias=shift_by[:, t:t + 1]).then_inc(normed, 1)
            return

        @block.tensor
        def _(pe):
            def route(g):
                pe.wait_ge(copied, g + 1)
                if g == 0:
                    pe.wait_ge(early_loaded, 16)
                for t in tiles(g):
                    pe.matmul(router[1][:, t * E:(t + 1) * E], xt[:, t * P:(t + 1) * P], router[0][:],
                              start=True, stop=True)

            if v is not None:
                pe.wait_ge(w_loaded, 16)
            for g in range(GROUPS):
                pe.wait_ge(*whole(g))
                if g >= 2:
                    pe.wait_ge(copied, g - 1)
                for j in range(GROUP):
                    last = pe.transpose(PT[g % 2][:, j * P:(j + 1) * P], xn[:, GROUP * g + j, :], ident[:])
                last.then_inc(turned, 1)
                if router is not None and g >= 1:
                    route(g - 1)
                if v is not None:
                    pe.wait_ge(copied, g + 1)
                    if g >= 2:
                        pe.wait_ge(v_copied, g - 1)
                    for j in range(GROUP):
                        t = GROUP * g + j
                        last = pe.matmul(PV[g % 2][:, j * P:(j + 1) * P], xt[:, t * P:(t + 1) * P], w_sb[:],
                                         start=True, stop=True)
                    last.then_inc(v_in_psum, 1)
            if router is not None:
                route(GROUPS - 1)

        @block.scalar
        def _(act):
            for g in range(GROUPS):
                tok = slice(g * BANK, (g + 1) * BANK)
                act.wait_ge(turned, g + 1)
                act.activation(xt[:, tok], PT[g % 2], ACT.Copy).then_inc(copied, 1)
                if v is not None:
                    act.wait_ge(v_in_psum, g + 1)
                    act.activation(v[:, rows(g), :], PV[g % 2].rearrange("p (j d) -> p j d", d=D),
                                   ACT.Copy).then_inc(v_copied, 1)
                if parts is not None:
                    act.wait_ge(copied, g + 1)
                    act.activation(parts[0][:, tok], xt[:, tok], ACT.Copy).then_inc(high, 1)
                if on_scalar is not None and g == 1:
                    act.wait_ge(early_loaded, 16)
                    on_scalar(act)


def moe(core, name, src, acc, w1, w2, wr, top2, b1=None, b2=None, **norm):
    with ExitStack() as ctx:
        st = Stage(core, name, ctx)
        xt = st.sb("xt", [P, TILES * P])
        xh = st.sb("xh", [P, TILES * P], F32R)
        xl = st.sb("xl", [P, TILES * P], F32R)
        w1_f = st.sb("w1_f", [P, 2, DFF])
        w1h = st.sb("w1h", [P, 2, DFF], F32R)
        w1l = st.sb("w1l", [P, 2, DFF], F32R)
        w2_f = st.sb("w2_f", [P, 2, FC, D])
        first = (w1[0], w1_f[:, 0, :], w1h[:, 0, :], w1l[:, 0, :], w2[0], w2_f[:, 0, :, :])
        acc_t = st.sb("acc_t", [P, TILES * P])
        zero = st.sb("zero", [P, DFF])
        w_route = st.sb("w_route", [P, E])
        loads = []
        if b1 is not None:
            b1_sb, b2_sb = st.sb("b1", [P, E * FC]), st.sb("b2", [P, E])
            loads += [(b1_sb[:], b1), (b2_sb[:], b2)]
            b1, b2 = b1_sb, b2_sb
        logits = core.ps[:, 7, 0:TILES * E]
        norm_turn(core, name + "_ln", src, xt, parts=(xh, xl), first=first, loads=loads,
                  early=(w_route[:], wr), router=(w_route, logits),
                  on_pool=lambda pool: pool.memset(zero[:], 0.0), **norm)
        with ExitStack() as c2:
            experts(core, Stage(core, name + "_exp", c2), name, acc, acc_t, zero, xt, xh, xl, w1_f, w1h, w1l, w2_f,
                    w1, w2, logits, top2, b1, b2)


def experts(core, st, name, acc, acc_t, zero, xt, xh, xl, w1_f, w1h, w1l, w2_f, w1, w2, logits, top2, b1_sb, b2_sb):
    ps, ident = core.ps, core.ident
    STEPS = 2 * GROUPS
    LAG = 3
    N = E * GROUPS
    w2h, w2l = (st.sb(n, [P, 2, FC, D], F32R) for n in ("w2h", "w2l"))
    h = st.sb("h", [P, FC, BANK])
    hh, hl = (st.sb(n, [P, 2, FC, BANK], F32R) for n in ("hh", "hl"))
    wide_gate = st.sb("wide_gate", [P, 2, TILES * P])
    scaled = st.sb("scaled", [P, 2, BANK])
    w1_loaded, w2_loaded, g_loaded = ([st.sem(f"{n}{q}") for q in range(2)]
                                      for n in ("w1_loaded", "w2_loaded", "g_loaded"))
    w1_high, w1_split = st.sem("w1_high"), st.sem("w1_split")
    w2_high, w2_split = st.sem("w2_high"), st.sem("w2_split")
    h_in_psum = st.sem("h_in_psum")
    h_ready = st.sem("h_ready")
    h_high = st.sem("h_high")
    h_split = st.sem("h_split")
    y_in_psum = st.sem("y_in_psum")
    y_scaled = st.sem("y_scaled")
    y_added = st.sem("y_added")
    out_turned = st.sem("out_turned")
    gate = st.sb("gate", [P, TILES, E])
    gate_t = st.sb("gate_t", [E, TILES * P])
    gate_rows = core.nc.dram_tensor(name + "_gates", (E, TILES * P), F32, kind="Internal").ap()
    lg = st.sb("lg", [P, TILES, E])
    best = st.sb("best", [P, TILES, 8])
    place_i = st.sb("place_i", [P, TILES, 8], U32)
    place = st.sb("place", [P, TILES, 8])
    small = st.sb("small", [P, 5, TILES])
    second_mask = st.sb("second_mask", [P, TILES, E])
    gap_t, exp_t, g1_t, g2_t, euler = (small[:, k, :] for k in range(5))
    euler_set, chain, gap, gap_exp, ranked, placed, gated, g_turned, g_copied, g_stored = (
        st.sem(n) for n in ("euler_set", "chain", "gap", "gap_exp", "ranked", "placed", "gated",
                            "g_turned", "g_copied", "g_stored"))
    if b1_sb is not None:
        b1_now, b1_set = st.sb("b1_now", [P, 2, FC]), st.sem("b1_set")
    block = st.ctx.enter_context(core.nc.Block())
    PH = [ps[:, 2 * k:2 * k + 2, :] for k in range(2)]
    PY = [ps[:, 4 + k, :] for k in range(4)]
    PG = PY[2:4]

    @block.sync
    def _(sp):
        def load_weights(e):
            q = e % 2
            if e >= 2:
                sp.wait_ge(w1_split, e - 1)
            sp.dma_start(w1_f[:, q, :], w1[e]).then_inc(w1_loaded[q], 16)
            if e >= 2:
                sp.wait_ge(w2_split, e - 1)
            sp.dma_start(w2_f[:, q, :, :], w2[e]).then_inc(w2_loaded[q], 16)

        def load_gates(e):
            if e >= 2:
                sp.wait_ge(y_scaled, 4 + GROUPS * (e - 1))
            sp.dma_start(wide_gate[:, e % 2, :], gate_rows[e].partition_broadcast(P)).then_inc(g_loaded[e % 2], 16)

        load_weights(1)
        sp.wait_ge(g_copied, GROUPS)
        sp.dma_start(gate_rows, gate_t[:]).then_inc(g_stored, 16)
        sp.wait_ge(g_stored, 16)
        load_gates(0)
        load_gates(1)
        for e in range(2, E):
            load_weights(e)
            load_gates(e)

    @block.gpsimd
    def _(pool):
        def set_b1(pair, e):
            if b1_sb is not None:
                pool.tensor_tensor(b1_now[:, e % 2, :], b1_sb[:, bass.ds(FC * (2 * pair + e), FC)], zero[:, 0:FC],
                                   ALU.add).then_inc(b1_set, 1)

        def split_w1(pair, e):
            q, n = e % 2, 2 * pair + e
            pool.wait_ge(w1_loaded[q], 16 * (pair + e // 2 + q))
            pool.tensor_tensor(w1h[:, q, :], w1_f[:, q, :], zero[:], ALU.add).then_inc(w1_high, 1)
            pool.wait_ge(w1_high, n)
            pool.tensor_tensor(w1l[:, q, :], w1_f[:, q, :], w1h[:, q, :].bitcast(F32), ALU.subtract).then_inc(w1_split, 1)

        def split_w2(pair, e):
            q, n = e % 2, 2 * pair + e
            if e:
                pool.wait_ge(w2_loaded[q], 16 * (pair + e // 2 + q))
            pool.tensor_tensor(w2h[:, q, :, :], w2_f[:, q, :, :], zero[:].rearrange("p (f d) -> p f d", d=D),
                               ALU.add).then_inc(w2_high, 1)
            pool.wait_ge(w2_high, n + 1)
            pool.tensor_tensor(w2l[:, q, :, :], w2_f[:, q, :, :], w2h[:, q, :, :].bitcast(F32),
                               ALU.subtract).then_inc(w2_split, 1)

        def add(pair, s):
            n, z = STEPS * pair + s, acc_t[:, (s % GROUPS) * BANK:(s % GROUPS + 1) * BANK]
            pool.wait_ge(y_scaled, 4 + n + 1)
            pool.wait_ge(y_added, 2 + n)
            pool.tensor_tensor(z, z, scaled[:, s % 2, :], ALU.add).then_inc(y_added, 1)

        pool.sem_inc(w1_split, 1)
        pool.sem_inc(y_added, 1)
        for e in range(2):
            set_b1(0, e)
        split_w2(0, 0)
        if top2:
            pool.memset(euler, float(np.e)).then_inc(euler_set, 1)
            pool.wait_ge(euler_set, 1)
            pool.wait_ge(gap, 1)
            pool.tensor_tensor(exp_t, euler, gap_t, ALU.pow).then_inc(gap_exp, 1)
        split_w1(0, 1)
        split_w2(0, 1)
        pool.memset(acc_t[:], 0.0).then_inc(y_added, 1)
        with pool.Fori(0, E // 2 - 1) as pair:
            for s in range(STEPS):
                add(pair, s)
                if s % GROUPS == 1:
                    pool.wait_ge(h_ready, 2 + 2 * (STEPS * pair + s + 3))
                    set_b1(pair, 2 + s // GROUPS)
                    split_w1(pair, 2 + s // GROUPS)
                if s % GROUPS == 2:
                    pool.wait_ge(y_in_psum, 2 + STEPS * pair + s + 2)
                    split_w2(pair, 2 + s // GROUPS)
        for s in range(STEPS):
            add(E // 2 - 1, s)

    @block.tensor
    def _(pe):
        def first_layer(pair, s):
            e, t = (s // GROUPS) % 2, s % GROUPS
            if t == 0:
                pe.wait_ge(w1_split, 2 * pair + s // GROUPS + 1)
            for k in range(2):
                pe.wait_ge(h_ready, 2 * (STEPS * pair + s) + k + 1)
                for c in range(2):
                    w = slice((2 * k + c) * P, (2 * k + c + 1) * P)
                    x = slice(t * BANK, (t + 1) * BANK)
                    pe.matmul(PH[k][:, c, :], w1h[:, e, w], xh[:, x], start=True, stop=False)
                    pe.matmul(PH[k][:, c, :], w1h[:, e, w], xl[:, x], start=False, stop=False)
                    last = pe.matmul(PH[k][:, c, :], w1l[:, e, w], xh[:, x], start=False, stop=True)
                last.then_inc(h_in_psum, 1)

        def second_layer(pair, s):
            e, q, n = s // GROUPS, s % 2, STEPS * pair + s
            y = PY[s % 4]
            if s % GROUPS == 0:
                pe.wait_ge(w2_split, 2 * pair + e + 1)
            pe.wait_ge(y_scaled, n + 1)
            for f in range(FC):
                if f % 2 == 0:
                    pe.wait_ge(h_split, 2 + 2 * n + f // 2 + 1)
                pe.matmul(y, w2h[:, e, f, :], hh[:, q, f, :], start=(f == 0), stop=False)
                pe.matmul(y, w2h[:, e, f, :], hl[:, q, f, :], start=False, stop=False)
                last = pe.matmul(y, w2l[:, e, f, :], hh[:, q, f, :], start=False, stop=(f == FC - 1))
            last.then_inc(y_in_psum, 1)

        def turn_gates():
            pe.wait_ge(gated, 1)
            for g in range(GROUPS):
                if g >= 2:
                    pe.wait_ge(g_copied, g - 1)
                for j in range(GROUP):
                    last = pe.transpose(PG[g % 2][0:E, j * P:(j + 1) * P], gate[:, GROUP * g + j, :], ident[:])
                last.then_inc(g_turned, 1)

        pe.sem_inc(y_in_psum, 2)
        first_layer(0, 0)
        for s in range(STEPS):
            first_layer(0, s + 1)
            if s == 1:
                turn_gates()
            if s == 2:
                pe.wait_ge(g_copied, GROUPS)
            second_layer(0, s)
        with pe.Fori(1, E // 2 - 1) as pair:
            for s in range(STEPS):
                first_layer(pair, s + 1)
                second_layer(pair, s)
        for s in range(STEPS):
            if s + 1 < STEPS:
                first_layer(E // 2 - 1, s + 1)
            second_layer(E // 2 - 1, s)
        pe.wait_ge(h_ready, 2 + 2 * N)
        for g in range(GROUPS):
            pe.wait_ge(y_added, 2 + N - GROUPS + g + 1)
            for j in range(GROUP):
                t = GROUP * g + j
                last = pe.transpose(ps[:, g, j * P:(j + 1) * P], acc_t[:, t * P:(t + 1) * P], ident[:])
            last.then_inc(out_turned, 1)

    @block.scalar
    def _(act):
        def hidden(pair, s):
            n, q, e = STEPS * pair + s, s % 2, s // GROUPS
            if b1_sb is not None and s % GROUPS == 0:
                act.wait_ge(b1_set, 2 * pair + e + 1)
            for k in range(2):
                half = slice(2 * k, 2 * k + 2)
                act.wait_ge(h_in_psum, 2 * n + k + 1)
                act.wait_ge(h_split, 2 * n + k + 1)
                if b1_sb is None:
                    act.activation(h[:, half, :], PH[k], ACT.Silu).then_inc(h_ready, 1)
                else:
                    for c in range(2):
                        f = 2 * k + c
                        last = act.activation(h[:, f, :], PH[k][:, c, :], ACT.Relu, bias=b1_now[:, e, f:f + 1])
                    last.then_inc(h_ready, 1)
                if k == 0:
                    act.wait_ge(y_in_psum, n + 1)
                act.wait_ge(h_ready, 2 + 2 * n + k + 1)
                act.activation(hh[:, q, half, :], h[:, half, :], ACT.Copy).then_inc(h_high, 1)

        act.sem_inc(h_ready, 2)
        hidden(0, 0)
        hidden(0, 1)
        for g in range(GROUPS):
            act.wait_ge(g_turned, g + 1)
            act.activation(gate_t[:, g * BANK:(g + 1) * BANK], PG[g % 2][0:E, :], ACT.Copy).then_inc(g_copied, 1)
        for s in range(2, STEPS):
            hidden(0, s)
        with act.Fori(1, E // 2) as pair:
            for s in range(STEPS):
                hidden(pair, s)

    @block.vector
    def _(dve):
        steps = [0]
        wide = [P, TILES, E]
        first, second = (place[:, :, k:k + 1].to_broadcast(wide) for k in range(2))

        def link(ins):
            steps[0] += 1
            ins.then_inc(chain, 1)
            dve.wait_ge(chain, steps[0])

        def rank():
            link(dve.tensor_copy(lg[:], logits.rearrange("p (t e) -> p t e", e=E)))
            for t in range(TILES):
                dve.max(best[:, t, :], lg[:, t, :]).then_inc(ranked, 1)
            for t in range(TILES):
                dve.wait_ge(ranked, t + 1)
                dve.max_index(place_i[:, t, :], best[:, t, :], lg[:, t, :]).then_inc(placed, 1)
            if top2:
                dve.tensor_tensor(gap_t, best[:, :, 1], best[:, :, 0], ALU.subtract).then_inc(gap, 1)

        def gates():
            dve.wait_ge(placed, TILES)
            link(dve.tensor_copy(place[:], place_i[:]))
            if not top2:
                dve.tensor_tensor(gate[:], core.iota8[:], first, ALU.is_equal).then_inc(gated, 1)
            else:
                link(dve.tensor_tensor(second_mask[:], core.iota8[:], second, ALU.is_equal))
                link(dve.tensor_tensor(gate[:], core.iota8[:], first, ALU.is_equal))
                dve.wait_ge(gap_exp, 1)
                link(dve.tensor_scalar(g2_t, exp_t, 1.0, 2.0, ALU.add, ALU.mult))
                link(dve.reciprocal(g1_t, g2_t))
                link(dve.tensor_tensor(g2_t, g1_t, exp_t, ALU.mult))
                link(dve.tensor_tensor(gate[:], gate[:], g1_t.unsqueeze(2).to_broadcast(wide), ALU.mult))
                link(dve.tensor_tensor(second_mask[:], second_mask[:], g2_t.unsqueeze(2).to_broadcast(wide), ALU.mult))
                dve.tensor_tensor(gate[:], gate[:], second_mask[:], ALU.add).then_inc(gated, 1)

        def split(pair, s):
            n, q = STEPS * pair + s, s % 2
            for k in range(2):
                half = slice(2 * k, 2 * k + 2)
                dve.wait_ge(h_high, 2 * n + k + 1)
                dve.tensor_tensor(hl[:, q, half, :], h[:, half, :], hh[:, q, half, :].bitcast(F32),
                                  ALU.subtract).then_inc(h_split, 1)

        def scale(pair, s):
            n, q, e = STEPS * pair + s, s % 2, s // GROUPS
            g = wide_gate[:, e, (s % GROUPS) * BANK:(s % GROUPS + 1) * BANK]
            dve.wait_ge(y_in_psum, 2 + n + 1)
            dve.wait_ge(y_added, n + 1)
            if s % GROUPS == 0:
                dve.wait_ge(g_loaded[e], 16 * (pair + 1))
            if b2_sb is None:
                dve.tensor_tensor(scaled[:, q, :], PY[s % 4], g, ALU.mult).then_inc(y_scaled, 1)
            else:
                dve.scalar_tensor_tensor(out=scaled[:, q, :], in0=PY[s % 4], scalar=b2_sb[:, bass.ds(2 * pair + e, 1)],
                                         in1=g, op0=ALU.add, op1=ALU.mult).then_inc(y_scaled, 1)

        dve.sem_inc(y_scaled, 4)
        dve.sem_inc(h_split, 2)
        rank()
        split(0, 0)
        gates()
        for s in range(1, LAG):
            split(0, s)
        with dve.Fori(0, E // 2 - 1) as pair:
            for s in range(STEPS):
                split(pair, s + LAG)
                scale(pair, s)
        for s in range(STEPS):
            if s + LAG < STEPS:
                split(E // 2 - 1, s + LAG)
            scale(E // 2 - 1, s)
        for g in range(GROUPS):
            dve.wait_ge(out_turned, g + 1)
            a = acc[:, GROUP * g:GROUP * (g + 1), :].rearrange("p a d -> p (a d)")
            dve.tensor_tensor(a, a, ps[:, g, :], ALU.add)


HEADS8, HD8 = 16, 8
PER = 4
HGROUPS = HEADS8 // PER
ROWS = P // PER


def attention8(core, name, x, wq, wk, wv, rope, row_consts):
    ps, ident = core.ps, core.ident
    NG = B * HGROUPS
    with ExitStack() as ctx:
        st = Stage(core, name, ctx)
        xt = st.sb("xt", [P, TILES * P])
        v = st.sb("v", [P, TILES, D])
        wq_c, wk_c = st.sb("wq_c", [P, D]), st.sb("wk_c", [P, D])
        wq_r, wk_r = (st.sb(n, [P, HGROUPS, PER, ROWS]) for n in ("wq_r", "wk_r"))
        rope_sb = st.sb("rope", [P, B + 1])
        rope_now = st.sb("rope_now", [P, 1])
        consts = st.sb("consts", [P, 3])
        zero = st.sb("zero", [P, BANK])
        tq, tk, hq, hk = (st.sb(n, [P, BANK]) for n in ("tq", "tk", "hq", "hk"))
        k_all = st.sb("k_all", [P, BANK], F32R)
        k_one = st.sb("k_one", [P, HGROUPS, PER, BANK], F32R)
        q_all = st.sb("q_all", [P, HGROUPS, BANK], F32R)
        tops = st.sb("tops", [P, 2, GROUP, P], F32R)
        probs = st.sb("probs", [P, 2, GROUP, PER, BANK])
        v_one = st.sb("v_one", [P, GROUP, HEADS8, ROWS])
        o_sb = st.sb("o_sb", [P, BANK])
        rec = st.sb("rec", [P, GROUP, PER])
        o_n = st.sb("o_n", [P, GROUP, PER, HD8])
        names = ("zeroed", "placed", "projected", "roped", "high", "q_split", "k_split",
                 "rope_set", "top_filled", "top_read", "rows_in_psum", "q_ready", "scored", "exped", "summed",
                 "v_set", "o_copied", "o_turned", "o_added", "inverted", "scaled")
        (zeroed, placed, projected, roped, high, q_split, k_split,
         rope_set, top_filled, top_read, rows_in_psum, q_ready, scored, exped, summed,
         v_set, o_copied, o_turned, o_added, inverted, scaled) = (st.sem(n) for n in names)
        k_spread = [st.sem(f"k_spread{gi}") for gi in range(HGROUPS)]
        PTOP = [ps[:, 2 * k:2 * k + 2, :] for k in range(2)]
        PSC = [ps[:, 4 + k, :] for k in range(2)]
        PO, PM = ps[:, 6, :], ps[:, 7, :]

        def place_weights(dve):
            dve.memset(wq_r[:], 0.0).then_inc(placed, 1)
            dve.memset(wk_r[:], 0.0).then_inc(placed, 1)
            dve.memset(tops[:].bitcast(F32), 0.0)
            dve.wait_ge(placed, 2)
            for w_c, w_r in ((wq_c, wq_r), (wk_c, wk_r)):
                for c in range(1, 4):
                    dve.tensor_copy(w_r[:, :, :, HD8 * c:HD8 * (c + 1)],
                                    w_c[:].rearrange("p (g h d) -> p g h d", h=PER, d=HD8))

        def clear(pool):
            pool.memset(v_one[:], 0.0).then_inc(zeroed, 1)
            pool.memset(zero[:], 0.0)
            pool.memset(k_one[:].bitcast(F32), 0.0)
            pool.wait_ge(zeroed, 1)
            pool.memset(v_one[:, :, :, HD8:HD8 + 1], 1.0)

        norm_turn(core, name + "_ln", x, xt, w_v=wv, v=v, on_vector=place_weights, on_pool=clear,
                  loads=((wq_c[:], wq), (wk_c[:], wk), (rope_sb[:], rope), (consts[:], row_consts)))
        block = ctx.enter_context(core.nc.Block())

        def place(b, k):
            return b + k // HGROUPS, k % HGROUPS

        @block.sync
        def _(sp):
            with sp.Fori(0, B) as b:
                for gi in range(HGROUPS):
                    sp.wait_ge(k_split, HGROUPS * b + gi + 1 + 1)
                    for hh in range(PER):
                        r = slice(ROWS * hh, ROWS * (hh + 1))
                        sp.dma_start(k_one[r, gi, hh, :].bitcast(F32), k_all[r, :].bitcast(F32))\
                          .then_inc(k_spread[gi], 16)
            for gi in range(HGROUPS):
                sp.wait_ge(k_spread[gi], 16 * PER * B)

        @block.gpsimd
        def _(pool):
            with pool.Fori(0, NG) as i:
                pool.wait_ge(roped, 2 * i + 1)
                pool.wait_ge(k_split, i + 1)
                pool.tensor_tensor(hk[:].bitcast(F32R), tk[:], zero[:], ALU.add).then_inc(high, 1)
                pool.wait_ge(roped, 2 * i + 2)
                pool.wait_ge(q_split, i + 1)
                pool.tensor_tensor(hq[:].bitcast(F32R), tq[:], zero[:], ALU.add).then_inc(high, 1)

        @block.tensor
        def _(pe):
            def project(b, k, w_r, to=PM):
                row, gi = place(b, k)
                pe.matmul(to, w_r[:, gi, :, :].rearrange("p h r -> p (h r)"), xt[:, bass.ts(row, BANK)],
                          start=True, stop=True).then_inc(projected, 1)

            def top_scores(b, k, hh, half):
                i = HGROUPS * b + k
                row, gi = place(b, k)
                if hh == 0 and half == 0:
                    pe.wait_ge(k_spread[gi], 16 * PER * (row + 1))
                    pe.wait_ge(q_split, i + 1 + 1)
                pe.wait_ge(top_read, 2 * PER * i + 2 * hh + half + 1)
                for c in range(2):
                    qc = 2 * half + c
                    last = pe.matmul(PTOP[half][:, c, :], q_all[:, gi, qc * P:(qc + 1) * P], k_one[:, gi, hh, :],
                                     start=True, stop=True)
                last.then_inc(top_filled, 1)

            def scores(m, gi, hh, half):
                for kc in (2 * half, 2 * half + 1):
                    pe.wait_ge(exped, 4 * PER * m + 4 * hh + kc + 1)
                    pe.matmul(PSC[kc % 2], k_one[:, gi, hh, kc * P:(kc + 1) * P], q_all[:, gi, :],
                              start=True, stop=True).then_inc(scored, 1)

            def sums(b, k, kc):
                m = HGROUPS * b + k
                row, gi = place(b, k)
                if kc == 0:
                    pe.wait_ge(exped, 2 + 4 * PER * (m + 1))
                    pe.wait_ge(o_copied, m + 1)
                    if gi == 0:
                        pe.wait_ge(v_set, row + 1)
                for hh in range(PER):
                    r = slice(ROWS * hh, ROWS * (hh + 1))
                    last = pe.matmul(PO[r, :], v_one[:, kc, PER * gi + hh, :], probs[:, gi % 2, kc, hh, :],
                                     start=(kc == 0), stop=(kc == GROUP - 1))
                if kc == GROUP - 1:
                    last.then_inc(summed, 1)

            def turn_out(m):
                pe.wait_ge(o_copied, m + 1 + 1)
                pe.wait_ge(o_added, m + 1)
                for j in range(GROUP):
                    last = pe.transpose(PM[:, j * P:(j + 1) * P], o_sb[:, j * P:(j + 1) * P], ident[:])
                last.then_inc(o_turned, 1)

            def group(b, k, following=2):
                m, gi = HGROUPS * b + k, k % HGROUPS
                pe.wait_ge(top_read, 2 + 2 * PER * (m + 1))
                pe.wait_ge(exped, 4 * PER * m + 1)
                for j in range(GROUP):
                    last = pe.matmul(PSC[0][:, j * P:(j + 1) * P], tops[:, gi % 2, j, :], core.ident_r[:],
                                     start=True, stop=True)
                last.then_inc(rows_in_psum, 1)
                for hh in range(PER):
                    for half in range(2):
                        if following >= 1:
                            top_scores(b, k + 1, hh, half)
                        if following >= 2 and (hh, half) == (0, 0):
                            if k >= 2:
                                pe.wait_ge(o_added, m - 1)
                            pe.wait_ge(roped, 2 * (m + 2))
                            project(b, k + 2, wk_r)
                        if (hh, half) == (0, 0):
                            pe.wait_ge(q_ready, m + 1)
                        scores(m, gi, hh, half)
                        if following >= 2 and (hh, half) == (1, 0):
                            pe.wait_ge(roped, 2 * (m + 2) + 1)
                            project(b, k + 2, wq_r)
                        if k >= 2 and (hh, half) == (2, 0):
                            if following >= 2:
                                pe.wait_ge(roped, 2 * (m + 2) + 2)
                            turn_out(m - 2)
                        if k >= 1 and half == (1 if hh else 0):
                            sums(b, k - 1, hh)

            pe.sem_inc(summed, 2)
            pe.sem_inc(o_turned, 1)
            for k in range(2):
                for which, w_r in enumerate((wk_r, wq_r)):
                    project(0, k, w_r, PTOP[k][:, which, :])
            for hh in range(PER):
                for half in range(2):
                    if hh == 0:
                        pe.wait_ge(roped, 2 * half + 2)
                    top_scores(0, 0, hh, half)
            for k in range(2):
                group(0, k)
            with pe.Fori(0, B - 1) as b:
                for k in range(2, HGROUPS + 2):
                    group(b, k)
            for k in range(2, HGROUPS):
                group(B - 1, k, following=HGROUPS - 1 - k)
            turn_out(NG - 2)
            for kc in range(GROUP):
                sums(B - 1, HGROUPS - 1, kc)
            turn_out(NG - 1)

        @block.scalar
        def _(act):
            def rotate_k(i, src=PM):
                act.wait_ge(k_split, i + 1)
                act.wait_ge(projected, 2 * i + 1)
                act.activation(tk[:], src, ACT.Identity, scale=rope_now[:, 0:1], bias=consts[:, 0:1]).then_inc(roped, 1)

            def rotate_q(i, src=PM):
                act.wait_ge(q_split, i + 1)
                act.wait_ge(projected, 2 * i + 2)
                act.activation(tq[:], src, ACT.Copy, scale=rope_now[:, 0:1]).then_inc(roped, 1)

            def copy_out(m):
                act.wait_ge(summed, 2 + m + 1)
                act.wait_ge(o_turned, m + 1)
                act.activation(o_sb[:], PO, ACT.Copy).then_inc(o_copied, 1)

            def group(b, k, following=2):
                m, gi = HGROUPS * b + k, k % HGROUPS
                if k >= 2:
                    copy_out(m - 2)
                if following >= 2:
                    if k == 2:
                        act.wait_ge(rope_set, b + 2)
                    rotate_k(m + 2)
                for hh in range(PER):
                    for kc in range(GROUP):
                        act.wait_ge(scored, 4 * PER * m + 4 * hh + kc + 1)
                        act.activation(probs[:, gi % 2, kc, hh, :], PSC[kc % 2], ACT.Exp,
                                       scale=HD8 ** -0.5).then_inc(exped, 1)
                        if following >= 2 and (hh, kc) == (1, 1):
                            rotate_q(m + 2)

            act.sem_inc(exped, 2)
            act.sem_inc(o_copied, 1)
            act.wait_ge(rope_set, 1)
            for i in range(2):
                rotate_k(i, PTOP[i][:, 0, :])
                rotate_q(i, PTOP[i][:, 1, :])
            for k in range(2):
                group(0, k)
            with act.Fori(0, B - 1) as b:
                for k in range(2, HGROUPS + 2):
                    group(b, k)
            for k in range(2, HGROUPS):
                group(B - 1, k, following=HGROUPS - 1 - k)
            copy_out(NG - 2)
            copy_out(NG - 1)

        @block.vector
        def _(dve):
            def split_k(b, k):
                if k:
                    row, gi = place(b, k - 1)
                    dve.wait_ge(k_spread[gi], 16 * PER * (row + 1))
                dve.wait_ge(high, 2 * (HGROUPS * b + k) + 1)
                dve.scalar_tensor_tensor(out=k_all[:], in0=hk[:], scalar=consts[:, 2:3], in1=tk[:],
                                         op0=ALU.mult, op1=ALU.add).then_inc(k_split, 1)

            def split_q(b, k):
                dve.wait_ge(high, 2 * (HGROUPS * b + k) + 2)
                dve.scalar_tensor_tensor(out=q_all[:, k % HGROUPS, :], in0=hq[:], scalar=consts[:, 1:2], in1=tq[:],
                                         op0=ALU.mult, op1=ALU.add).then_inc(q_split, 1)

            def top(b, k, hh, half):
                dve.wait_ge(top_filled, 2 * PER * (HGROUPS * b + k) + 2 * hh + half + 1)
                dve.tensor_reduce(tops[:, k % 2, 2 * half:2 * half + 2, ROWS * hh], PTOP[half], AX.X, ALU.max,
                                  negate=True).then_inc(top_read, 1)

            def add_out(b, gi):
                m = HGROUPS * b + gi
                dve.wait_ge(o_turned, m + 1 + 1)
                o = PM.rearrange("p (j h r) -> p j h r", j=GROUP, h=PER)
                dve.reciprocal(rec[:], o[:, :, :, HD8]).then_inc(inverted, 1)
                dve.wait_ge(inverted, m + 1)
                dve.tensor_tensor(o_n[:], o[:, :, :, 0:HD8], rec[:].unsqueeze(3).to_broadcast([P, GROUP, PER, HD8]),
                                  ALU.mult).then_inc(scaled, 1)
                dve.wait_ge(scaled, m + 1)
                xs = x[:, bass.ts(b, GROUP), gi * PER * HD8:(gi + 1) * PER * HD8]
                dve.tensor_tensor(xs, xs, o_n[:].rearrange("p j h d -> p j (h d)"), ALU.add).then_inc(o_added, 1)

            def set_rope(b):
                dve.tensor_tensor(rope_now[:], rope_sb[:, bass.ds(b, 1)], zero[:, 0:1], ALU.add).then_inc(rope_set, 1)

            def set_v(b):
                dve.tensor_tensor(v_one[:, :, :, 0:HD8],
                                  v[:, bass.ts(b, GROUP), :].rearrange("p j (h d) -> p j h d", d=HD8),
                                  zero[:, 0:BANK].rearrange("p (j h d) -> p j h d", j=GROUP, d=HD8),
                                  ALU.add).then_inc(v_set, 1)

            def group(b, k, following=2):
                m, gi = HGROUPS * b + k, k % HGROUPS
                if k == 2 and following >= 2:
                    dve.wait_ge(roped, 2 * (m + 2))
                    set_rope(b + 1)
                dve.wait_ge(rows_in_psum, m + 1)
                q = q_all[:, gi, :]
                dve.tensor_tensor(q, PSC[0], q.bitcast(F32), ALU.add).then_inc(q_ready, 1)
                if k == HGROUPS + 1:
                    dve.wait_ge(summed, m + 1)
                    set_v(b + 1)
                for hh in range(PER):
                    for half in range(2):
                        if following >= 1:
                            top(b, k + 1, hh, half)
                        if following >= 2 and (hh, half) == (1, 0):
                            split_k(b, k + 2)
                        if following >= 2 and (hh, half) == (2, 1):
                            split_q(b, k + 2)
                    if k >= 2 and hh == 2:
                        add_out(b, k - 2)

            dve.sem_inc(top_read, 2)
            for start_at_one in (q_split, k_split, o_added):
                dve.sem_inc(start_at_one, 1)
            set_rope(0)
            for k in range(2):
                split_k(0, k)
                split_q(0, k)
            set_v(0)
            for hh in range(PER):
                for half in range(2):
                    top(0, 0, hh, half)
            for k in range(2):
                group(0, k)
            with dve.Fori(0, B - 1) as b:
                for k in range(2, HGROUPS + 2):
                    group(b, k)
            for k in range(2, HGROUPS):
                group(B - 1, k, following=HGROUPS - 1 - k)
            add_out(B - 1, HGROUPS - 2)
            add_out(B - 1, HGROUPS - 1)


HEADS64, HD64 = 16, 64
INNER = HEADS64 * HD64
PAIRS = HEADS64 // 2
BIG = -1e30
SCORE_AT = {3: (0, 0, 0), 2: (1, 0, 512), 0: (1, 384, 896), 1: (2, 0, 1024)}
SCORE_BANKS = ((3,), (2, 0), (1,))
CAUSAL = sum((qc + 1) * P for qc in range(4))
TURN_AT = {0: (0, 0, 0), 1: (1, 0, 512), 2: (2, 0, 896), 3: (2, 256, 1152)}
TURN_BANKS = ((0,), (1,), (2, 3))


def values64(core, name, xh, xl, w_vh, w_vl, v, w_f, wh, wl):
    ps = core.ps
    with ExitStack() as ctx:
        st = Stage(core, name, ctx)
        in_psum, high = st.sem("in_psum"), st.sem("high")
        copied = [st.sem("copied_act"), st.sem("copied_dve")]
        block = ctx.enter_context(core.nc.Block())
        scale = lambda w: 1.0 if w < 2 else HD64 ** -0.5
        split_at = {2 * w + 2: w for w in range(4)}

        @block.tensor
        def _(pe):
            for t in range(TILES):
                tok = slice(t * P, (t + 1) * P)
                for k in range(2):
                    if t >= 2:
                        pe.wait_ge(copied[k], t - 1)
                    to, c = ps[:, 2 * (t % 2) + k, :], slice(k * BANK, (k + 1) * BANK)
                    pe.matmul(to, xh[:, tok], w_vh[:, c], start=True, stop=False)
                    pe.matmul(to, xl[:, tok], w_vh[:, c], start=False, stop=False)
                    pe.matmul(to, xh[:, tok], w_vl[:, c], start=False, stop=True).then_inc(in_psum, 1)

        @block.scalar
        def _(act):
            for t in range(TILES):
                act.wait_ge(in_psum, 2 * t + 1)
                act.activation(v[:, t, 0:BANK], ps[:, 2 * (t % 2), :], ACT.Copy).then_inc(copied[0], 1)
                if t in split_at:
                    w = split_at[t]
                    act.activation(wh[:, w, :], w_f[w], ACT.Copy, scale=scale(w)).then_inc(high, 1)

        @block.vector
        def _(dve):
            for t in range(TILES):
                dve.wait_ge(in_psum, 2 * t + 2)
                dve.tensor_copy(v[:, t, BANK:], ps[:, 2 * (t % 2) + 1, :]).then_inc(copied[1], 1)
                if t - 1 in split_at:
                    w = split_at[t - 1]
                    dve.wait_ge(high, w + 1)
                    dve.scalar_tensor_tensor(out=wl[:, w, :], in0=w_f[w], scalar=scale(w),
                                             in1=wh[:, w, :].bitcast(F32), op0=ALU.mult, op1=ALU.subtract)


def attention64(core, name, x, wkq, wv, wo1, wo2, tables, mask, gamma):
    with ExitStack() as ctx:
        st = Stage(core, name, ctx)
        v_all = st.sb("v_all", [P, TILES, INNER])
        y = v_all[:, :, 0:D]
        with ExitStack() as c1:
            heads64(core, Stage(core, name + "_main", c1), name, x, v_all, y, wkq, wv, wo1, wo2, tables, mask)
        norm_turn(core, name + "_ln2", y, xn=y, affine=(gamma, None), add_to=x, add_scale=1.0)


def heads64(core, st, name, x, v_all, y, wkq, wv, wo1, wo2, tables, mask):
    ps, ident, ctx = core.ps, core.ident, st.ctx
    NP = B * PAIRS
    xh, xl = (st.sb(n, [P, TILES * P], F32R) for n in ("xh", "xl"))
    wh, wl = st.sb("wh", [P, 4, INNER], F32R), st.sb("wl", [P, 4, INNER], F32R)
    wo1_sb, wo2_sb = st.sb("wo1", [P, PAIRS, D]), st.sb("wo2", [P, D])
    tab = st.sb("tab", [P, 2, BANK])
    mask_r = st.sb("mask_r", [P, P], F32R)
    part = st.sb("part", [P, 4, BANK])
    q = st.sb("q", [P, 2, BANK])
    k_one = st.sb("k_one", [P, 2, 2, BANK])
    w_vh, w_vl = (st.sb(n, [P, INNER], F32R) for n in ("w_vh", "w_vl"))
    v_now = st.sb("v_now", [P, 2, GROUP, P])
    neg_top = st.sb("neg_top", [P, 2, GROUP])
    total, rec = st.sb("total", [P, 2, GROUP]), st.sb("rec", [P, 2, GROUP])
    probs = st.sb("probs", [P, 2, CAUSAL])
    turned = st.sb("turned", [P, 2, CAUSAL])
    o_t = st.sb("o_t", [P, PAIRS, BANK])
    hid = st.sb("hid", [P, BANK])

    xn = part[:].rearrange("p a (t d) -> p (a t) d", d=D)
    xt = o_t[:, 0:TILES * P // BANK, :].rearrange("p a n -> p (a n)")
    w_v, mask_f = q[:].rearrange("p a n -> p (a n)"), hid[:, 0:P]
    w_f = [buf[:].rearrange("p a n -> p (a n)")[:, k * INNER:(k + 1) * INNER] for buf in (probs, turned) for k in range(2)]
    w_v_high = st.sem("w_v_high")

    def clear_and_split(pool):
        pool.memset(k_one[:], 0.0)
        pool.wait_ge(w_v_high, 1)
        pool.tensor_tensor(w_vl[:], w_v, w_vh[:].bitcast(F32), ALU.subtract)

    norm_turn(core, name + "_ln", x, xt, xn=xn, parts=(xh, xl),
              on_vector=lambda dve: dve.tensor_copy(mask_r[:], mask_f), on_pool=clear_and_split,
              on_scalar=lambda act: act.activation(w_vh[:], w_v, ACT.Copy).then_inc(w_v_high, 1),
              early=(w_v, wv), loads=[(mask_f, mask), (wo1_sb[:], wo1.rearrange("(j p) d -> p j d", p=P)), (wo2_sb[:], wo2),
                     (tab[:], tables)] + [(w_f[w], wkq[w]) for w in range(4)])
    values64(core, name + "_v", xh, xl, w_vh, w_vl, v_all, w_f, wh, wl)

    names = ("projected", "parted", "q_ready", "k_ready", "s_ready", "top_done", "exped",
             "inverted", "normed", "t_ready", "t_copied", "summed", "o_copied", "hidden", "relued", "y_ready", "y_copied")
    (projected, parted, q_ready, k_ready, s_ready, top_done, exped,
     inverted, normed, t_ready, t_copied, summed, o_copied, hidden, relued, y_ready, y_copied) = (st.sem(n) for n in names)
    v_loaded = [st.sem(f"v_loaded{j}") for j in range(2)]
    PS = [ps[:, k, :] for k in range(3)]
    PT = [ps[:, 3 + k, :] for k in range(2)]
    PM = [ps[:, 5 + k, :] for k in range(2)]
    PO = ps[:, 7, :]
    block = ctx.enter_context(core.nc.Block())

    def place(b, k):
        return b + k // PAIRS, k % PAIRS

    @block.sync
    def _(sp):
        with sp.Fori(0, B) as b:
            for j in range(PAIRS):
                sp.wait_ge(summed, PAIRS * b + j + 1)
                sp.dma_start(v_now[:, j % 2, :, :], v_all[:, bass.ts(b, GROUP), j * P:(j + 1) * P])\
                  .then_inc(v_loaded[j % 2], 16)
        for j in range(2):
            sp.wait_ge(v_loaded[j], 16 * NP // 2)

    @block.gpsimd
    def _(pool):
        def rotate(p, par):
            pool.wait_ge(parted, 2 + 4 * p + 2)
            pool.wait_ge(s_ready, 6 * p + 1)
            pool.wait_ge(q_ready, p + 1)
            for hh in range(2):
                r = slice(HD64 * hh, HD64 * (hh + 1))
                if hh:
                    pool.wait_ge(k_ready, 1 + 2 * p + 1)
                pool.tensor_tensor(k_one[r, par, hh, :], part[r, 0, :], part[r, 1, :], ALU.add).then_inc(k_ready, 1)
            pool.wait_ge(parted, 2 + 4 * p + 4)
            pool.wait_ge(k_ready, 1 + 2 * (p + 1))
            pool.tensor_tensor(q[:, par, :], part[:, 2, :], part[:, 3, :], ALU.add).then_inc(q_ready, 1)

        pool.sem_inc(q_ready, 1)
        pool.sem_inc(k_ready, 1)
        with pool.Fori(0, NP // 2) as p2:
            for par in range(2):
                rotate(2 * p2 + par, par)

    @block.tensor
    def _(pe):
        def project(b, k, w):
            row, j = place(b, k)
            pe.wait_ge(parted, 4 * (PAIRS * b + k) + w + 1)
            c, tok = slice(j * P, (j + 1) * P), bass.ts(row, BANK)
            pe.matmul(PM[w % 2], wh[:, w, c], xh[:, tok], start=True, stop=False)
            pe.matmul(PM[w % 2], wh[:, w, c], xl[:, tok], start=False, stop=False)
            pe.matmul(PM[w % 2], wl[:, w, c], xh[:, tok], start=False, stop=True).then_inc(projected, 1)

        def scores(p, j, hh):
            n = 2 * p + hh
            if hh == 0:
                pe.wait_ge(q_ready, 1 + p + 1)
                pe.wait_ge(k_ready, 1 + 2 * (p + 1))
            for bank, chunks in enumerate(SCORE_BANKS):
                pe.wait_ge(exped, 3 * n + bank + 2)
                for qc in chunks:
                    _, at, _ = SCORE_AT[qc]
                    keys = (qc + 1) * P
                    pe.matmul(PS[bank][:, at:at + keys], q[:, j % 2, qc * P:(qc + 1) * P], k_one[:, j % 2, hh, 0:keys],
                              start=True, stop=False)
                    last = pe.matmul(PS[bank][:, at + keys - P:at + keys], core.ident_r[:], mask_r[:],
                                     start=False, stop=True)
                last.then_inc(s_ready, 1)

        def turn(p, hh, fills=range(3)):
            n = 2 * p + hh
            if 0 in fills:
                pe.wait_ge(normed, n + 1)
            for fill in fills:
                chunks = TURN_BANKS[fill]
                pt = PT[(3 * hh + fill) % 2]
                pe.wait_ge(t_copied, 3 * n + fill + 1)
                for kc in chunks:
                    _, at, _ = TURN_AT[kc]
                    for qc in range(kc, GROUP):
                        row = SCORE_AT[qc][2] + kc * P
                        to = at + (qc - kc) * P
                        last = pe.transpose(pt[:, to:to + P], probs[:, hh, row:row + P], ident[:])
                last.then_inc(t_ready, 1)

        def sums(b, k):
            p = PAIRS * b + k
            pe.wait_ge(t_copied, 2 + 6 * (p + 1))
            pe.wait_ge(o_copied, p + 1)
            pe.wait_ge(v_loaded[k % 2], 16 * (PAIRS // 2 * b + k // 2 + 1))
            for kc in range(GROUP):
                at, n = TURN_AT[kc][2], BANK - kc * P
                for hh in range(2):
                    r = slice(HD64 * hh, HD64 * (hh + 1))
                    last = pe.matmul(PO[r, kc * P:], v_now[:, k % 2, kc, r], turned[:, hh, at:at + n],
                                     start=(kc == 0), stop=(kc == GROUP - 1))
            last.then_inc(summed, 1)

        def mix(b, parts):
            pe.wait_ge(parted, 2 + parts)
            pe.wait_ge(o_copied, 1 + PAIRS * (b + 1))
            for j in range(PAIRS):
                last = pe.matmul(PM[0], wo1_sb[:, j, :], o_t[:, j, :], start=(j == 0), stop=(j == PAIRS - 1))
            last.then_inc(hidden, 1)

        def mix2(b, parts):
            pe.wait_ge(parted, 2 + parts)
            pe.wait_ge(relued, b + 1)
            for t in range(GROUP):
                last = pe.matmul(PM[1][:, t * P:(t + 1) * P], hid[:, t * P:(t + 1) * P], wo2_sb[:], start=True, stop=True)
            last.then_inc(y_ready, 1)

        def pair(b, k, last=False):
            p, j = PAIRS * b + k, k % PAIRS
            scores(p, j, 0)
            if not last:
                project(b, k + 1, 0)
            if k:
                turn(p - 1, 1, range(2))
            if not last:
                if k == 2:
                    pe.wait_ge(y_copied, b + 1)
                project(b, k + 1, 1)
            if k:
                turn(p - 1, 1, range(2, 3))
            if k == PAIRS + 1:
                mix(b, 4 * (p + 1) + 1)
            scores(p, j, 1)
            if not last:
                if k == PAIRS + 1:
                    pe.wait_ge(relued, b + 1)
                project(b, k + 1, 2)
                project(b, k + 1, 3)
            if k:
                sums(b, k - 1)
            turn(p, 0)
            if k == PAIRS + 1:
                mix2(b, 4 * (p + 1) + 4)

        pe.sem_inc(s_ready, 7)
        pe.sem_inc(t_ready, 6)
        pe.sem_inc(y_ready, 1)
        pe.sem_inc(summed, 2)
        for w in range(4):
            project(0, 0, w)
        for k in range(2):
            pair(0, k)
        with pe.Fori(0, B - 1) as b:
            for k in range(2, PAIRS + 2):
                pair(b, k)
        for k in range(2, PAIRS):
            pair(B - 1, k, last=(k == PAIRS - 1))
        turn(NP - 1, 1)
        sums(B - 1, PAIRS - 1)
        mix(B - 1, 4 * NP)
        mix2(B - 1, 4 * NP)

    @block.scalar
    def _(act):
        def exps(p, hh):
            n = 2 * p + hh
            for bank, chunks in enumerate(SCORE_BANKS):
                act.wait_ge(top_done, 3 * n + bank + 1)
                if bank == 0:
                    act.wait_ge(t_ready, 3 * n + 3)
                for qc in chunks:
                    _, at, row = SCORE_AT[qc]
                    keys = (qc + 1) * P
                    last = act.activation(probs[:, hh, row:row + keys], PS[bank][:, at:at + keys], ACT.Exp,
                                          bias=neg_top[:, hh, qc:qc + 1], accum_out=total[:, hh, qc:qc + 1])
                last.then_inc(exped, 1)

        def copy_turned(p, hh):
            for fill, chunks in enumerate(TURN_BANKS):
                act.wait_ge(t_ready, 6 + 3 * (2 * p + hh) + fill + 1)
                row = TURN_AT[chunks[0]][2]
                size = sum(BANK - kc * P for kc in chunks)
                act.activation(turned[:, hh, row:row + size], PT[(3 * hh + fill) % 2][:, 0:size],
                               ACT.Copy).then_inc(t_copied, 1)

        def copy_out(p, j):
            act.wait_ge(summed, 2 + p + 1)
            act.activation(o_t[:, j, :], PO, ACT.Copy).then_inc(o_copied, 1)

        def relu(b):
            act.wait_ge(hidden, b + 1)
            act.wait_ge(y_ready, b + 1)
            act.activation(hid[:], PM[0], ACT.Relu).then_inc(relued, 1)

        def pair(b, k):
            p, j = PAIRS * b + k, k % PAIRS
            exps(p, 0)
            if k:
                copy_turned(p - 1, 1)
            if k == PAIRS + 1:
                relu(b)
            exps(p, 1)
            if k:
                copy_out(p - 1, (k - 1) % PAIRS)
            copy_turned(p, 0)

        act.sem_inc(exped, 4)
        act.sem_inc(o_copied, 1)
        act.sem_inc(t_copied, 2)
        for k in range(2):
            pair(0, k)
        with act.Fori(0, B - 1) as b:
            for k in range(2, PAIRS + 2):
                pair(b, k)
        for k in range(2, PAIRS):
            pair(B - 1, k)
        copy_turned(NP - 1, 1)
        copy_out(NP - 1, PAIRS - 1)
        relu(B - 1)

    @block.vector
    def _(dve):
        def tops(p, hh):
            n = 2 * p + hh
            dve.wait_ge(exped, 3 * n + 1)
            for bank, chunks in enumerate(SCORE_BANKS):
                dve.wait_ge(s_ready, 7 + 3 * n + bank + 1)
                for qc in chunks:
                    _, at, _ = SCORE_AT[qc]
                    last = dve.tensor_reduce(neg_top[:, hh, qc:qc + 1], PS[bank][:, at:at + (qc + 1) * P], AX.X,
                                             ALU.max, negate=True)
                last.then_inc(top_done, 1)

        def norms(p, hh):
            n = 2 * p + hh
            dve.wait_ge(exped, 4 + 3 * (n + 1))
            dve.reciprocal(rec[:, hh, :], total[:, hh, :]).then_inc(inverted, 1)
            dve.wait_ge(inverted, n + 1)
            for qc in range(GROUP):
                r = slice(SCORE_AT[qc][2], SCORE_AT[qc][2] + (qc + 1) * P)
                last = dve.tensor_scalar(probs[:, hh, r], probs[:, hh, r], rec[:, hh, qc:qc + 1], None, ALU.mult)
            last.then_inc(normed, 1)

        def take_part(p, w):
            dve.wait_ge(projected, 4 * p + w + 1)
            if w == 0:
                dve.wait_ge(k_ready, 2 * p + 1)
            if w == 2:
                dve.wait_ge(q_ready, p + 1)
            dve.tensor_tensor(part[:, w, :], PM[w % 2], tab[:, w % 2, :], ALU.mult).then_inc(parted, 1)

        def copy_y(b):
            dve.wait_ge(y_ready, 1 + b + 1)
            dve.tensor_scalar(y[:, bass.ts(b, GROUP), :], PM[1].rearrange("p (t d) -> p t d", d=D), 1.0, None,
                              ALU.mult).then_inc(y_copied, 1)

        def pair(b, k, last=False):
            p = PAIRS * b + k
            for hh in range(2):
                tops(p, hh)
                if not last:
                    take_part(p + 1, 2 * hh)
                    take_part(p + 1, 2 * hh + 1)
                norms(p, hh)
            if k == PAIRS + 1:
                copy_y(b)

        dve.sem_inc(parted, 2)
        dve.sem_inc(y_copied, 1)
        for w in range(4):
            take_part(0, w)
        for k in range(2):
            pair(0, k)
        with dve.Fori(0, B - 1) as b:
            for k in range(2, PAIRS + 2):
                pair(b, k)
        for k in range(2, PAIRS):
            pair(B - 1, k, last=(k == PAIRS - 1))
        copy_y(B - 1)


HEADS4, HD4 = 4, 32


def attention_rows(core, name, x, y, wqkv, bqkv, wo, bo):
    ps, ident = core.ps, core.ident
    U = TILES // B
    N = U * B
    score = [("score", u) for u in range(U)]
    output = [("output", u) for u in range(U)]
    PHASES = score[:2] + [p for u in range(U - 2) for p in (output[u], score[u + 2])] + output[U - 2:]
    with ExitStack() as ctx:
        st = Stage(core, name, ctx)
        xt, xi = st.sb("xt", [P, TILES * P]), st.sb("xi", [P, TILES, D])
        w_sb, bias = st.sb("wqkv", [P, 3 * D]), st.sb("bias", [P, 3 * D])
        wo_sb, bo_sb = st.sb("wo", [P, D]), st.sb("bo", [P, D])
        bias_h, bias_l = (st.sb(n, [P, 3 * D], F32R) for n in ("bias_h", "bias_l"))
        bias_high = st.sem("bias_high")

        def split_bias(dve):
            dve.tensor_copy(bias_h[:], bias[:]).then_inc(bias_high, 1)
            dve.wait_ge(bias_high, 1)
            dve.tensor_tensor(bias_l[:], bias[:], bias_h[:].bitcast(F32), ALU.subtract)

        norm_turn(core, name + "_ln", x, xt, xn=xi, on_vector=split_bias,
                  loads=((w_sb[:], wqkv), (bias[:], bqkv.partition_broadcast(P)), (wo_sb[:], wo),
                         (bo_sb[:], bo.partition_broadcast(P))))
        qkv = st.sb("qkv", [P, B, U, 3 * D])
        prod = st.sb("prod", [P, B, B, D])
        sc = st.sb("sc", [P, N, B, HEADS4])
        mx, total = st.sb("mx", [P, N, 1, HEADS4]), st.sb("total", [P, N, 1, HEADS4])
        o = st.sb("o", [P, B, U, D])
        ot = st.sb("ot", [P, 2, BANK])
        names = ("projected", "copied", "multiplied", "own_product", "reduced", "chain",
                 "shifted", "exped", "weights", "turned", "o_copied", "mixed", "added")
        (projected, copied, multiplied, own_product, reduced, chain,
         shifted, exped, weights, turned, o_copied, mixed, added) = (st.sem(n) for n in names)
        block = ctx.enter_context(core.nc.Block())
        PQ = [ps[:, q, 0:3 * D] for q in range(4)]
        PT = [ps[:, 4 + q, :] for q in range(2)]
        PX = [ps[:, 6 + q, :] for q in range(2)]
        wide = [P, B, HEADS4, HD4]
        by_head = lambda ap: ap.rearrange("p s (h d) -> p s h d", d=HD4)

        def product(engine, kind, u, s):
            if kind == "score":
                return engine.tensor_tensor(prod[:, s, :, :], qkv[:, s:s + 1, u, 0:D].to_broadcast([P, B, D]),
                                            qkv[:, :, u, D:2 * D], ALU.mult)
            return engine.tensor_tensor(by_head(prod[:, s, :, :]), by_head(qkv[:, :, u, 2 * D:3 * D]),
                                        sc[:, B * u + s, :, :].unsqueeze(3).to_broadcast(wide), ALU.mult)

        def wait_product(engine, kind, u):
            if kind == "score":
                engine.wait_ge(copied, B * (u + 1))
            else:
                engine.wait_ge(weights, u + 1)

        @block.tensor
        def _(pe):
            for n in range(N):
                t = U * (n % B) + n // B
                if n >= 4:
                    pe.wait_ge(copied, n - 3)
                pe.matmul(PQ[n % 4], xt[:, t * P:(t + 1) * P], w_sb[:], start=True, stop=False)
                pe.matmul(PQ[n % 4], core.first_row_r[:], bias_h[:], start=False, stop=False)
                pe.matmul(PQ[n % 4], core.first_row_r[:], bias_l[:], start=False, stop=True).then_inc(projected, 1)
            for u in range(U):
                pe.wait_ge(reduced, B * (PHASES.index(("output", u)) + 1))
                if u >= 2:
                    pe.wait_ge(o_copied, u - 1)
                for s in range(B):
                    last = pe.transpose(PT[u % 2][:, s * P:(s + 1) * P], o[:, s, u, :], ident[:])
                last.then_inc(turned, 1)
                if u >= 2:
                    pe.wait_ge(added, u - 1)
                pe.wait_ge(o_copied, u + 1)
                for s in range(B):
                    x = PX[u % 2][:, s * P:(s + 1) * P]
                    pe.matmul(x, ot[:, u % 2, s * P:(s + 1) * P], wo_sb[:], start=True, stop=False)
                    last = pe.matmul(x, core.first_row[:], bo_sb[:], start=False, stop=True)
                last.then_inc(mixed, 1)

        @block.scalar
        def _(act):
            def copy_qkv(u):
                for s in range(B):
                    n = B * u + s
                    act.wait_ge(projected, n + 1)
                    act.activation(qkv[:, s, u, :], PQ[n % 4], ACT.Copy).then_inc(copied, 1)

            def exps(u):
                z = sc[:, B * u:B * (u + 1), :, :]
                act.wait_ge(shifted, u + 1)
                act.activation(z, z, ACT.Exp, scale=HD4 ** -0.5).then_inc(exped, 1)

            def copy_o(u):
                act.wait_ge(turned, u + 1)
                if u >= 2:
                    act.wait_ge(mixed, u - 1)
                act.activation(ot[:, u % 2, :], PT[u % 2], ACT.Copy).then_inc(o_copied, 1)

            copy_qkv(0)
            copy_qkv(1)
            exps(0)
            copy_qkv(2)
            exps(1)
            copy_qkv(3)
            copy_o(0)
            exps(2)
            copy_o(1)
            exps(3)
            copy_o(2)
            copy_o(3)

        @block.gpsimd
        def _(pool):
            for i, (kind, u) in enumerate(PHASES):
                wait_product(pool, kind, u)
                for s in range(B - 1):
                    if i >= 1:
                        pool.wait_ge(reduced, B * (i - 1) + s + 1)
                    product(pool, kind, u, s).then_inc(multiplied, 1)

        @block.vector
        def _(dve):
            steps = [0]

            def link(ins):
                steps[0] += 1
                ins.then_inc(chain, 1)
                dve.wait_ge(chain, steps[0])

            def phase(kind, u, between=None):
                i = PHASES.index((kind, u))
                wait_product(dve, kind, u)
                if i >= 1:
                    dve.wait_ge(reduced, B * i)
                product(dve, kind, u, B - 1).then_inc(own_product, 1)
                for s in range(B):
                    if s == B // 2 and between is not None:
                        weigh(between)
                    if s < B - 1:
                        dve.wait_ge(multiplied, (B - 1) * i + s + 1)
                    else:
                        dve.wait_ge(own_product, i + 1)
                    if kind == "score":
                        dve.tensor_reduce(sc[:, B * u + s, :, :], by_head(prod[:, s, :, :]),
                                          AX.X, ALU.add).then_inc(reduced, 1)
                    else:
                        dve.tensor_reduce(o[:, s, u, :], prod[:, s, :, :].rearrange("p s c -> p c s"),
                                          AX.X, ALU.add).then_inc(reduced, 1)

            def shift(u):
                n = slice(B * u, B * (u + 1))
                dve.wait_ge(reduced, B * (PHASES.index(("score", u)) + 1))
                link(dve.tensor_reduce(mx[:, n, 0, :], sc[:, n].rearrange("p n k h -> p n h k"), AX.X, ALU.max))
                dve.tensor_tensor(sc[:, n], sc[:, n], mx[:, n].to_broadcast([P, B, B, HEADS4]),
                                  ALU.subtract).then_inc(shifted, 1)

            def weigh(u):
                n = slice(B * u, B * (u + 1))
                dve.wait_ge(exped, u + 1)
                link(dve.tensor_reduce(total[:, n, 0, :], sc[:, n].rearrange("p n k h -> p n h k"), AX.X, ALU.add))
                link(dve.reciprocal(total[:, n], total[:, n]))
                dve.tensor_tensor(sc[:, n], sc[:, n], total[:, n].to_broadcast([P, B, B, HEADS4]),
                                  ALU.mult).then_inc(weights, 1)

            def add_out(u):
                tiles = lambda ap: ap.rearrange("p (s u) d -> p s u d", u=U)[:, :, u, :]
                dve.wait_ge(mixed, u + 1)
                dve.tensor_tensor(tiles(y), PX[u % 2].rearrange("p (s d) -> p s d", d=D), tiles(xi),
                                  ALU.add).then_inc(added, 1)

            unweighted = None
            for i, (kind, u) in enumerate(PHASES):
                phase(kind, u, between=unweighted)
                unweighted = None
                if kind == "score":
                    shift(u)
                    unweighted = u
                if kind == "output" and u in (1, 2):
                    add_out(u - 1)
            add_out(U - 2)
            add_out(U - 1)


def store(core, out):
    with ExitStack() as ctx:
        st = Stage(core, "store", ctx)
        stored = st.sem("stored")
        block = ctx.enter_context(core.nc.Block())

        @block.sync
        def _(sp):
            sp.dma_start(out.rearrange("b (t p) d -> p (b t) d", p=P), core.x[:]).then_inc(stored, 16)
            sp.wait_ge(stored, 16)


def silu_experts(core, name, a):
    moe(core, name, core.x, core.x, a["L0_W1"], a["L0_W2"], a["L0_Wr"], top2=True)


def row_experts(core, name, a):
    with ExitStack() as c:
        st = Stage(core, name, c)
        y = st.sb("y", [P, TILES, D])
        attention_rows(core, name + "_mha", core.x, y, a["L1_Wqkv"], a["L1_bqkv"], a["L1_Wo"], a["L1_bo"])
        moe(core, name + "_moe", y, y, a["L1_W1"], a["L1_W2"], a["L1_Wg"], top2=False, b1=a["L1_b1"], b2=a["L1_b2"],
            xn=y, affine=(a["L1_g1"], a["L1_be1"]))
        norm_turn(core, name + "_ln2", y, xn=y, affine=(a["L1_g2"], a["L1_be2"]), add_to=core.x)


def program(nc, a, out, upto=99, start=0):
    with ExitStack() as ctx:
        core = Core(nc, ctx)
        setup(core, a["x"])
        run = lambda n: start < n <= upto
        if run(1):
            silu_experts(core, "f0a", a)
        if run(2):
            attention8(core, "a8", core.x, a["L0_Wq"], a["L0_Wk"], a["L0_Wv"], a["rope8"], a["rows8"])
        if run(3):
            silu_experts(core, "f0b", a)
        if run(4):
            row_experts(core, "r0", a)
        if run(5):
            attention64(core, "a64", core.x, a["L1_Wkq"], a["L1_Wv"], a["L1_Wo1"], a["L1_Wo2"], a["rope64"],
                        a["causal"], a["L1_gamma"])
        if run(6):
            row_experts(core, "r1", a)
        store(core, out)


def layouts(i):
    c = np.ascontiguousarray
    t = lambda n: np.asarray(i[n])
    chunks = lambda w: c(w.reshape(E, FC, P, D).transpose(0, 2, 1, 3))
    theta = 1.0 / 10000.0 ** (np.arange(0, HD8, 2, dtype=np.float32) / HD8)
    angle = np.arange(B, dtype=np.float32)[:, None] * np.concatenate([theta, theta])[None, :]
    sign = np.where(np.arange(HD8) < HD8 // 2, 1.0, -1.0)
    rope8 = np.zeros((P, B + 1), np.float32)
    rope8[:, :B] = np.tile((np.cos(angle) + sign * np.sin(angle)).T, (P // HD8, 1))
    row = np.arange(P) % ROWS
    rows8 = np.stack([row == 0, -((row >= 16) & (row < 24)).astype(np.float32), -(row >= 24).astype(np.float32)], 1)
    inv_freq = 1.0 / 10000.0 ** (np.arange(0, HD64, 2, dtype=np.float32) / HD64)
    freqs = np.arange(S, dtype=np.float32)[None, :] * np.tile(inv_freq, 2)[:, None]
    swap = np.where(np.arange(HD64) < HD64 // 2, -1.0, 1.0)[:, None]
    both = np.stack([np.cos(freqs), swap * np.sin(freqs)], 1)
    rope64 = np.tile(both, (2, 1, 1)).astype(np.float32)
    w = t("L1_attn_W_qkv").reshape(D, 3, HEADS64, 2, HD64 // 2)
    flat = lambda m: m.reshape(D, INNER)
    wkq = np.stack([flat(m) for m in (w[:, 1], w[:, 1, :, ::-1], w[:, 0], w[:, 0, :, ::-1])])
    return {
        "x": c(t("L0_attn_x")),
        "L1_Wkq": c(wkq),
        "L1_Wv": c(flat(w[:, 2])),
        "L1_Wo1": c(t("L1_attn_W_o1")),
        "L1_Wo2": c(t("L1_attn_W_o2")),
        "L1_gamma": c(t("L1_attn_gamma")),
        "rope64": rope64,
        "causal": np.triu(np.full((P, P), BIG, np.float32), 1),
        "L0_Wq": c(t("L0_attn_Wq").T),
        "L0_Wk": c(t("L0_attn_Wk").T),
        "L0_Wv": c(t("L0_attn_Wv").T),
        "L1_Wqkv": c(t("L1_ffn_Wqkv").T),
        "L1_bqkv": c(t("L1_ffn_bqkv")),
        "L1_Wo": c(t("L1_ffn_Wo").T),
        "L1_bo": c(t("L1_ffn_bo")),
        "L1_g1": c(t("L1_ffn_g1")),
        "L1_be1": c(t("L1_ffn_be1")),
        "L1_g2": c(t("L1_ffn_g2")),
        "L1_be2": c(t("L1_ffn_be2")),
        "L1_Wg": c(t("L1_ffn_Wg").T),
        "L1_W1": c(t("L1_ffn_W1")),
        "L1_b1": c(t("L1_ffn_b1").reshape(E, FC, P).transpose(2, 0, 1).reshape(P, E * FC)),
        "L1_W2": chunks(t("L1_ffn_W2")),
        "L1_b2": c(t("L1_ffn_b2").T),
        "rope8": rope8,
        "rows8": rows8.astype(np.float32),
        "L0_W1": c(t("L0_ffn_W1").transpose(0, 2, 1)),
        "L0_W2": chunks(t("L0_ffn_W2").transpose(0, 2, 1)),
        "L0_Wr": c(t("L0_ffn_Wr").T),
    }


def kernel(**inputs):
    import concourse.bacc as bacc
    from concourse.bass_utils import run_bass_kernel_spmd

    nc = bacc.Bacc("TRN2", target_bir_lowering=False, num_devices=1)
    arrays = layouts(inputs)
    aps = {n: nc.dram_tensor(f"in_{n}", v.shape, mybir.dt.from_np(v.dtype), kind="ExternalInput").ap()
           for n, v in arrays.items()}
    out = nc.dram_tensor("out", (B, S, D), F32, kind="ExternalOutput").ap()
    program(nc, aps, out)
    r = run_bass_kernel_spmd(nc, [{f"in_{n}": v for n, v in arrays.items()}], core_ids=[0])
    return r.results[0]["out"]
```
